# Optimizing a Trainium2 kernel written in Bass

```python
import numpy as np
import jax
import jax.numpy as jnp

def _softmax(x, axis=-1):
    return jax.nn.softmax(x, axis=axis)

def _gelu(x):
    return jax.nn.gelu(x, approximate=True)

def _silu(x):
    return jax.nn.silu(x)

def _sigmoid(x):
    return jax.nn.sigmoid(x)

def _layernorm(x, axis=-1, eps=1e-05):
    m = jnp.mean(x, axis=axis, keepdims=True)
    v = jnp.var(x, axis=axis, keepdims=True)
    return (x - m) / jnp.sqrt(v + eps)

def _scatter_add(tgt, idx, src, axis=0):
    return tgt.at[idx].add(src)

def _segment_sum(src, seg, n):
    return jax.ops.segment_sum(src, seg, n)
kernel_name = 'mk_adj_resnorm_d4_adj_r2_b4bfcc'

def setup_inputs(seed: int=0):
    np.random.seed(seed)
    _w = jnp.asarray

    def _rec_inputs():
        import jax
        import jax.numpy as jnp
        _gk = jax.random.key(seed)
        x = -0.000125 + 0.9999 * jax.random.normal(jax.random.fold_in(_gk, 1), (128, 128, 128), jnp.float32)
        _a = jax.random.bernoulli(jax.random.fold_in(_gk, 2), 0.0625, (128, 128))
        _a = jnp.logical_or(_a, jnp.swapaxes(_a, -1, -2))
        _a = jnp.logical_or(_a, jnp.eye(128, dtype=bool))
        _af = _a.astype(jnp.float32)
        _af = _af * jax.random.uniform(jax.random.fold_in(_gk, 3), (128, 128), jnp.float32, 0.05, 0.000488281)
        adj = _af
        return (x, adj)
    x, adj = _rec_inputs()

    def _L0_gnn_setup():
        import jax, jax.numpy as jnp
        import numpy as np
        B, T, D, H = (64, 1024, 128, 128)
        MAX_SKIP = 4

        def _lstm_last(Wih, Whh, bih, bhh, xs):
            N, _, Hd = xs.shape
            bias = bih + bhh

            def step(carry, x_t):
                h, c = carry
                g = x_t @ Wih.T + h @ Whh.T + bias
                i, f, gg, o = jnp.split(g, 4, axis=-1)
                c = jax.nn.sigmoid(f) * c + jax.nn.sigmoid(i) * jnp.tanh(gg)
                h = jax.nn.sigmoid(o) * jnp.tanh(c)
                return ((h, c), None)
            init = (jnp.zeros((N, Hd), xs.dtype), jnp.zeros((N, Hd), xs.dtype))
            (h_last, _), _ = jax.lax.scan(step, init, jnp.swapaxes(xs, 0, 1))
            return h_last
        key = jax.random.key(seed)
        ks = jax.random.split(key, 8)
        s = 0.05
        x = jax.random.normal(ks[0], (B, T, D), jnp.float32)
        adj = jax.random.uniform(ks[1], (T, T), jnp.float32) / T
        Wg0 = jax.random.normal(ks[2], (D, H), jnp.float32) * s
        bg0 = jnp.zeros((H,), jnp.float32)
        Wg1 = jax.random.normal(ks[3], (H, H), jnp.float32) * s
        bg1 = jnp.zeros((H,), jnp.float32)
        Wih = jax.random.normal(ks[4], (MAX_SKIP, 4 * H, H), jnp.float32) * s
        Whh = jax.random.normal(ks[5], (MAX_SKIP, 4 * H, H), jnp.float32) * s
        bih = jax.random.normal(ks[6], (MAX_SKIP, 4 * H), jnp.float32) * s
        bhh = jax.random.normal(ks[7], (MAX_SKIP, 4 * H), jnp.float32) * s
        return dict(x=x, adj=adj, Wg0=Wg0, bg0=bg0, Wg1=Wg1, bg1=bg1, Wih=Wih, Whh=Whh, bih=bih, bhh=bhh)
    _L0_gnn_all = _L0_gnn_setup()
    _L0_gnn_in = {k: v for k, v in _L0_gnn_all.items() if k in ('Wg0', 'bg0', 'Wg1', 'bg1', 'Wih', 'Whh', 'bih', 'bhh')}
    del _L0_gnn_all

    def _L1_gnn_setup():
        import jax, jax.numpy as jnp
        import numpy as np
        B, N, IN_DIM, OUT_DIM, H = (2, 2048, 128, 128, 4)
        HEAD_DIM = OUT_DIM // H
        EDGE_P = 0.01
        key = jax.random.key(seed)
        k1, k2, k3 = jax.random.split(key, 3)
        h = jax.random.normal(k1, (B, N, IN_DIM), dtype=jnp.float32)
        W = jax.random.normal(k2, (IN_DIM, 3 * OUT_DIM), dtype=jnp.float32) / np.sqrt(IN_DIM)
        adj = (jax.random.uniform(k3, (N, N)) < EDGE_P).astype(jnp.float32)
        adj = jnp.maximum(adj, jnp.eye(N, dtype=jnp.float32))
        return {'h': h, 'W': W, 'adj': adj}
    _L1_gnn_all = _L1_gnn_setup()
    _L1_gnn_in = {k: v for k, v in _L1_gnn_all.items() if k in ('W',)}
    del _L1_gnn_all

    def _L2_gnn_setup():
        import jax, jax.numpy as jnp
        import numpy as np
        EPS = 1e-05

        def _batchnorm(x, gamma, beta):
            mu = jnp.mean(x, axis=0)
            var = jnp.var(x, axis=0)
            return (x - mu) * jax.lax.rsqrt(var + EPS) * gamma + beta
        key = jax.random.key(seed)
        ks = jax.random.split(key, 4)
        b, n, d, h, o = (32, 1024, 128, 256, 128)
        features = jax.random.normal(ks[0], (b, n, d), dtype=jnp.float32)
        A = jax.random.uniform(ks[1], (n, n), dtype=jnp.float32)
        lim1 = float(np.sqrt(6.0 / (d + h)))
        W1 = jax.random.uniform(ks[2], (h, d), minval=-lim1, maxval=lim1, dtype=jnp.float32)
        b1 = jnp.zeros((h,), jnp.float32)
        lim2 = float(np.sqrt(6.0 / (h + o)))
        W2 = jax.random.uniform(ks[3], (o, h), minval=-lim2, maxval=lim2, dtype=jnp.float32)
        b2 = jnp.zeros((o,), jnp.float32)
        g1 = jnp.ones((h,), jnp.float32)
        be1 = jnp.zeros((h,), jnp.float32)
        g2 = jnp.ones((o,), jnp.float32)
        be2 = jnp.zeros((o,), jnp.float32)
        return {'features': features, 'A': A, 'W1': W1, 'b1': b1, 'g1': g1, 'be1': be1, 'W2': W2, 'b2': b2, 'g2': g2, 'be2': be2}
    _L2_gnn_all = _L2_gnn_setup()
    _L2_gnn_in = {k: v for k, v in _L2_gnn_all.items() if k in ('W1', 'b1', 'g1', 'be1', 'W2', 'b2', 'g2', 'be2')}
    del _L2_gnn_all

    def _L3_gnn_setup():
        import jax, jax.numpy as jnp
        import numpy as np
        B, J, F_IN, F_OUT = (8192, 17, 128, 128)
        key = jax.random.key(seed)
        k1, k2, k3, k4 = jax.random.split(key, 4)
        gain = 1.414
        bound = gain * np.sqrt(6.0 / (F_IN + F_OUT))
        W = jax.random.uniform(k2, (3, F_IN, F_OUT), dtype=jnp.float32, minval=-bound, maxval=bound)
        stdv = 1.0 / np.sqrt(F_OUT)
        bias = jax.random.uniform(k4, (F_OUT,), dtype=jnp.float32, minval=-stdv, maxval=stdv)
        return {'x': jax.random.normal(k1, (B, J, F_IN), dtype=jnp.float32), 'W': W, 'adj': jax.random.uniform(k3, (J, J), dtype=jnp.float32), 'bias': bias}
    _L3_gnn_all = _L3_gnn_setup()
    _L3_gnn_in = {k: v for k, v in _L3_gnn_all.items() if k in ('W', 'bias')}
    del _L3_gnn_all
    return {'x': x, 'adj': adj, 'L0_gnn_Wg0': _L0_gnn_in['Wg0'], 'L0_gnn_bg0': _L0_gnn_in['bg0'], 'L0_gnn_Wg1': _L0_gnn_in['Wg1'], 'L0_gnn_bg1': _L0_gnn_in['bg1'], 'L0_gnn_Wih': _L0_gnn_in['Wih'], 'L0_gnn_Whh': _L0_gnn_in['Whh'], 'L0_gnn_bih': _L0_gnn_in['bih'], 'L0_gnn_bhh': _L0_gnn_in['bhh'], 'L1_gnn_W': _L1_gnn_in['W'], 'L2_gnn_W1': _L2_gnn_in['W1'], 'L2_gnn_b1': _L2_gnn_in['b1'], 'L2_gnn_g1': _L2_gnn_in['g1'], 'L2_gnn_be1': _L2_gnn_in['be1'], 'L2_gnn_W2': _L2_gnn_in['W2'], 'L2_gnn_b2': _L2_gnn_in['b2'], 'L2_gnn_g2': _L2_gnn_in['g2'], 'L2_gnn_be2': _L2_gnn_in['be2'], 'L3_gnn_W': _L3_gnn_in['W'], 'L3_gnn_bias': _L3_gnn_in['bias']}

def reference(x, adj, L0_gnn_Wg0, L0_gnn_bg0, L0_gnn_Wg1, L0_gnn_bg1, L0_gnn_Wih, L0_gnn_Whh, L0_gnn_bih, L0_gnn_bhh, L1_gnn_W, L2_gnn_W1, L2_gnn_b1, L2_gnn_g1, L2_gnn_be1, L2_gnn_W2, L2_gnn_b2, L2_gnn_g2, L2_gnn_be2, L3_gnn_W, L3_gnn_bias):
    import jax
    import jax.numpy as jnp

    def _L0_gnn_ref(x, adj, Wg0, bg0, Wg1, bg1, Wih, Whh, bih, bhh):
        import jax, jax.numpy as jnp
        import numpy as np
        B, T, D, H = (64, 1024, 128, 128)
        MAX_SKIP = 4

        def _lstm_last(Wih, Whh, bih, bhh, xs):
            N, _, Hd = xs.shape
            bias = bih + bhh

            def step(carry, x_t):
                h, c = carry
                g = x_t @ Wih.T + h @ Whh.T + bias
                i, f, gg, o = jnp.split(g, 4, axis=-1)
                c = jax.nn.sigmoid(f) * c + jax.nn.sigmoid(i) * jnp.tanh(gg)
                h = jax.nn.sigmoid(o) * jnp.tanh(c)
                return ((h, c), None)
            init = (jnp.zeros((N, Hd), xs.dtype), jnp.zeros((N, Hd), xs.dtype))
            (h_last, _), _ = jax.lax.scan(step, init, jnp.swapaxes(xs, 0, 1))
            return h_last
        h = jax.nn.relu(jnp.einsum('ts,bsh->bth', adj, x @ Wg0 + bg0))
        h = jax.nn.relu(jnp.einsum('ts,bsh->bth', adj, h @ Wg1 + bg1))
        Bv, Tv, Hd = h.shape
        for p in range(1, MAX_SKIP + 1):
            nw = Tv // p
            wins = h[:, :nw * p, :].reshape(Bv * nw, p, Hd)
            last = _lstm_last(Wih[p - 1], Whh[p - 1], bih[p - 1], bhh[p - 1], wins)
            idx = jnp.arange(nw) * p + (p - 1)
            h = h.at[:, idx, :].set(last.reshape(Bv, nw, Hd))
        return h

    def _L1_gnn_ref(h, W, adj):
        import jax, jax.numpy as jnp
        import numpy as np
        B, N, IN_DIM, OUT_DIM, H = (2, 2048, 128, 128, 4)
        HEAD_DIM = OUT_DIM // H
        EDGE_P = 0.01
        Bn, Nn, _ = h.shape
        qkv = h @ W
        qkv = qkv.reshape(Bn, Nn, 3, H, HEAD_DIM).transpose(2, 0, 3, 1, 4)
        q, k, v = (qkv[0], qkv[1], qkv[2])
        mask = jnp.where(adj == 0, -jnp.inf, 0.0)
        scores = jnp.einsum('bhid,bhjd->bhij', q, k) / np.sqrt(HEAD_DIM) + mask
        attn = jax.nn.softmax(scores, axis=-1)
        out = jnp.einsum('bhij,bhjd->bhid', attn, v)
        return out.transpose(0, 2, 1, 3).reshape(Bn, Nn, OUT_DIM)

    def _L2_gnn_ref(features, A, W1, b1, g1, be1, W2, b2, g2, be2):
        import jax, jax.numpy as jnp
        import numpy as np
        EPS = 1e-05

        def _batchnorm(x, gamma, beta):
            mu = jnp.mean(x, axis=0)
            var = jnp.var(x, axis=0)
            return (x - mu) * jax.lax.rsqrt(var + EPS) * gamma + beta
        b, n, d = features.shape
        A_norm = A + jnp.eye(n, dtype=A.dtype)
        deg = jnp.sum(A_norm, axis=0) + jnp.sum(A_norm, axis=1) - jnp.diagonal(A_norm)
        dinv = jax.lax.rsqrt(deg)
        A_hat = A_norm * dinv[:, None] * dinv[None, :]
        agg = jnp.einsum('nm,bmd->bnd', A_hat, features)
        x = agg.reshape(-1, d)
        h = jax.nn.relu(_batchnorm(x @ W1.T + b1, g1, be1))
        out = h @ W2.T + b2
        out = _batchnorm(out, g2, be2)
        return out.reshape(b, n, -1)

    def _L3_gnn_ref(x, W, adj, bias):
        import jax, jax.numpy as jnp
        import numpy as np
        B, J, F_IN, F_OUT = (8192, 17, 128, 128)
        adj_0 = jnp.diag(jnp.diagonal(adj))
        adj_1 = jnp.triu(adj, k=1)
        adj_2 = jnp.tril(adj, k=-1)
        h = jnp.einsum('bjf,kfo->kbjo', x, W)
        out = jnp.einsum('ij,bjo->bio', adj_0, h[0]) + jnp.einsum('ij,bjo->bio', adj_1, h[1]) + jnp.einsum('ij,bjo->bio', adj_2, h[2])
        return out + bias[None, None, :]
    x = _layernorm(x + _L0_gnn_ref(x, adj, L0_gnn_Wg0, L0_gnn_bg0, L0_gnn_Wg1, L0_gnn_bg1, L0_gnn_Wih, L0_gnn_Whh, L0_gnn_bih, L0_gnn_bhh), axis=-1)
    x = _layernorm(x + _L1_gnn_ref(x, L1_gnn_W, adj), axis=-1)
    x = _layernorm(x + _L2_gnn_ref(x, adj, L2_gnn_W1, L2_gnn_b1, L2_gnn_g1, L2_gnn_be1, L2_gnn_W2, L2_gnn_b2, L2_gnn_g2, L2_gnn_be2), axis=-1)
    x = _layernorm(x + _L3_gnn_ref(x, L3_gnn_W, adj, L3_gnn_bias), axis=-1)
    return x

_drawn_inputs = setup_inputs


def setup_inputs(seed=0):
    import zlib

    import numpy as np

    out = dict(_drawn_inputs(seed))
    spreads = {'L0_gnn_bg0': (0.0, 0.8),
     'L0_gnn_bg1': (0.0, 0.8),
     'L2_gnn_b1': (0.0, 0.8),
     'L2_gnn_g1': (1.0, 0.2),
     'L2_gnn_be1': (0.0, 0.1),
     'L2_gnn_b2': (0.0, 0.8),
     'L2_gnn_g2': (1.0, 0.2),
     'L2_gnn_be2': (0.0, 0.1)}
    factors = {'L0_gnn_Wg0': 8.0, 'L0_gnn_Wg1': 8.0, 'L0_gnn_Wih': 7.292, 'L0_gnn_Whh': 8.0}
    for name, (base, spread) in spreads.items():
        noise = np.random.default_rng([zlib.crc32(name.encode()), seed]).standard_normal(out[name].shape)
        drawn = base * np.exp(spread * noise) if base else spread * noise
        out[name] = jnp.asarray(drawn.astype(out[name].dtype))
    for name, factor in factors.items():
        out[name] = (out[name] * factor).astype(out[name].dtype)
    return out
```

```python
from contextlib import ExitStack

import concourse.bass as bass
from concourse import mybir

ALU = mybir.AluOpType
ACT = mybir.ActivationFunctionType
AX = mybir.AxisListType
F32 = mybir.dt.float32
F32R = mybir.dt.float32r
BF16 = mybir.dt.bfloat16

P = 128
EPS = 1e-5
MASKED = -1e30
LANES = 2
LB = 8
LC = LB * P
HALF = LC // 2
GB = 4
GC = GB * P
HEADS = 4
DH = P // HEADS
VW = DH + 1
SKIPS = 4
I, F, G, O = range(4)


def lstm_steps():
    steps = [(1, 0, 0, P, (I, G, O)), (1, 0, 1, P, (I, G, O))]
    for p in range(2, SKIPS + 1):
        for t in range(p):
            steps.append((p, t, None, P // p, (I, G, O) if t == 0 else (I, G, F, O)))
    return steps


def wait_if(eng, sem, value):
    if not (isinstance(value, int) and value <= 0):
        eng.wait_ge(sem, value)


def gnn_stack(nc, x_sbd, adj, adjT, Wg0, bg0, Wg1, bg1, WihT, WhhT, bih, bhh, Wqkv, W1T, b1, g1, be1,
              W2T, b2, g2, be2, W3, bias3, out_tbd):
    B = x_sbd.shape[1]
    ROUNDS = B // (LANES * LB)
    GROUPS = B // GB
    STEPS = lstm_steps()
    NSTEP = len(STEPS)
    NGATE = sum(len(s[4]) for s in STEPS)
    NLATER = sum(s[1] > 0 for s in STEPS)
    gate_at = []
    for s in STEPS:
        gate_at.append((gate_at[-1] + len(STEPS[len(gate_at) - 1][4])) if gate_at else 0)
    last_use = []
    seen = {}
    for k, s in enumerate(STEPS):
        for j, gate in enumerate(s[4]):
            last_use.append(seen.get(gate))
            seen[gate] = gate_at[k] + j + 1

    EVENTS = [("gcn", n) for n in range(4)] + [("lstm", n) for n in range(NSTEP)] + [("norm", 0)]
    CYCLE = len(EVENTS)
    START = (4, 4 + CYCLE // 2)
    SPLIT = (0, CYCLE // 2)

    def agenda():
        slots = [[] for _ in range(CYCLE)]
        for lane in range(LANES):
            slots[SPLIT[lane]].append(("split", 0, lane, 0))
            for e, (what, n) in enumerate(EVENTS):
                at = START[lane] + e
                slots[at % CYCLE].append((what, n, lane, at // CYCLE))
        return [event for slot in slots for event in slot]

    AGENDA = agenda()

    def cycles(eng, do):
        for what, n, lane, late in AGENDA:
            if late == 0:
                do(what, n, lane, 0)
        with eng.Fori(1, ROUNDS) as r:
            for what, n, lane, late in AGENDA:
                do(what, n, lane, r - late if late else r)
        for what, n, lane, late in AGENDA:
            if late:
                do(what, n, lane, ROUNDS - late)

    ctx = ExitStack()
    with ctx:
        def sb(name, cols, dt=F32):
            return ctx.enter_context(nc.sbuf_tensor(name, [P, cols], dt))

        def sem(name):
            return ctx.enter_context(nc.semaphore(name))

        def lane_sems(name):
            return [sem(f"{name}_{s}") for s in range(LANES)]

        banks = ctx.enter_context(nc.psum_tensor("banks", [P, 8, 512], F32))

        xs_all = sb("x_all", B * P)
        consts = sb("consts", 2560)
        mask = sb("mask", GC, BF16)
        ident_bf = sb("ident_bf", P, BF16)

        class Area:
            def __init__(self, whole, at=0):
                self.whole, self.at = whole, at

            def take(self, cols):
                self.at += cols
                assert self.at <= self.whole.shape[1], (self.at, self.whole.shape)
                return self.whole[:, self.at - cols:self.at]

        def pair(pool, cols):
            return (pool.take(cols), pool.take(cols))

        def cut(hl, a, b):
            return (hl[0][:, a:b], hl[1][:, a:b])

        c = Area(consts)
        ident = c.take(P)
        gcn_bias0 = c.take(GC)
        gcn_bias1 = c.take(GC)
        out_bias = c.take(GC)
        lstm_bias = c.take(SKIPS * 4)
        bias_parts = c.take(2 * SKIPS * 4)
        minus_half = c.take(2 * LB)
        bn_cols = c.take(16)
        bn_work = c.take(32)
        small = [c.take(6 * LB + 6 * LB) for _ in range(LANES)]
        rden = c.take(GB * HEADS)
        maxes = c.take(GB * HEADS)
        hat_work = c.take(8)
        ones_sq = c.take(P)

        wqkv_r = pair(Area(sb("wqkv_rounded", 2 * 3 * P, F32R)), 3 * P)

        early = ExitStack()
        r = Area(early.enter_context(nc.sbuf_tensor("early_rounded", [P, 12 * LC + 2 * (7 * 4 + 3) * P], F32R)))
        x_r = [pair(r, LC) for _ in range(LANES)]
        mid_r = [pair(r, LC) for _ in range(LANES)]
        h_r = [pair(r, LC) for _ in range(LANES)]
        wih_r = pair(r, SKIPS * 4 * P)
        whh_r = pair(r, (SKIPS - 1) * 4 * P)
        wg0_r, wg1_r, adjT_r = pair(r, P), pair(r, P), pair(r, P)
        hs_r = mid_r

        f = Area(early.enter_context(nc.sbuf_tensor("early_scratch", [P, 12 * LC], F32)))
        x_in = [f.take(LC) for _ in range(LANES)]
        tmp = [f.take(LC) for _ in range(LANES)]
        h_f = [f.take(LC) for _ in range(LANES)]
        gate_f = [[f.take(HALF) for _ in range(4)] for _ in range(LANES)]
        cell_f = [f.take(HALF) for _ in range(LANES)]
        hs_f = [f.take(HALF) for _ in range(LANES)]

        w = Area(xs_all)
        raw = {"ih": w.take(SKIPS * 4 * P), "hh": w.take((SKIPS - 1) * 4 * P), "g0": w.take(P), "g1": w.take(P),
               "adjT": w.take(P), "qkv": w.take(3 * P), "adj": w.take(P), "bg0": w.take(P)}
        splits = [("ih", wih_r), ("hh", whh_r), ("g0", wg0_r), ("g1", wg1_r), ("adjT", adjT_r), ("qkv", wqkv_r)]

        early.close()

        r2 = Area(sb("late_rounded", 14 * GC + 2 * 11 * P, F32R))
        area = sb("late_area", B * P)
        hid_at = r2.at
        hid_r = [pair(r2, 2 * GC) for _ in range(2)]
        attention = Area(r2.whole, hid_at)
        xT_r, q_r, k_r = pair(attention, GC), pair(attention, GC), pair(attention, GC)
        x2_r = pair(r2, GC)
        agg_r = [pair(r2, GC) for _ in range(2)]
        x3_r = agg_r
        w1_r, w2_r, w3_r = pair(r2, 2 * P), pair(r2, 2 * P), pair(r2, 3 * P)
        hatT_r, adjk_r = pair(r2, P), pair(r2, 3 * P)

        f2 = Area(area)
        xg = f2.take(GC)
        prob = f2.take(HEADS * GC)
        probT = [f2.take(HEADS * P) for _ in range(GB)]
        vals = f2.take(GB * HEADS * VW)
        y_f = f2.take(GC)
        raw2 = {"w1": f2.take(2 * P), "w2": f2.take(2 * P), "w3": f2.take(3 * P), "hatT": f2.take(P),
                "adjk": f2.take(3 * P)}
        nadj, nadjT = f2.take(P), f2.take(P)
        diag = f2.take(P)
        splits2 = [("w1", w1_r), ("w2", w2_r), ("w3", w3_r), ("hatT", hatT_r), ("adjk", adjk_r)]
        misc = sb("late_scratch", 5760)
        f3 = Area(misc)
        bn1_stats = f3.take(GROUPS * 2 * 6)
        bn2_stats = f3.take(GROUPS * 6)
        hid_f = [f3.take(GC) for _ in range(2)]
        z_f = f3.take(GC)
        y3 = f3.take(GC)
        x3_f = [f3.take(GC) for _ in range(2)]
        y4 = f3.take(GC)
        o_f = [f3.take(GC) for _ in range(2)]

        weights_in = sem("weights_in")
        late_weights_in = sem("late_weights_in")
        ident_zero, ident_one = sem("ident_zero"), sem("ident_one")
        weights_hi, weights_lo = sem("weights_hi"), sem("weights_lo")
        rowsum_product = sem("rowsum_product")
        bias0_made, consts_made = sem("bias0_made"), sem("consts_made")
        pow_ready = sem("pow_ready")
        ones_made = sem("ones_made")

        x_loaded = lane_sems("x_loaded")
        x_again = lane_sems("x_again")
        x_hi, x_lo = lane_sems("x_hi"), lane_sems("x_lo")
        gcn_sums = lane_sems("gcn_sums")
        gcn_biased = lane_sems("gcn_biased")
        gcn_hi, gcn_lo = lane_sems("gcn_hi"), lane_sems("gcn_lo")
        gate_sums = lane_sems("gate_sums")
        gates_open = lane_sems("gates_open")
        cell_parts = lane_sems("cell_parts")
        cells = lane_sems("cells")
        cell_tanh = lane_sems("cell_tanh")
        states = lane_sems("states")
        states_hi, states_lo = lane_sems("states_hi"), lane_sems("states_lo")
        h_turned = lane_sems("h_turned")
        norm_work = lane_sems("norm_work")
        variances, rstds = lane_sems("variances"), lane_sems("rstds")
        x1_kept = lane_sems("x1_kept")

        def mm3(pe, out, wt, mv, start=True, stop=True):
            pe.matmul(out, wt[0], mv[0], start=start, stop=False)
            pe.matmul(out, wt[1], mv[0], start=False, stop=False)
            return pe.matmul(out, wt[0], mv[1], start=False, stop=stop)

        def f32(ap):
            return ap.bitcast(F32)

        def by_batch(ap, n):
            return ap.rearrange("q (b t) -> q b t", b=n)

        def windows(ap, step):
            p, t, half, nw, _ = step
            if half is not None:
                return ap[:, half * HALF:(half + 1) * HALF]
            return by_batch(ap, LB)[:, :, 0:nw * p].rearrange("q b (w p) -> q b w p", p=p)[:, :, :, t]

        def step_cols(step):
            return HALF if step[2] is not None else LB * step[3]

        def like_windows(ap, step):
            n = step_cols(step)
            return ap[:, 0:n] if step[2] is not None else ap[:, 0:n].rearrange("q (b w) -> q b w", b=LB)

        def bank(lane, n):
            return banks[:, 4 * lane + n, :]

        def ln_cols(s, nb):
            t = small[s]
            st = t[:, 0:6 * nb].rearrange("q (b k) -> q b k", k=6)
            rest = [t[:, 6 * LB + j * LB:6 * LB + j * LB + nb] for j in range(6)]
            return st, rest

        def ln_statistics(dve, y, s, nb, work, base, done):
            st, (d, m2, q, mean, var, _) = ln_cols(s, nb)
            for b in range(nb):
                ins = nc.vector.bn_stats(st[:, b, :], y[:, b * P:(b + 1) * P])
            ins.then_inc(work, 1)
            dve.wait_ge(work, base + 1)
            nc.vector.tensor_tensor(d, st[:, :, 1], st[:, :, 4], ALU.subtract)
            nc.vector.scalar_tensor_tensor(out=m2, in0=st[:, :, 2], scalar=P * EPS, in1=st[:, :, 5],
                                           op0=ALU.add, op1=ALU.add).then_inc(work, 1)
            dve.wait_ge(work, base + 2)
            nc.vector.scalar_tensor_tensor(out=q, in0=d, scalar=0.25, in1=d, op0=ALU.mult, op1=ALU.mult)
            nc.vector.scalar_tensor_tensor(out=mean, in0=d, scalar=0.5, in1=st[:, :, 4],
                                           op0=ALU.mult, op1=ALU.add).then_inc(work, 1)
            dve.wait_ge(work, base + 3)
            nc.vector.scalar_tensor_tensor(out=var, in0=m2, scalar=1.0 / P, in1=q,
                                           op0=ALU.mult, op1=ALU.add).then_inc(done, 1)

        def ln_rstd(s, nb):
            _, (_, _, _, _, var, rstd) = ln_cols(s, nb)
            return nc.gpsimd.tensor_tensor(rstd, var, minus_half[:, 0:nb], ALU.pow)

        def ln_apply(dst, y, s, nb):
            _, (_, _, _, mean, _, rstd) = ln_cols(s, nb)
            for b in range(nb):
                ins = nc.vector.tensor_scalar(dst[:, b * P:(b + 1) * P], y[:, b * P:(b + 1) * P],
                                              mean[:, b:b + 1], rstd[:, b:b + 1], ALU.subtract, ALU.mult)
            return ins

        xg_copied, x_turned, xT_hi, xT_lo = sem("xg_copied"), sem("x_turned"), sem("xT_hi"), sem("xT_lo")
        qk_sums, qk_hi, qk_lo, v_sums, v_kept = (sem("qk_sums"), sem("qk_hi"), sem("qk_lo"), sem("v_sums"),
                                                 sem("v_kept"))
        v_ones = sem("v_ones")
        scores, row_max, shifted, exps = sem("scores"), sem("row_max"), sem("shifted"), sem("exps")
        prob_turned, probT_kept, attended = sem("prob_turned"), sem("probT_kept"), sem("attended")
        att_work, var2, rstd2, x2_kept = sem("att_work"), sem("var2"), sem("rstd2"), sem("x2_kept")
        ATT_WORK = 8
        hat_work_done, hat_pow, hat_product, hat_turned = (sem("hat_work_done"), sem("hat_pow"),
                                                           sem("hat_product"), sem("hat_turned"))
        adjk_made = sem("adjk_made")
        late_hi, late_lo = sem("late_hi"), sem("late_lo")
        x2_hi, x2_lo, agg_sums, agg_kept, agg_hi, agg_lo = (sem("x2_hi"), sem("x2_lo"), sem("agg_sums"),
                                                            sem("agg_kept"), sem("agg_hi"), sem("agg_lo"))
        w1_sums, bn1_done = sem("w1_sums"), sem("bn1_done")
        bn_work_done, bn_var, bn_rstd = sem("bn_work_done"), sem("bn_var"), sem("bn_rstd")
        aggb_hi, aggb_lo, w1b_sums, hid_kept, hid_hi, hid_lo = (sem("aggb_hi"), sem("aggb_lo"), sem("w1b_sums"),
                                                                sem("hid_kept"), sem("hid_hi"), sem("hid_lo"))
        w2_sums, z_kept, bn2_done = sem("w2_sums"), sem("z_kept"), sem("bn2_done")
        z_scaled, z_turned, ln3_work, var3, rstd3, x3_kept = (sem("z_scaled"), sem("z_turned"), sem("ln3_work"),
                                                              sem("var3"), sem("rstd3"), sem("x3_kept"))
        x3_hi, x3_lo, mixed, mixed_hi, mixed_lo, w3_sums = (sem("x3_hi"), sem("x3_lo"), sem("mixed"),
                                                            sem("mixed_hi"), sem("mixed_lo"), sem("w3_sums"))
        ln4_work, var4, rstd4, out_ready, out_stored = (sem("ln4_work"), sem("var4"), sem("rstd4"),
                                                        sem("out_ready"), [sem(f"out_stored_{u}") for u in range(2)])

        mix_r = hid_r[0][0], hid_r[0][1]
        NW = 14
        NLW = 3

        def xcols(g, n=GC):
            if isinstance(g, int):
                return xs_all[:, g * n:(g + 1) * n]
            return xs_all[:, bass.ds(g * n, n)]

        def acols(g):
            if isinstance(g, int):
                return area[:, g * GC:(g + 1) * GC]
            return area[:, bass.ds(g * GC, GC)]

        def round_batches(rr, lane):
            first = rr * (LANES * LB) + lane * LB
            return slice(first, first + LB) if isinstance(first, int) else bass.ds(first, LB)

        block = ctx.enter_context(nc.Block())

        @block.sync
        def _(sp):
            def load(dst, src):
                sp.dma_start(dst, src).then_inc(weights_in, 16)

            load(raw["adjT"], adjT)
            load(raw["g0"], Wg0)
            load(raw["g1"], Wg1)
            load(raw["adj"], adj)
            load(raw["bg0"], bg0.unsqueeze(0).broadcast_to([P, P]))
            for b in range(GB):
                load(gcn_bias1[:, b * P:(b + 1) * P], bg1.unsqueeze(0).broadcast_to([P, P]))
            load(raw["ih"], WihT)
            load(raw["hh"], WhhT)
            load(bias_parts[:, 0:SKIPS * 4], bih)
            load(bias_parts[:, SKIPS * 4:2 * SKIPS * 4], bhh)
            load(raw["qkv"], Wqkv)

            def do(what, n, lane, rr):
                if what == "split":
                    wait_if(sp, x_lo[lane], rr)
                    sp.dma_start(by_batch(x_in[lane], LB), x_sbd[:, round_batches(rr, lane), :])\
                      .then_inc(x_loaded[lane], 16)
                if what == "lstm" and n == 0:
                    sp.wait_ge(gcn_hi[lane], rr * 8 + 8)
                    sp.wait_ge(gcn_lo[lane], rr * 8 + 8)
                    sp.dma_start(by_batch(tmp[lane], LB), x_sbd[:, round_batches(rr, lane), :])\
                      .then_inc(x_again[lane], 16)

            cycles(sp, do)

            for lane in range(LANES):
                sp.wait_ge(x1_kept[lane], ROUNDS)
            for dst, src in ((raw2["w1"], W1T), (raw2["w2"], W2T), (raw2["w3"], W3), (nadj, adj), (nadjT, adjT)):
                sp.dma_start(dst, src).then_inc(late_weights_in, 16)
            for b in range(GB):
                sp.dma_start(out_bias[:, b * P:(b + 1) * P], bias3.unsqueeze(0).broadcast_to([P, P]))\
                  .then_inc(late_weights_in, 16)
            for j, v in enumerate((b1, g1, be1)):
                sp.dma_start(bn_cols[:, 2 * j:2 * j + 2], v).then_inc(late_weights_in, 16)
            for j, v in enumerate((b2, g2, be2)):
                sp.dma_start(bn_cols[:, 6 + j:7 + j], v.unsqueeze(1)).then_inc(late_weights_in, 16)

            def put(pair_no, u):
                g = pair_no * 2 + u
                sp.wait_ge(out_ready, g + 1)
                first = g * GB
                rows = slice(first, first + GB) if isinstance(first, int) else bass.ds(first, GB)
                sp.dma_start(out_tbd[:, rows, :], by_batch(o_f[u], GB)).then_inc(out_stored[u], 16)

            with sp.Fori(0, GROUPS // 2) as i:
                for u in range(2):
                    put(i, u)
            for u in range(2):
                sp.wait_ge(out_stored[u], 16 * (GROUPS // 2))

        LATE = 5 + GB + 6

        @block.gpsimd
        def _(pool):
            nc.gpsimd.memset(ident, 0.0).then_inc(ident_zero, 1)
            nc.gpsimd.memset(minus_half, -0.5).then_inc(pow_ready, 1)
            nc.gpsimd.memset(ones_sq, 1.0).then_inc(ones_made, 1)
            pool.wait_ge(ident_zero, 1)
            nc.gpsimd.affine_select(out=ident, in_=ident, compare_op=ALU.not_equal, fill=1.0, base=0,
                                    pattern=[[-1, P]], channel_multiplier=1).then_inc(ident_one, 1)
            for n, (name, (hi, lo)) in enumerate(splits):
                pool.wait_ge(weights_hi, n + 1)
                nc.gpsimd.tensor_tensor(lo, raw[name], f32(hi), ALU.subtract).then_inc(weights_lo, 1)

            pool.wait_ge(pow_ready, 1)

            def do(what, n, lane, rr):
                if what == "split":
                    pool.wait_ge(x_hi[lane], rr + 1)
                    nc.gpsimd.tensor_tensor(x_r[lane][1], x_in[lane], f32(x_r[lane][0]), ALU.subtract)\
                      .then_inc(x_lo[lane], 1)
                if what == "lstm":
                    step = STEPS[n]
                    last = step[1] == step[0] - 1
                    src = h_f[lane] if last else hs_f[lane]
                    dst = h_r[lane] if last else hs_r[lane]
                    view = (lambda a: windows(a, step)) if last else (lambda a: like_windows(a, step))
                    pool.wait_ge(states_hi[lane], rr * NSTEP + n + 1)
                    nc.gpsimd.tensor_tensor(view(dst[1]), view(src), f32(view(dst[0])), ALU.subtract)\
                      .then_inc(states_lo[lane], 1)
                if what == "norm":
                    pool.wait_ge(variances[lane], rr + 1)
                    ln_rstd(lane, LB).then_inc(rstds[lane], 1)

            cycles(pool, do)

            for lane in range(LANES):
                pool.wait_ge(x1_kept[lane], ROUNDS)
            nc.gpsimd.memset(vals, 1.0).then_inc(v_ones, 1)

            def copy_group(g):
                wait_if(pool, x_turned, g)
                nc.gpsimd.tensor_copy(xg, xcols(g)).then_inc(xg_copied, 1)

            def rstd_of(g):
                pool.wait_ge(var2, g + 1)
                ln_rstd(0, GB).then_inc(rstd2, 1)

            copy_group(0)
            copy_group(1)
            rstd_of(0)
            with pool.Fori(1, GROUPS - 1) as g:
                copy_group(g + 1)
                rstd_of(g)
            rstd_of(GROUPS - 1)

            pool.wait_ge(late_weights_in, 16 * LATE)
            for k, (comp, sign) in enumerate(((ALU.is_equal, 1), (ALU.is_gt, 1), (ALU.is_gt, -1))):
                nc.gpsimd.affine_select(out=raw2["adjk"][:, k * P:(k + 1) * P], in_=nadjT, compare_op=comp, fill=0.0,
                                        base=0, pattern=[[-sign, P]], channel_multiplier=sign).then_inc(adjk_made, 1)
            pool.wait_ge(hat_work_done, 4)
            nc.gpsimd.tensor_tensor(hat_work[:, 5:6], hat_work[:, 4:5], minus_half[:, 0:1], ALU.pow)\
              .then_inc(hat_pow, 1)
            for n, (name, (hi, lo)) in enumerate(splits2):
                pool.wait_ge(late_hi, n + 1)
                nc.gpsimd.tensor_tensor(lo, raw2[name], f32(hi), ALU.subtract).then_inc(late_lo, 1)

            def x2_low(g):
                pool.wait_ge(x2_hi, g + 1)
                nc.gpsimd.tensor_tensor(x2_r[1], xcols(g), f32(x2_r[0]), ALU.subtract).then_inc(x2_lo, 1)

            x2_low(0)
            with pool.Fori(1, GROUPS) as g:
                x2_low(g)

            pool.wait_ge(bn_var, 1)
            nc.gpsimd.tensor_tensor(bn_work[:, 8:10], bn_work[:, 6:8], minus_half[:, 0:2], ALU.pow)\
              .then_inc(bn_rstd, 1)

            def second_pass(i, u):
                g = i * 2 + u
                pool.wait_ge(aggb_hi, g + 1)
                nc.gpsimd.tensor_tensor(agg_r[u][1], acols(g), f32(agg_r[u][0]), ALU.subtract).then_inc(aggb_lo, 1)

            def hidden_low(i, u):
                g = i * 2 + u
                pool.wait_ge(hid_hi, g * 2 + 2)
                nc.gpsimd.tensor_tensor(hid_r[u][1][:, GC:2 * GC], hid_f[1], f32(hid_r[u][0][:, GC:2 * GC]),
                                        ALU.subtract).then_inc(hid_lo, 1)

            second_pass(0, 0)
            with pool.Fori(0, GROUPS // 2 - 1) as i:
                second_pass(i, 1)
                hidden_low(i, 0)
                second_pass(i + 1, 0)
                hidden_low(i, 1)
            second_pass(GROUPS // 2 - 1, 1)
            hidden_low(GROUPS // 2 - 1, 0)
            hidden_low(GROUPS // 2 - 1, 1)

            pool.wait_ge(bn_var, 2)
            nc.gpsimd.tensor_tensor(bn_work[:, 8:9], bn_work[:, 6:7], minus_half[:, 0:1], ALU.pow)\
              .then_inc(bn_rstd, 1)

            def third(i, u):
                g = i * 2 + u
                pool.wait_ge(var3, g + 1)
                ln_rstd(0, GB).then_inc(rstd3, 1)
                pool.wait_ge(x3_hi, g + 1)
                nc.gpsimd.tensor_tensor(x3_r[u][1], x3_f[u], f32(x3_r[u][0]), ALU.subtract).then_inc(x3_lo, 1)

            def fourth(i, u):
                g = i * 2 + u
                pool.wait_ge(var4, g + 1)
                ln_rstd(1, GB).then_inc(rstd4, 1)

            third(0, 0)
            with pool.Fori(0, GROUPS // 2 - 1) as i:
                third(i, 1)
                fourth(i, 0)
                third(i + 1, 0)
                fourth(i, 1)
            third(GROUPS // 2 - 1, 1)
            fourth(GROUPS // 2 - 1, 0)
            fourth(GROUPS // 2 - 1, 1)

        @block.scalar
        def _(act):
            def copy(dst, src):
                return nc.scalar.activation(dst, src, ACT.Copy)

            act.wait_ge(weights_in, 16 * NW)
            for name, (hi, _) in splits:
                copy(hi, raw[name]).then_inc(weights_hi, 1)
            act.wait_ge(rowsum_product, 1)
            for b in range(GB):
                ins = copy(gcn_bias0[:, b * P:(b + 1) * P], bank(0, 0)[:, 0:P])
            ins.then_inc(bias0_made, 1)
            act.wait_ge(consts_made, 1)

            def do(what, n, lane, rr):
                if what == "split":
                    act.wait_ge(x_loaded[lane], rr * 16 + 16)
                    wait_if(act, gcn_sums[lane], rr * 8 - 6)
                    copy(x_r[lane][0], x_in[lane]).then_inc(x_hi[lane], 1)
                if what == "gcn":
                    for half in range(2):
                        cols = slice(half * HALF, (half + 1) * HALF)
                        k = 2 * n + half
                        if n == 0:
                            act.wait_ge(gcn_sums[lane], rr * 8 + k + 1)
                            copy(mid_r[lane][0][:, cols], bank(lane, half)).then_inc(gcn_hi[lane], 1)
                        elif n == 1:
                            act.wait_ge(gcn_biased[lane], rr * 4 + half + 1)
                            nc.scalar.activation(h_r[lane][0][:, cols], tmp[lane][:, cols], ACT.Relu)\
                              .then_inc(gcn_hi[lane], 1)
                        elif n == 2:
                            act.wait_ge(gcn_biased[lane], rr * 4 + 2 + half + 1)
                            copy(mid_r[lane][0][:, cols], tmp[lane][:, cols]).then_inc(gcn_hi[lane], 1)
                        else:
                            act.wait_ge(gcn_sums[lane], rr * 8 + k + 1)
                            nc.scalar.activation(h_r[lane][0][:, cols], bank(lane, 2 + half), ACT.Relu)\
                              .then_inc(gcn_hi[lane], 1)
                if what == "lstm":
                    step = STEPS[n]
                    cols = step_cols(step)
                    wait_if(act, states[lane], rr * NSTEP + n)
                    for j, gate in enumerate(step[4]):
                        act.wait_ge(gate_sums[lane], rr * NGATE + gate_at[n] + j + 1)
                        at = (step[0] - 1) * 4 + gate
                        nc.scalar.activation(gate_f[lane][gate][:, 0:cols], bank(lane, gate)[:, 0:cols],
                                             ACT.Tanh if gate == G else ACT.Sigmoid,
                                             bias=lstm_bias[:, at:at + 1]).then_inc(gates_open[lane], 1)
                    act.wait_ge(cells[lane], rr * NSTEP + n + 1)
                    nc.scalar.activation(gate_f[lane][G][:, 0:cols], cell_f[lane][:, 0:cols], ACT.Tanh)\
                      .then_inc(cell_tanh[lane], 1)

            cycles(act, do)

            def turned(g):
                act.wait_ge(x_turned, g + 1)
                wait_if(act, v_sums, g)
                copy(xT_r[0], banks[:, 4, :]).then_inc(xT_hi, 1)

            def queries(g):
                wait_if(act, scores, g)
                act.wait_ge(qk_sums, g * 2 + 1)
                nc.scalar.activation(q_r[0], banks[:, 5, :], ACT.Copy, scale=DH ** -0.5).then_inc(qk_hi, 1)
                act.wait_ge(qk_sums, g * 2 + 2)
                copy(k_r[0], banks[:, 4, :]).then_inc(qk_hi, 1)

            def soft(g):
                act.wait_ge(shifted, g + 1)
                nc.scalar.activation(prob, prob, ACT.Exp).then_inc(exps, 1)
                for b in range(GB):
                    act.wait_ge(prob_turned, g * GB + b + 1)
                    wait_if(act, attended, g * GB - GB + b + 1)
                    copy(probT[b], banks[:, (2, 3, 6, 7)[b], :]).then_inc(probT_kept, 1)

            turned(0)
            queries(0)
            turned(1)
            queries(1)
            soft(0)
            with act.Fori(1, GROUPS - 1) as g:
                turned(g + 1)
                queries(g + 1)
                soft(g)
            soft(GROUPS - 1)

            act.wait_ge(late_weights_in, 16 * LATE)
            act.wait_ge(adjk_made, 3)
            act.wait_ge(hat_turned, 1)
            for name, (hi, _) in splits2:
                copy(hi, raw2[name]).then_inc(late_hi, 1)

            def first_pass_x(g):
                wait_if(act, agg_sums, g)
                copy(x2_r[0], xcols(g)).then_inc(x2_hi, 1)

            def first_pass(g):
                act.wait_ge(agg_sums, g + 1)
                wait_if(act, w1_sums, g * 2)
                copy(agg_r[0][0], banks[:, 0, :]).then_inc(agg_hi, 1)
                copy(acols(g), banks[:, 0, :]).then_inc(agg_kept, 1)

            act.wait_ge(late_lo, len(splits2))
            first_pass_x(0)
            first_pass_x(1)
            first_pass(0)
            with act.Fori(1, GROUPS - 1) as g:
                first_pass_x(g + 1)
                first_pass(g)
            first_pass(GROUPS - 1)

            act.wait_ge(bn_work_done, 6)

            def hidden(i, u):
                g = i * 2 + u
                for m in range(2):
                    act.wait_ge(w1b_sums, g * 2 + m + 1)
                    wait_if(act, hid_lo, g * 2)
                    nc.scalar.activation(hid_f[m], banks[:, 2 * u + m, :], ACT.Relu, bias=bn_work[:, 14 + m:15 + m],
                                         scale=bn_work[:, 10 + m:11 + m]).then_inc(hid_kept, 1)

            def second_sums(i, u):
                g = i * 2 + u
                act.wait_ge(w2_sums, g + 1)
                copy(acols(g), banks[:, 4 + u, :]).then_inc(z_kept, 1)

            def hidden_pair(i):
                hidden(i, 1)
                second_sums(i, 0)
                hidden(i + 1, 0)
                second_sums(i, 1)

            hidden(0, 0)
            hidden_pair(0)
            with act.Fori(1, GROUPS // 2 - 1) as i:
                hidden_pair(i)
            hidden(GROUPS // 2 - 1, 1)
            second_sums(GROUPS // 2 - 1, 0)
            second_sums(GROUPS // 2 - 1, 1)

            act.wait_ge(bn_work_done, 11)

            def scaled(i, u):
                g = i * 2 + u
                wait_if(act, z_turned, g)
                nc.scalar.activation(z_f, acols(g), ACT.Identity, bias=bn_work[:, 14:15],
                                     scale=bn_work[:, 10:11]).then_inc(z_scaled, 1)

            def x3_high(i, u):
                g = i * 2 + u
                act.wait_ge(x3_kept, g + 1)
                wait_if(act, mixed, (g - 2) * GB + GB)
                copy(x3_r[u][0], x3_f[u]).then_inc(x3_hi, 1)

            def mixing(i, u):
                g = i * 2 + u
                for b in range(GB):
                    act.wait_ge(mixed, g * GB + b + 1)
                    at = (b % 2) * 3 * P
                    wait_if(act, w3_sums, g * GB + b - 1)
                    copy(mix_r[0][:, at:at + 3 * P], banks[:, 2 + b, 0:3 * P]).then_inc(mixed_hi, 1)

            def last_pair_of(i):
                x3_high(i, 1)
                mixing(i, 0)
                scaled(i + 1, 0)
                x3_high(i + 1, 0)
                mixing(i, 1)
                scaled(i + 1, 1)

            scaled(0, 0)
            x3_high(0, 0)
            scaled(0, 1)
            last_pair_of(0)
            with act.Fori(1, GROUPS // 2 - 1) as i:
                last_pair_of(i)
            x3_high(GROUPS // 2 - 1, 1)
            mixing(GROUPS // 2 - 1, 0)
            mixing(GROUPS // 2 - 1, 1)

        @block.vector
        def _(dve):
            dve.wait_ge(weights_in, 16 * NW)
            dve.wait_ge(ident_one, 1)
            nc.vector.tensor_tensor(lstm_bias, bias_parts[:, 0:4 * SKIPS], bias_parts[:, 4 * SKIPS:8 * SKIPS], ALU.add)
            nc.vector.tensor_copy(ident_bf[:, :], ident)
            for b in range(GB):
                ins = nc.vector.tensor_scalar(mask[:, b * P:(b + 1) * P], raw["adj"], 0.0, MASKED,
                                              ALU.is_equal, ALU.mult)
            ins.then_inc(consts_made, 1)
            dve.wait_ge(bias0_made, 1)

            def do(what, n, lane, rr):
                if what == "gcn":
                    for half in range(2):
                        cols = slice(half * HALF, (half + 1) * HALF)
                        k = 2 * n + half
                        if n == 0:
                            dve.wait_ge(gcn_hi[lane], rr * 8 + k + 1)
                            nc.vector.tensor_tensor(mid_r[lane][1][:, cols], bank(lane, half),
                                                    f32(mid_r[lane][0][:, cols]), ALU.subtract)\
                              .then_inc(gcn_lo[lane], 1)
                        elif n == 1 or n == 2:
                            dve.wait_ge(gcn_sums[lane], rr * 8 + k + 1)
                            if n == 1:
                                wait_if(dve, x1_kept[lane], rr)
                            nc.vector.tensor_tensor(tmp[lane][:, cols], bank(lane, (2 if n == 1 else 0) + half),
                                                    gcn_bias0 if n == 1 else gcn_bias1, ALU.add)\
                              .then_inc(gcn_biased[lane], 1)
                            dve.wait_ge(gcn_hi[lane], rr * 8 + k + 1)
                            dst = (h_r if n == 1 else mid_r)[lane]
                            nc.vector.scalar_tensor_tensor(
                                out=dst[1][:, cols], in0=tmp[lane][:, cols], scalar=0.0,
                                in1=f32(dst[0][:, cols]), op0=ALU.max if n == 1 else ALU.add,
                                op1=ALU.subtract).then_inc(gcn_lo[lane], 1)
                        else:
                            dve.wait_ge(gcn_hi[lane], rr * 8 + k + 1)
                            nc.vector.scalar_tensor_tensor(
                                out=h_r[lane][1][:, cols], in0=bank(lane, 2 + half), scalar=0.0,
                                in1=f32(h_r[lane][0][:, cols]), op0=ALU.max, op1=ALU.subtract)\
                              .then_inc(gcn_lo[lane], 1)
                if what == "lstm":
                    step = STEPS[n]
                    p, t, _, _, gates = step
                    cols = step_cols(step)
                    gi, gf, gg, go = (gate_f[lane][q][:, 0:cols] for q in range(4))
                    cell = cell_f[lane][:, 0:cols]
                    at = rr * NGATE + gate_at[n]
                    dve.wait_ge(gates_open[lane], at + 2)
                    if t == 0:
                        nc.vector.tensor_tensor(cell, gi, gg, ALU.mult).then_inc(cells[lane], 1)
                    else:
                        later = rr * NLATER + sum(q[1] > 0 for q in STEPS[:n])
                        nc.vector.tensor_tensor(gi, gi, gg, ALU.mult)
                        dve.wait_ge(gates_open[lane], at + 3)
                        nc.vector.tensor_tensor(cell, gf, cell, ALU.mult).then_inc(cell_parts[lane], 1)
                        dve.wait_ge(cell_parts[lane], later + 1)
                        nc.vector.tensor_tensor(cell, cell, gi, ALU.add).then_inc(cells[lane], 1)
                    last = t == p - 1
                    src = h_f[lane] if last else hs_f[lane]
                    dst = h_r[lane] if last else hs_r[lane]
                    view = (lambda a: windows(a, step)) if last else (lambda a: like_windows(a, step))
                    dve.wait_ge(cell_tanh[lane], rr * NSTEP + n + 1)
                    nc.vector.tensor_tensor(view(src), like_windows(gate_f[lane][O], step),
                                            like_windows(gate_f[lane][G], step), ALU.mult).then_inc(states[lane], 1)
                    dve.wait_ge(states[lane], rr * NSTEP + n + 1)
                    nc.vector.tensor_copy(view(dst[0]), view(src)).then_inc(states_hi[lane], 1)
                if what == "norm":
                    dve.wait_ge(x_again[lane], rr * 16 + 16)
                    for half in range(2):
                        cols = slice(half * HALF, (half + 1) * HALF)
                        dve.wait_ge(h_turned[lane], rr * 2 + half + 1)
                        nc.vector.tensor_tensor(tmp[lane][:, cols], tmp[lane][:, cols], bank(lane, half), ALU.add)\
                          .then_inc(norm_work[lane], 1)
                    dve.wait_ge(norm_work[lane], rr * 5 + 2)
                    ln_statistics(dve, tmp[lane], lane, LB, norm_work[lane], rr * 5 + 2, variances[lane])
                    dve.wait_ge(rstds[lane], rr + 1)
                    at = rr * LANES + lane
                    ln_apply(xcols(at, LC), tmp[lane], lane, LB).then_inc(x1_kept[lane], 1)

            cycles(dve, do)

            def turned_low(g):
                dve.wait_ge(xT_hi, g + 1)
                nc.vector.tensor_tensor(xT_r[1], banks[:, 4, :], f32(xT_r[0]), ALU.subtract).then_inc(xT_lo, 1)

            score_banks = banks[:, 0:HEADS, :].rearrange("q h (b j) -> q (h b) j", b=GB)
            prob_v = prob.rearrange("q (h j) -> q h j", j=P)

            def largest(g):
                dve.wait_ge(scores, g + 1)
                nc.vector.tensor_reduce(out=maxes, in_=score_banks, axis=AX.X, op=ALU.max).then_inc(row_max, 1)

            def q_low(g):
                dve.wait_ge(qk_hi, g * 2 + 1)
                nc.vector.scalar_tensor_tensor(out=q_r[1], in0=banks[:, 5, :], scalar=DH ** -0.5, in1=f32(q_r[0]),
                                               op0=ALU.mult, op1=ALU.subtract).then_inc(qk_lo, 1)

            def shift(g):
                dve.wait_ge(row_max, g + 1)
                wait_if(dve, prob_turned, g * GB)
                nc.vector.tensor_tensor(prob_v, score_banks, maxes.unsqueeze(2).broadcast_to([P, GB * HEADS, P]),
                                        ALU.subtract).then_inc(shifted, 1)

            def k_low(g):
                dve.wait_ge(qk_hi, g * 2 + 2)
                nc.vector.tensor_tensor(k_r[1], banks[:, 4, :], f32(k_r[0]), ALU.subtract).then_inc(qk_lo, 1)

            def keep_values(g):
                dve.wait_ge(v_sums, g + 1)
                wait_if(dve, attended, g * GB)
                nc.vector.tensor_copy(vals.rearrange("q (n d) -> q n d", d=VW)[:, :, 0:DH],
                                      banks[:, 5, :].rearrange("q (n d) -> q n d", d=DH)).then_inc(v_kept, 1)

            def finish_group(g):
                dve.wait_ge(attended, g * GB + GB)
                n = GB * HEADS // 2
                outs = [banks[:, j, 0:n * VW].rearrange("q (n d) -> q n d", d=VW) for j in range(2)]
                for j in range(2):
                    nc.vector.reciprocal(rden[:, j * n:(j + 1) * n].unsqueeze(2), outs[j][:, :, DH:VW])\
                      .then_inc(att_work, 1)
                dve.wait_ge(att_work, g * ATT_WORK + 2)
                for j in range(2):
                    nc.vector.tensor_tensor(
                        y_f[:, j * n * DH:(j + 1) * n * DH].rearrange("q (n d) -> q n d", d=DH), outs[j][:, :, 0:DH],
                        rden[:, j * n:(j + 1) * n].unsqueeze(2).broadcast_to([P, n, DH]), ALU.mult)\
                      .then_inc(att_work, 1)
                dve.wait_ge(att_work, g * ATT_WORK + 4)
                nc.vector.tensor_tensor(y_f, y_f, xcols(g), ALU.add).then_inc(att_work, 1)
                dve.wait_ge(att_work, g * ATT_WORK + 5)
                ln_statistics(dve, y_f, 0, GB, att_work, g * ATT_WORK + 5, var2)
                dve.wait_ge(rstd2, g + 1)
                ln_apply(xcols(g), y_f, 0, GB).then_inc(x2_kept, 1)

            dve.wait_ge(v_ones, 1)
            turned_low(0)
            q_low(0)
            k_low(0)
            keep_values(0)
            turned_low(1)
            largest(0)
            q_low(1)
            shift(0)
            k_low(1)
            keep_values(1)
            finish_group(0)
            with dve.Fori(1, GROUPS - 1) as g:
                turned_low(g + 1)
                largest(g)
                q_low(g + 1)
                shift(g)
                k_low(g + 1)
                keep_values(g + 1)
                finish_group(g)
            largest(GROUPS - 1)
            shift(GROUPS - 1)
            finish_group(GROUPS - 1)

            dve.wait_ge(late_weights_in, 16 * LATE)
            dve.wait_ge(adjk_made, 3)
            nc.vector.tensor_tensor(nadj, nadj, ident, ALU.add)
            nc.vector.tensor_tensor(nadjT, nadjT, ident, ALU.add).then_inc(hat_work_done, 1)
            dve.wait_ge(hat_work_done, 1)
            nc.vector.tensor_reduce(out=hat_work[:, 0:1], in_=nadj, axis=AX.X, op=ALU.add)
            nc.vector.tensor_reduce(out=hat_work[:, 1:2], in_=nadjT, axis=AX.X, op=ALU.add)
            nc.vector.tensor_tensor(diag, nadj, ident, ALU.mult).then_inc(hat_work_done, 1)
            dve.wait_ge(hat_work_done, 2)
            nc.vector.tensor_reduce(out=hat_work[:, 2:3], in_=diag, axis=AX.X, op=ALU.add)
            nc.vector.tensor_tensor(hat_work[:, 3:4], hat_work[:, 0:1], hat_work[:, 1:2], ALU.add)\
              .then_inc(hat_work_done, 1)
            dve.wait_ge(hat_work_done, 3)
            nc.vector.tensor_tensor(hat_work[:, 4:5], hat_work[:, 3:4], hat_work[:, 2:3], ALU.subtract)\
              .then_inc(hat_work_done, 1)
            dve.wait_ge(hat_pow, 1)
            nc.vector.tensor_scalar(diag, ident, hat_work[:, 5:6], None, ALU.mult).then_inc(hat_work_done, 1)
            nc.vector.tensor_scalar(nadjT, nadjT, hat_work[:, 5:6], None, ALU.mult).then_inc(hat_work_done, 1)
            dve.wait_ge(hat_work_done, 6)
            dve.wait_ge(hat_product, 1)
            nc.vector.tensor_tensor(raw2["hatT"], nadjT, banks[:, 1, 0:P], ALU.mult).then_inc(hat_turned, 1)

            def first_low(g):
                dve.wait_ge(agg_kept, g + 1)
                nc.vector.tensor_tensor(agg_r[0][1], banks[:, 0, :], f32(agg_r[0][0]), ALU.subtract)\
                  .then_inc(agg_lo, 1)

            bn1_v = bn1_stats.rearrange("q (m g k) -> q m g k", m=2, k=6)
            bn2_v = bn2_stats.rearrange("q (g k) -> q g k", k=6)

            def stat_cols(v, g):
                return v[:, g, :] if isinstance(g, int) else v[:, bass.ds(g, 1), :].squeeze()

            def first_stats(g):
                for m in range(2):
                    dve.wait_ge(w1_sums, g * 2 + m + 1)
                    at = m * GROUPS * 6 + g * 6
                    dst = bn1_stats[:, at:at + 6] if isinstance(at, int) else bn1_stats[:, bass.ds(at, 6)]
                    nc.vector.bn_stats(dst, banks[:, 1 + m, :]).then_inc(bn1_done, 1)

            first_low(0)
            with dve.Fori(0, GROUPS - 1) as g:
                first_low(g + 1)
                first_stats(g)
            first_stats(GROUPS - 1)

            dve.wait_ge(bn1_done, 2 * GROUPS)
            for m in range(2):
                ins = nc.vector.bn_aggr(bn_work[:, 2 * m:2 * m + 2], bn1_v[:, m, :, :].rearrange("q g k -> q (g k)"))
            ins.then_inc(bn_work_done, 1)
            dve.wait_ge(bn_work_done, 1)
            mv = bn_work[:, 0:4].rearrange("q (m k) -> q m k", k=2)
            nc.vector.tensor_tensor(bn_work[:, 4:6], mv[:, :, 0], bn_cols[:, 0:2], ALU.add).then_inc(bn_work_done, 1)
            nc.vector.tensor_scalar(bn_work[:, 6:8], mv[:, :, 1], EPS, None, ALU.add).then_inc(bn_var, 1)
            dve.wait_ge(bn_work_done, 2)
            nc.vector.tensor_tensor(bn_work[:, 12:14], bn_cols[:, 0:2], bn_work[:, 4:6], ALU.subtract)\
              .then_inc(bn_work_done, 1)
            dve.wait_ge(bn_rstd, 1)
            nc.vector.tensor_tensor(bn_work[:, 10:12], bn_work[:, 8:10], bn_cols[:, 2:4], ALU.mult)\
              .then_inc(bn_work_done, 1)
            dve.wait_ge(bn_work_done, 4)
            nc.vector.tensor_tensor(bn_work[:, 16:18], bn_work[:, 12:14], bn_work[:, 10:12], ALU.mult)\
              .then_inc(bn_work_done, 1)
            dve.wait_ge(bn_work_done, 5)
            nc.vector.tensor_tensor(bn_work[:, 14:16], bn_work[:, 16:18], bn_cols[:, 4:6], ALU.add)\
              .then_inc(bn_work_done, 1)

            def agg_high(i, u):
                g = i * 2 + u
                wait_if(dve, w1b_sums, (g - 2) * 2 + 2)
                nc.vector.tensor_copy(agg_r[u][0], acols(g)).then_inc(aggb_hi, 1)

            def hidden_parts(i, u):
                g = i * 2 + u
                wait_if(dve, w2_sums, g - 1)
                for m in range(2):
                    cols = slice(m * GC, (m + 1) * GC)
                    dve.wait_ge(hid_kept, g * 2 + m + 1)
                    nc.vector.tensor_copy(hid_r[u][0][:, cols], hid_f[m]).then_inc(hid_hi, 1)
                dve.wait_ge(hid_hi, g * 2 + 2)
                nc.vector.tensor_tensor(hid_r[u][1][:, 0:GC], hid_f[0], f32(hid_r[u][0][:, 0:GC]), ALU.subtract)\
                  .then_inc(hid_lo, 1)

            def second_stats(i, u):
                g = i * 2 + u
                dve.wait_ge(z_kept, g + 1)
                at = g * 6
                dst = bn2_stats[:, at:at + 6] if isinstance(at, int) else bn2_stats[:, bass.ds(at, 6)]
                nc.vector.bn_stats(dst, acols(g)).then_inc(bn2_done, 1)

            agg_high(0, 0)
            agg_high(0, 1)
            hidden_parts(0, 0)
            agg_high(1, 0)
            hidden_parts(0, 1)
            second_stats(0, 0)
            with dve.Fori(1, GROUPS // 2 - 1) as i:
                agg_high(i, 1)
                hidden_parts(i, 0)
                second_stats(i - 1, 1)
                agg_high(i + 1, 0)
                hidden_parts(i, 1)
                second_stats(i, 0)
            last_pair = GROUPS // 2 - 1
            agg_high(last_pair, 1)
            hidden_parts(last_pair, 0)
            second_stats(last_pair - 1, 1)
            hidden_parts(last_pair, 1)
            second_stats(last_pair, 0)
            second_stats(last_pair, 1)

            dve.wait_ge(bn2_done, GROUPS)
            nc.vector.bn_aggr(bn_work[:, 0:2], bn2_stats).then_inc(bn_work_done, 1)
            dve.wait_ge(bn_work_done, 7)
            nc.vector.tensor_tensor(bn_work[:, 4:5], bn_work[:, 0:1], bn_cols[:, 6:7], ALU.add)\
              .then_inc(bn_work_done, 1)
            nc.vector.tensor_scalar(bn_work[:, 6:7], bn_work[:, 1:2], EPS, None, ALU.add).then_inc(bn_var, 1)
            dve.wait_ge(bn_work_done, 8)
            nc.vector.tensor_tensor(bn_work[:, 12:13], bn_cols[:, 6:7], bn_work[:, 4:5], ALU.subtract)\
              .then_inc(bn_work_done, 1)
            dve.wait_ge(bn_rstd, 2)
            dve.wait_ge(hid_kept, 2 * GROUPS)
            nc.vector.tensor_tensor(bn_work[:, 10:11], bn_work[:, 8:9], bn_cols[:, 7:8], ALU.mult)\
              .then_inc(bn_work_done, 1)
            dve.wait_ge(bn_work_done, 10)
            nc.vector.scalar_tensor_tensor(out=bn_work[:, 14:15], in0=bn_work[:, 12:13], scalar=bn_work[:, 10:11],
                                           in1=bn_cols[:, 8:9], op0=ALU.mult, op1=ALU.add).then_inc(bn_work_done, 1)

            def third_norm(i, u):
                g = i * 2 + u
                dve.wait_ge(z_turned, g + 1)
                nc.vector.tensor_tensor(y3, banks[:, 0, :], xcols(g), ALU.add).then_inc(ln3_work, 1)
                dve.wait_ge(ln3_work, g * 4 + 1)
                ln_statistics(dve, y3, 0, GB, ln3_work, g * 4 + 1, var3)
                dve.wait_ge(rstd3, g + 1)
                wait_if(dve, x3_lo, g - 1)
                ln_apply(x3_f[u], y3, 0, GB).then_inc(x3_kept, 1)

            def mix_low(i, u):
                g = i * 2 + u
                for b in range(GB):
                    at = (b % 2) * 3 * P
                    dve.wait_ge(mixed_hi, g * GB + b + 1)
                    nc.vector.tensor_tensor(mix_r[1][:, at:at + 3 * P], banks[:, 2 + b, 0:3 * P],
                                            f32(mix_r[0][:, at:at + 3 * P]), ALU.subtract).then_inc(mixed_lo, 1)

            def fourth_norm(i, u):
                g = i * 2 + u
                dve.wait_ge(x3_kept, g + 1)
                dve.wait_ge(x3_lo, g + 1)
                nc.vector.tensor_tensor(x3_f[u], x3_f[u], out_bias, ALU.add).then_inc(ln4_work, 1)
                dve.wait_ge(ln4_work, g * 5 + 1)
                dve.wait_ge(w3_sums, g * GB + GB)
                nc.vector.tensor_tensor(y4, banks[:, 1, :], x3_f[u], ALU.add).then_inc(ln4_work, 1)
                dve.wait_ge(ln4_work, g * 5 + 2)
                ln_statistics(dve, y4, 1, GB, ln4_work, g * 5 + 2, var4)
                dve.wait_ge(rstd4, g + 1)
                wait_if(dve, out_stored[u], i * 16)
                ln_apply(o_f[u], y4, 1, GB).then_inc(out_ready, 1)

            third_norm(0, 0)
            third_norm(0, 1)
            mix_low(0, 0)
            fourth_norm(0, 0)
            third_norm(1, 0)
            mix_low(0, 1)
            fourth_norm(0, 1)
            with dve.Fori(1, GROUPS // 2 - 1) as i:
                third_norm(i, 1)
                mix_low(i, 0)
                fourth_norm(i, 0)
                third_norm(i + 1, 0)
                mix_low(i, 1)
                fourth_norm(i, 1)
            third_norm(last_pair, 1)
            mix_low(last_pair, 0)
            fourth_norm(last_pair, 0)
            mix_low(last_pair, 1)
            fourth_norm(last_pair, 1)

        @block.tensor
        def _(pe):
            pe.wait_ge(weights_in, 16 * NW)
            pe.matmul(bank(0, 0)[:, 0:P], raw["bg0"], raw["adjT"], start=True, stop=True).then_inc(rowsum_product, 1)
            pe.wait_ge(weights_lo, len(splits))
            pe.wait_ge(ident_one, 1)
            pe.wait_ge(bias0_made, 1)

            def do(what, n, lane, rr):
                if what == "gcn":
                    for half in range(2):
                        k = 2 * n + half
                        out = bank(lane, (0, 2, 0, 2)[n] + half)
                        if n == 0:
                            pe.wait_ge(x_lo[lane], rr + 1)
                            wait_if(pe, norm_work[lane], rr * 5 - 3)
                        else:
                            pe.wait_ge(gcn_hi[lane], rr * 8 + 2 * (n - 1) + half + 1)
                            pe.wait_ge(gcn_lo[lane], rr * 8 + 2 * (n - 1) + half + 1)
                        if n == 1:
                            ins = mm3(pe, out, wg0_r, cut(mid_r[lane], half * HALF, (half + 1) * HALF))
                        else:
                            src = (x_r, None, h_r, mid_r)[n][lane]
                            moving = wg1_r if n == 2 else adjT_r
                            for b in range(LB // 2):
                                at = half * HALF + b * P
                                ins = mm3(pe, out[:, b * P:(b + 1) * P], cut(src, at, at + P), moving)
                        ins.then_inc(gcn_sums[lane], 1)
                if what == "lstm":
                    step = STEPS[n]
                    p, t, _, _, gates = step
                    if n == 0:
                        pe.wait_ge(gcn_hi[lane], rr * 8 + 7)
                        pe.wait_ge(gcn_lo[lane], rr * 8 + 7)
                    if n == 1:
                        pe.wait_ge(gcn_lo[lane], rr * 8 + 8)
                    inputs = [windows(h_r[lane][j], step) for j in range(2)]
                    if t == 0 and n > 1:
                        pe.wait_ge(states_lo[lane], rr * NSTEP + n)
                    for j, gate in enumerate(gates):
                        out = like_windows(bank(lane, gate), step)
                        free = last_use[gate_at[n] + j]
                        if free is not None:
                            pe.wait_ge(gates_open[lane], rr * NGATE + free)
                        elif gate == O:
                            pe.wait_ge(gcn_lo[lane], rr * 8 + 8)
                        at = ((p - 1) * 4 + gate) * P
                        ins = mm3(pe, out, cut(wih_r, at, at + P), inputs, stop=(t == 0))
                        if t == 0:
                            ins.then_inc(gate_sums[lane], 1)
                    if t:
                        pe.wait_ge(states_lo[lane], rr * NSTEP + n)
                        carried = [like_windows(hs_r[lane][j], step) for j in range(2)]
                        for gate in gates:
                            at = ((p - 2) * 4 + gate) * P
                            mm3(pe, like_windows(bank(lane, gate), step), cut(whh_r, at, at + P), carried,
                                start=False).then_inc(gate_sums[lane], 1)
                if what == "norm":
                    pe.wait_ge(states[lane], rr * NSTEP + NSTEP)
                    pe.wait_ge(gates_open[lane], rr * NGATE + NGATE)
                    for half in range(2):
                        for b in range(LB // 2):
                            at = half * HALF + b * P
                            ins = pe.transpose(bank(lane, half)[:, b * P:(b + 1) * P], h_f[lane][:, at:at + P], ident)
                        ins.then_inc(h_turned[lane], 1)

            cycles(pe, do)

            for lane in range(LANES):
                pe.wait_ge(x1_kept[lane], ROUNDS)

            def turn(g):
                pe.wait_ge(xg_copied, g + 1)
                wait_if(pe, qk_lo, g * 2)
                for b in range(GB):
                    ins = pe.transpose(banks[:, 4, b * P:(b + 1) * P], xg[:, b * P:(b + 1) * P], ident)
                ins.then_inc(x_turned, 1)

            def project(g):
                pe.wait_ge(xT_lo, g + 1)
                wait_if(pe, v_kept, g)
                mm3(pe, banks[:, 5, :], cut(wqkv_r, 0, P), xT_r).then_inc(qk_sums, 1)
                mm3(pe, banks[:, 4, :], cut(wqkv_r, P, 2 * P), xT_r).then_inc(qk_sums, 1)
                pe.wait_ge(qk_lo, g * 2 + 1)
                for b in range(GB):
                    ins = mm3(pe, banks[:, 5, b * P:(b + 1) * P], cut(xT_r, b * P, (b + 1) * P),
                              cut(wqkv_r, 2 * P, 3 * P))
                ins.then_inc(v_sums, 1)

            def score(g):
                pe.wait_ge(qk_lo, g * 2 + 2)
                wait_if(pe, att_work, (g - 1) * ATT_WORK + 4)
                wait_if(pe, probT_kept, g * GB)
                for h in range(HEADS):
                    pe.matmul(banks[:, h, :], ident_bf[:, :], mask[:, :], start=True, stop=False)
                for b in range(GB):
                    for h in range(HEADS):
                        rows, cols = slice(h * DH, (h + 1) * DH), slice(b * P, (b + 1) * P)
                        out = banks[:, h, cols]
                        pe.matmul(out, q_r[0][rows, cols], k_r[0][rows, cols], start=False, stop=False)
                        pe.matmul(out, q_r[1][rows, cols], k_r[0][rows, cols], start=False, stop=False)
                        ins = pe.matmul(out, q_r[0][rows, cols], k_r[1][rows, cols], start=False, stop=b == GB - 1)
                ins.then_inc(scores, 1)

            def attend(g):
                pe.wait_ge(exps, g + 1)
                pv = prob.rearrange("q (h b j) -> q h b j", h=HEADS, b=GB)
                for b in range(GB):
                    for h in range(HEADS):
                        ins = pe.transpose(banks[:, (2, 3, 6, 7)[b], h * P:(h + 1) * P], pv[:, h, b, :], ident)
                    ins.then_inc(prob_turned, 1)
                pe.wait_ge(v_kept, g + 1)
                for b in range(GB):
                    pe.wait_ge(probT_kept, g * GB + b + 1)
                    for h in range(HEADS):
                        at, to = (b * HEADS + h) * VW, ((b % 2) * HEADS + h) * VW
                        ins = pe.matmul(banks[:, b // 2, to:to + VW], probT[b][:, h * P:(h + 1) * P],
                                        vals[:, at:at + VW], start=True, stop=True)
                    ins.then_inc(attended, 1)

            turn(0)
            project(0)
            turn(1)
            score(0)
            project(1)
            attend(0)
            with pe.Fori(1, GROUPS - 1) as g:
                turn(g + 1)
                score(g)
                project(g + 1)
                attend(g)
            score(GROUPS - 1)
            attend(GROUPS - 1)

            pe.wait_ge(hat_work_done, 5)
            pe.wait_ge(att_work, GROUPS * ATT_WORK)
            pe.wait_ge(ones_made, 1)
            pe.matmul(banks[:, 1, 0:P], ones_sq, diag, start=True, stop=True).then_inc(hat_product, 1)
            pe.wait_ge(late_lo, len(splits2))

            def aggregate(g):
                pe.wait_ge(x2_lo, g + 1)
                wait_if(pe, agg_kept, g)
                wait_if(pe, agg_lo, g)
                for b in range(GB):
                    ins = mm3(pe, banks[:, 0, b * P:(b + 1) * P], cut(x2_r, b * P, (b + 1) * P), hatT_r)
                ins.then_inc(agg_sums, 1)

            def first_layer(g):
                pe.wait_ge(agg_lo, g + 1)
                for m in range(2):
                    wait_if(pe, bn1_done, (g - 1) * 2 + m + 1)
                    mm3(pe, banks[:, 1 + m, :], cut(w1_r, m * P, (m + 1) * P), agg_r[0]).then_inc(w1_sums, 1)

            aggregate(0)
            aggregate(1)
            first_layer(0)
            with pe.Fori(1, GROUPS - 1) as g:
                aggregate(g + 1)
                first_layer(g)
            first_layer(GROUPS - 1)

            pe.wait_ge(bn1_done, 2 * GROUPS)

            def first_again(i, u):
                g = i * 2 + u
                pe.wait_ge(aggb_lo, g + 1)
                for m in range(2):
                    wait_if(pe, hid_kept, (g - 2) * 2 + m + 1)
                    mm3(pe, banks[:, 2 * u + m, :], cut(w1_r, m * P, (m + 1) * P), agg_r[u]).then_inc(w1b_sums, 1)

            def second_layer(i, u):
                g = i * 2 + u
                pe.wait_ge(hid_lo, g * 2 + 2)
                wait_if(pe, z_kept, g - 1)
                out = banks[:, 4 + u, :]
                mm3(pe, out, cut(w2_r, 0, P), cut(hid_r[u], 0, GC), stop=False)
                mm3(pe, out, cut(w2_r, P, 2 * P), cut(hid_r[u], GC, 2 * GC), start=False).then_inc(w2_sums, 1)

            last_pair = GROUPS // 2 - 1
            first_again(0, 0)
            first_again(0, 1)
            second_layer(0, 0)
            first_again(1, 0)
            second_layer(0, 1)
            with pe.Fori(1, last_pair) as i:
                first_again(i, 1)
                second_layer(i, 0)
                first_again(i + 1, 0)
                second_layer(i, 1)
            first_again(last_pair, 1)
            second_layer(last_pair, 0)
            second_layer(last_pair, 1)

            pe.wait_ge(bn2_done, GROUPS)
            pe.wait_ge(z_kept, GROUPS)

            def turn_z(i, u):
                g = i * 2 + u
                pe.wait_ge(z_scaled, g + 1)
                wait_if(pe, ln3_work, (g - 1) * 4 + 1)
                for b in range(GB):
                    ins = pe.transpose(banks[:, 0, b * P:(b + 1) * P], z_f[:, b * P:(b + 1) * P], ident)
                ins.then_inc(z_turned, 1)

            def mix(i, u):
                g = i * 2 + u
                pe.wait_ge(x3_lo, g + 1)
                for b in range(GB):
                    wait_if(pe, mixed_lo, (g - 1) * GB + b + 1)
                    mm3(pe, banks[:, 2 + b, 0:3 * P], cut(x3_r[u], b * P, (b + 1) * P), adjk_r).then_inc(mixed, 1)

            def third_layer(i, u):
                g = i * 2 + u
                wait_if(pe, ln4_work, (g - 1) * 5 + 2)
                for b in range(GB):
                    pe.wait_ge(mixed_lo, g * GB + b + 1)
                    for k in range(3):
                        at = (b % 2) * 3 * P + k * P
                        ins = mm3(pe, banks[:, 1, b * P:(b + 1) * P], cut(mix_r, at, at + P),
                                  cut(w3_r, k * P, (k + 1) * P), start=k == 0, stop=k == 2)
                    ins.then_inc(w3_sums, 1)

            turn_z(0, 0)
            turn_z(0, 1)
            mix(0, 0)
            third_layer(0, 0)
            turn_z(1, 0)
            mix(0, 1)
            third_layer(0, 1)
            with pe.Fori(1, last_pair) as i:
                turn_z(i, 1)
                mix(i, 0)
                third_layer(i, 0)
                turn_z(i + 1, 0)
                mix(i, 1)
                third_layer(i, 1)
            turn_z(last_pair, 1)
            mix(last_pair, 0)
            third_layer(last_pair, 0)
            mix(last_pair, 1)
            third_layer(last_pair, 1)


_INS = ['x', 'adj', 'adjT', 'Wg0', 'bg0', 'Wg1', 'bg1', 'WihT', 'WhhT', 'bih', 'bhh', 'Wqkv', 'W1T', 'b1', 'g1', 'be1',
        'W2T', 'b2', 'g2', 'be2', 'W3', 'bias3']


def kernel(x, adj, L0_gnn_Wg0, L0_gnn_bg0, L0_gnn_Wg1, L0_gnn_bg1, L0_gnn_Wih, L0_gnn_Whh, L0_gnn_bih, L0_gnn_bhh,
           L1_gnn_W, L2_gnn_W1, L2_gnn_b1, L2_gnn_g1, L2_gnn_be1, L2_gnn_W2, L2_gnn_b2, L2_gnn_g2, L2_gnn_be2,
           L3_gnn_W, L3_gnn_bias):
    import numpy as np
    import concourse.bacc as bacc
    from concourse.bass_utils import run_bass_kernel_spmd

    def gate_columns(a):
        return np.asarray(a).reshape(SKIPS * 4, P).T

    def halves(a):
        return np.asarray(a).reshape(2, P).T

    laid = {
        'x': np.asarray(x).transpose(1, 0, 2),
        'adj': adj, 'adjT': np.asarray(adj).T,
        'Wg0': L0_gnn_Wg0, 'bg0': L0_gnn_bg0, 'Wg1': L0_gnn_Wg1, 'bg1': L0_gnn_bg1,
        'WihT': np.asarray(L0_gnn_Wih).transpose(2, 0, 1).reshape(P, -1),
        'WhhT': np.asarray(L0_gnn_Whh)[1:].transpose(2, 0, 1).reshape(P, -1),
        'bih': gate_columns(L0_gnn_bih), 'bhh': gate_columns(L0_gnn_bhh),
        'Wqkv': L1_gnn_W,
        'W1T': np.asarray(L2_gnn_W1).T, 'b1': halves(L2_gnn_b1), 'g1': halves(L2_gnn_g1), 'be1': halves(L2_gnn_be1),
        'W2T': np.asarray(L2_gnn_W2).T.reshape(2, P, P).transpose(1, 0, 2).reshape(P, -1),
        'b2': L2_gnn_b2, 'g2': L2_gnn_g2, 'be2': L2_gnn_be2,
        'W3': np.asarray(L3_gnn_W).transpose(1, 0, 2).reshape(P, -1), 'bias3': L3_gnn_bias,
    }
    nc = bacc.Bacc("TRN2", target_bir_lowering=False, num_devices=1)
    arrays, args = {}, []
    for name in _INS:
        a = np.ascontiguousarray(laid[name])
        arrays[f"in_{name}_dram"] = a
        args.append(nc.dram_tensor(f"in_{name}_dram", a.shape, mybir.dt.from_np(a.dtype), kind="ExternalInput").ap())
    shape = laid['x'].shape
    args.append(nc.dram_tensor("out_dram", shape, F32, kind="ExternalOutput").ap())
    gnn_stack(nc, *args)
    r = run_bass_kernel_spmd(nc, [arrays], core_ids=[0])
    return r.results[0]["out_dram"].transpose(1, 0, 2)
```

```python
from contextlib import ExitStack

import concourse.bass as bass
from concourse import mybir

ALU = mybir.AluOpType
ACT = mybir.ActivationFunctionType
AX = mybir.AxisListType
F32 = mybir.dt.float32
F32R = mybir.dt.float32r
BF16 = mybir.dt.bfloat16

P = 128
EPS = 1e-5
MASKED = -1e30
LANES = 2
LB = 8
LC = LB * P
HALF = LC // 2
GB = 4
GC = GB * P
HEADS = 4
DH = P // HEADS
VW = 2 * DH
SKIPS = 4
I, F, G, O = range(4)


def lstm_steps():
    steps = [(1, 0, 0, P, (I, G, O)), (1, 0, 1, P, (I, G, O))]
    for p in range(2, SKIPS + 1):
        for t in range(p):
            steps.append((p, t, None, P // p, (I, G, O) if t == 0 else (I, G, F, O)))
    return steps


def wait_if(eng, sem, value):
    if not (isinstance(value, int) and value <= 0):
        eng.wait_ge(sem, value)


def gnn_stack(nc, x_sbd, adj, adjT, Wg0, bg0, Wg1, bg1, WihT, WhhT, bih, bhh, Wqkv, W1T, b1, g1, be1,
              W2T, b2, g2, be2, W3, bias3, out_tbd):
    B = x_sbd.shape[1]
    ROUNDS = B // (LANES * LB)
    GROUPS = B // GB
    STEPS = lstm_steps()
    NSTEP = len(STEPS)
    NGATE = sum(len(s[4]) for s in STEPS)
    NLATER = sum(s[1] > 0 for s in STEPS)
    gate_at = []
    for s in STEPS:
        gate_at.append((gate_at[-1] + len(STEPS[len(gate_at) - 1][4])) if gate_at else 0)
    last_use = []
    seen = {}
    for k, s in enumerate(STEPS):
        for j, gate in enumerate(s[4]):
            last_use.append(seen.get(gate))
            seen[gate] = gate_at[k] + j + 1

    EVENTS = [("gcn", n) for n in range(4)] + [("lstm", n) for n in range(NSTEP)] + \
        [("residual", 0), ("statistics", 0), ("norm", 0)]
    CYCLE = 4 + NSTEP + 1
    START = (4, 4 + CYCLE // 2)
    SPLIT = (0, CYCLE // 2)

    def agenda():
        slots = [[] for _ in range(CYCLE)]
        for lane in range(LANES):
            slots[SPLIT[lane]].append(("split", 0, lane, 0))
            for e, (what, n) in enumerate(EVENTS):
                at = START[lane] + e
                slots[at % CYCLE].append((what, n, lane, at // CYCLE))
        return [event for slot in slots for event in sorted(slot, key=lambda v: v[0] in ("statistics", "norm"))]

    AGENDA = agenda()

    def cycles(eng, do):
        for what, n, lane, late in AGENDA:
            if late == 0:
                do(what, n, lane, 0)
        with eng.Fori(1, ROUNDS) as r:
            for what, n, lane, late in AGENDA:
                do(what, n, lane, r - late if late else r)
        for what, n, lane, late in AGENDA:
            if late:
                do(what, n, lane, ROUNDS - late)

    def groups(eng, order, do):
        for head in range(4):
            for what, part, late in order:
                if head >= late:
                    do(what, part, head - late, (head - late) % 2)
        with eng.Fori(2, GROUPS // 2) as i:
            for head in range(2):
                for what, part, late in order:
                    do(what, part, i * 2 + (head - late), (head - late) % 2)
        for head in range(GROUPS, GROUPS + max(late for _, _, late in order)):
            for what, part, late in order:
                if late > head - GROUPS:
                    do(what, part, head - late, (head - late) % 2)

    ctx = ExitStack()
    with ctx:
        def sb(name, cols, dt=F32):
            return ctx.enter_context(nc.sbuf_tensor(name, [P, cols], dt))

        def sem(name):
            return ctx.enter_context(nc.semaphore(name))

        def lane_sems(name):
            return [sem(f"{name}_{s}") for s in range(LANES)]

        banks = ctx.enter_context(nc.psum_tensor("banks", [P, 8, 512], F32))

        xs_all = sb("x_all", B * P)
        consts = sb("consts", 2560)
        mask = sb("mask", GC, BF16)
        ident_bf = sb("ident_bf", P, BF16)

        class Area:
            def __init__(self, whole, at=0):
                self.whole, self.at = whole, at

            def take(self, cols):
                self.at += cols
                assert self.at <= self.whole.shape[1], (self.at, self.whole.shape)
                return self.whole[:, self.at - cols:self.at]

        def pair(pool, cols):
            return (pool.take(cols), pool.take(cols))

        def cut(hl, a, b):
            return (hl[0][:, a:b], hl[1][:, a:b])

        c = Area(consts)
        ident = c.take(P)
        gcn_bias0 = c.take(GC)
        gcn_bias1 = c.take(GC)
        out_bias = c.take(1)
        lstm_bias = c.take(SKIPS * 4)
        bias_parts = c.take(2 * SKIPS * 4)
        minus_half = c.take(2 * LB)
        bn_cols = c.take(16)
        bn_work = c.take(32)
        small = [c.take(6 * LB + 6 * LB) for _ in range(LANES)]
        rden = c.take(GB * HEADS)
        maxes = c.take(GB * HEADS)
        shift_cols = c.take(GB)
        hat_work = c.take(8)
        ones_sq = c.take(P)

        wqkv_r = pair(Area(sb("wqkv_rounded", 2 * 3 * P, F32R)), 3 * P)

        early = ExitStack()
        r = Area(early.enter_context(nc.sbuf_tensor("early_rounded", [P, 12 * LC + 2 * (7 * 4 + 3) * P], F32R)))
        x_r = [pair(r, LC) for _ in range(LANES)]
        mid_r = [pair(r, LC) for _ in range(LANES)]
        h_r = [pair(r, LC) for _ in range(LANES)]
        wih_r = pair(r, SKIPS * 4 * P)
        whh_r = pair(r, (SKIPS - 1) * 4 * P)
        wg0_r, wg1_r, adjT_r = pair(r, P), pair(r, P), pair(r, P)
        hs_r = mid_r

        f = Area(early.enter_context(nc.sbuf_tensor("early_scratch", [P, 12 * LC], F32)))
        x_in = [f.take(LC) for _ in range(LANES)]
        tmp = [f.take(LC) for _ in range(LANES)]
        h_f = [f.take(LC) for _ in range(LANES)]
        gate_f = [[f.take(HALF) for _ in range(4)] for _ in range(LANES)]
        cell_f = [f.take(HALF) for _ in range(LANES)]
        hs_f = [f.take(HALF) for _ in range(LANES)]

        w = Area(xs_all)
        raw = {"ih": w.take(SKIPS * 4 * P), "hh": w.take((SKIPS - 1) * 4 * P), "g0": w.take(P), "g1": w.take(P),
               "adjT": w.take(P), "qkv": w.take(3 * P), "adj": w.take(P), "bg0": w.take(P)}
        splits = [("ih", wih_r), ("hh", whh_r), ("g0", wg0_r), ("g1", wg1_r), ("adjT", adjT_r), ("qkv", wqkv_r)]

        early.close()

        mid = ExitStack()
        rm = Area(mid.enter_context(nc.sbuf_tensor("attention_rounded", [P, 20 * GC], F32R)))
        xT_r, q_r = pair(rm, GC), pair(rm, GC)
        kd_r = [pair(rm, HEADS * GC) for _ in range(2)]
        fm = Area(mid.enter_context(nc.sbuf_tensor("attention_scratch", [P, 17 * GC], F32)))
        xg = fm.take(GC)
        prob = [fm.take(HEADS * P) for _ in range(GB)]
        probT = [fm.take(HEADS * P) for _ in range(GB)]
        vals = [fm.take(GB * HEADS * VW) for _ in range(2)]
        attT = [fm.take(GC) for _ in range(2)]
        y_f = fm.take(GC)
        mid.close()

        r2 = Area(sb("late_rounded", 14 * GC + 2 * 11 * P, F32R))
        area = sb("late_area", B * P)
        hid_at = r2.at
        hid_r = [pair(r2, 2 * GC) for _ in range(2)]
        mix_r = pair(Area(r2.whole, hid_at), GB * 3 * P)
        x2_r = pair(r2, GC)
        agg_r = [pair(r2, GC) for _ in range(2)]
        x3_r = agg_r
        w1_r, w2_r, w3_r = pair(r2, 2 * P), pair(r2, 2 * P), pair(r2, 3 * P)
        hatT_r, adjk_r = pair(r2, P), pair(r2, 3 * P)

        f2 = Area(area)
        raw2 = {"w1": f2.take(2 * P), "w2": f2.take(2 * P), "w3": f2.take(3 * P), "hatT": f2.take(P),
                "adjk": f2.take(3 * P)}
        nadj, nadjT = f2.take(P), f2.take(P)
        diag = f2.take(P)
        splits2 = [("w1", w1_r), ("w2", w2_r), ("w3", w3_r), ("hatT", hatT_r), ("adjk", adjk_r)]
        misc = sb("late_scratch", 6208)
        f3 = Area(misc)
        bn1_stats = f3.take(GROUPS * 2 * 6)
        bn2_stats = f3.take(GROUPS * 6)
        hid_f = [f3.take(GC) for _ in range(2)]
        z_f = f3.take(GC)
        y3 = f3.take(GC)
        x3_f = [f3.take(GC) for _ in range(2)]
        y4 = f3.take(GC)
        oT_f = f3.take(GC)
        o_f = [f3.take(GC) for _ in range(2)]

        weights_in = sem("weights_in")
        late_weights_in = sem("late_weights_in")
        ident_zero, ident_one = sem("ident_zero"), sem("ident_one")
        weights_hi, weights_lo = sem("weights_hi"), sem("weights_lo")
        rowsum_product = sem("rowsum_product")
        bias0_made, consts_made = sem("bias0_made"), sem("consts_made")
        pow_ready = sem("pow_ready")
        ones_made = sem("ones_made")

        x_loaded = lane_sems("x_loaded")
        x_again = lane_sems("x_again")
        x_hi, x_lo = lane_sems("x_hi"), lane_sems("x_lo")
        gcn_sums = lane_sems("gcn_sums")
        gcn_biased = lane_sems("gcn_biased")
        gcn_hi, gcn_lo = lane_sems("gcn_hi"), lane_sems("gcn_lo")
        gate_sums = lane_sems("gate_sums")
        gates_open = lane_sems("gates_open")
        cell_parts = lane_sems("cell_parts")
        cells = lane_sems("cells")
        cell_tanh = lane_sems("cell_tanh")
        states = lane_sems("states")
        states_hi, states_lo = lane_sems("states_hi"), lane_sems("states_lo")
        h_turned = lane_sems("h_turned")
        norm_work = lane_sems("norm_work")
        variances, rstds = lane_sems("variances"), lane_sems("rstds")
        x1_kept = lane_sems("x1_kept")

        def mm3(pe, out, wt, mv, start=True, stop=True):
            pe.matmul(out, wt[0], mv[0], start=start, stop=False)
            pe.matmul(out, wt[1], mv[0], start=False, stop=False)
            return pe.matmul(out, wt[0], mv[1], start=False, stop=stop)

        def f32(ap):
            return ap.bitcast(F32)

        def by_batch(ap, n):
            return ap.rearrange("q (b t) -> q b t", b=n)

        def windows(ap, step):
            p, t, half, nw, _ = step
            if half is not None:
                return ap[:, half * HALF:(half + 1) * HALF]
            return by_batch(ap, LB)[:, :, 0:nw * p].rearrange("q b (w p) -> q b w p", p=p)[:, :, :, t]

        def step_cols(step):
            return HALF if step[2] is not None else LB * step[3]

        def like_windows(ap, step):
            n = step_cols(step)
            return ap[:, 0:n] if step[2] is not None else ap[:, 0:n].rearrange("q (b w) -> q b w", b=LB)

        def bank(lane, n):
            return banks[:, 4 * lane + n, :]

        def ln_cols(s, nb):
            t = small[s]
            st = t[:, 0:6 * nb].rearrange("q (b k) -> q b k", k=6)
            rest = [t[:, 6 * LB + j * LB:6 * LB + j * LB + nb] for j in range(6)]
            return st, rest

        def ln_statistics(dve, y, s, nb, work, base, done, negate=False):
            st, (d, m2, q, mean, var, _) = ln_cols(s, nb)
            for b in range(nb):
                ins = nc.vector.bn_stats(st[:, b, :], y[:, b * P:(b + 1) * P])
            ins.then_inc(work, 1)
            dve.wait_ge(work, base + 1)
            nc.vector.tensor_tensor(d, st[:, :, 1], st[:, :, 4], ALU.subtract)
            nc.vector.scalar_tensor_tensor(out=m2, in0=st[:, :, 2], scalar=P * EPS, in1=st[:, :, 5],
                                           op0=ALU.add, op1=ALU.add).then_inc(work, 1)
            dve.wait_ge(work, base + 2)
            nc.vector.scalar_tensor_tensor(out=q, in0=d, scalar=0.25, in1=d, op0=ALU.mult, op1=ALU.mult)
            nc.vector.scalar_tensor_tensor(out=mean, in0=d, scalar=-0.5 if negate else 0.5, in1=st[:, :, 4],
                                           op0=ALU.mult, op1=ALU.subtract if negate else ALU.add).then_inc(work, 1)
            dve.wait_ge(work, base + 3)
            nc.vector.scalar_tensor_tensor(out=var, in0=m2, scalar=1.0 / P, in1=q,
                                           op0=ALU.mult, op1=ALU.add).then_inc(done, 1)

        def ln_rstd(s, nb):
            _, (_, _, _, _, var, rstd) = ln_cols(s, nb)
            return nc.gpsimd.tensor_tensor(rstd, var, minus_half[:, 0:nb], ALU.pow)

        def ln_apply(dst, y, s, nb):
            _, (_, _, _, mean, _, rstd) = ln_cols(s, nb)
            for b in range(nb):
                ins = nc.vector.tensor_scalar(dst[:, b * P:(b + 1) * P], y[:, b * P:(b + 1) * P],
                                              mean[:, b:b + 1], rstd[:, b:b + 1], ALU.subtract, ALU.mult)
            return ins

        xg_copied, x_turned, xT_hi, xT_lo = sem("xg_copied"), sem("x_turned"), sem("xT_hi"), sem("xT_lo")
        k_sums, k_hi, k_lo, q_sums, q_hi, q_lo = (sem("k_sums"), sem("k_hi"), sem("k_lo"), sem("q_sums"),
                                                  sem("q_hi"), sem("q_lo"))
        v_sums, v_kept, v_ones, k_zeros = sem("v_sums"), sem("v_kept"), sem("v_ones"), sem("k_zeros")
        scores, row_max, shifted, exps = sem("scores"), sem("row_max"), sem("shifted"), sem("exps")
        prob_turned, probT_kept, attended = sem("prob_turned"), sem("probT_kept"), sem("attended")
        y_sums = sem("y_sums")
        att_kept, att_turned = sem("att_kept"), sem("att_turned")
        att_work, var2, rstd2, x2_kept = sem("att_work"), sem("var2"), sem("rstd2"), sem("x2_kept")
        ATT_WORK = 5
        hat_work_done, hat_pow, hat_product, hat_turned = (sem("hat_work_done"), sem("hat_pow"),
                                                           sem("hat_product"), sem("hat_turned"))
        adjk_made = sem("adjk_made")
        late_hi, late_lo = sem("late_hi"), sem("late_lo")
        x2_hi, x2_lo, agg_sums, agg_kept, agg_hi, agg_lo = (sem("x2_hi"), sem("x2_lo"), sem("agg_sums"),
                                                            sem("agg_kept"), sem("agg_hi"), sem("agg_lo"))
        w1_sums, bn1_done = sem("w1_sums"), sem("bn1_done")
        bn_work_done, bn_var, bn_rstd = sem("bn_work_done"), sem("bn_var"), sem("bn_rstd")
        aggb_hi, aggb_lo, w1b_sums, hid_kept, hid_hi, hid_lo = (sem("aggb_hi"), sem("aggb_lo"), sem("w1b_sums"),
                                                                sem("hid_kept"), sem("hid_hi"), sem("hid_lo"))
        w2_sums, z_kept, bn2_done = sem("w2_sums"), sem("z_kept"), sem("bn2_done")
        z_scaled, z_turned, ln3_work, var3, rstd3, x3_kept = (sem("z_scaled"), sem("z_turned"), sem("ln3_work"),
                                                              sem("var3"), sem("rstd3"), sem("x3_kept"))
        x3_hi, x3_lo, mixed, mixed_hi, mixed_lo = (sem("x3_hi"), sem("x3_lo"), sem("mixed"), sem("mixed_hi"),
                                                   sem("mixed_lo"))
        w3_sums, w3_kept, o_turned = sem("w3_sums"), sem("w3_kept"), sem("o_turned")
        ln4_work, var4, rstd4, shift4 = sem("ln4_work"), sem("var4"), sem("rstd4"), sem("shift4")
        out_ready, out_stored = sem("out_ready"), [sem(f"out_stored_{u}") for u in range(2)]

        NW = 14

        def key_block(ap, h):
            return ap.rearrange("q (b h j) -> q b h j", b=GB, h=HEADS)[h * DH:(h + 1) * DH, :, h, :]

        def xcols(g, n=GC):
            if isinstance(g, int):
                return xs_all[:, g * n:(g + 1) * n]
            return xs_all[:, bass.ds(g * n, n)]

        def acols(g):
            if isinstance(g, int):
                return area[:, g * GC:(g + 1) * GC]
            return area[:, bass.ds(g * GC, GC)]

        def round_batches(rr, lane):
            first = rr * (LANES * LB) + lane * LB
            return slice(first, first + LB) if isinstance(first, int) else bass.ds(first, LB)

        block = ctx.enter_context(nc.Block())

        @block.sync
        def _(sp):
            def load(dst, src):
                sp.dma_start(dst, src).then_inc(weights_in, 16)

            load(raw["adjT"], adjT)
            load(raw["g0"], Wg0)
            load(raw["g1"], Wg1)
            load(raw["adj"], adj)
            load(raw["bg0"], bg0.unsqueeze(0).broadcast_to([P, P]))
            for b in range(GB):
                load(gcn_bias1[:, b * P:(b + 1) * P], bg1.unsqueeze(0).broadcast_to([P, P]))
            load(raw["ih"], WihT)
            load(raw["hh"], WhhT)
            load(bias_parts[:, 0:SKIPS * 4], bih)
            load(bias_parts[:, SKIPS * 4:2 * SKIPS * 4], bhh)
            load(raw["qkv"], Wqkv)

            def do(what, n, lane, rr):
                if what == "split":
                    wait_if(sp, x_lo[lane], rr)
                    sp.dma_start(by_batch(x_in[lane], LB), x_sbd[:, round_batches(rr, lane), :])\
                      .then_inc(x_loaded[lane], 16)
                if what == "lstm" and n == 0:
                    sp.wait_ge(gcn_hi[lane], rr * 8 + 8)
                    sp.wait_ge(gcn_lo[lane], rr * 8 + 8)
                    sp.dma_start(by_batch(tmp[lane], LB), x_sbd[:, round_batches(rr, lane), :])\
                      .then_inc(x_again[lane], 16)

            cycles(sp, do)

            for lane in range(LANES):
                sp.wait_ge(x1_kept[lane], ROUNDS)
            sp.wait_ge(x2_kept, GROUPS)
            for dst, src in ((raw2["w1"], W1T), (raw2["w2"], W2T), (raw2["w3"], W3), (nadj, adj), (nadjT, adjT)):
                sp.dma_start(dst, src).then_inc(late_weights_in, 16)
            sp.dma_start(out_bias, bias3.unsqueeze(1)).then_inc(late_weights_in, 16)
            for j, v in enumerate((b1, g1, be1)):
                sp.dma_start(bn_cols[:, 2 * j:2 * j + 2], v).then_inc(late_weights_in, 16)
            for j, v in enumerate((b2, g2, be2)):
                sp.dma_start(bn_cols[:, 6 + j:7 + j], v.unsqueeze(1)).then_inc(late_weights_in, 16)

            def put(pair_no, u):
                g = pair_no * 2 + u
                sp.wait_ge(out_ready, g + 1)
                first = g * GB
                rows = slice(first, first + GB) if isinstance(first, int) else bass.ds(first, GB)
                sp.dma_start(out_tbd[:, rows, :], by_batch(o_f[u], GB)).then_inc(out_stored[u], 16)

            with sp.Fori(0, GROUPS // 2) as i:
                for u in range(2):
                    put(i, u)
            for u in range(2):
                sp.wait_ge(out_stored[u], 16 * (GROUPS // 2))

        LATE = 5 + 1 + 6

        @block.gpsimd
        def _(pool):
            nc.gpsimd.memset(ident, 0.0).then_inc(ident_zero, 1)
            nc.gpsimd.memset(minus_half, -0.5).then_inc(pow_ready, 1)
            nc.gpsimd.memset(ones_sq, 1.0).then_inc(ones_made, 1)
            pool.wait_ge(ident_zero, 1)
            nc.gpsimd.affine_select(out=ident, in_=ident, compare_op=ALU.not_equal, fill=1.0, base=0,
                                    pattern=[[-1, P]], channel_multiplier=1).then_inc(ident_one, 1)
            for n, (name, (hi, lo)) in enumerate(splits):
                pool.wait_ge(weights_hi, n + 1)
                nc.gpsimd.tensor_tensor(lo, raw[name], f32(hi), ALU.subtract).then_inc(weights_lo, 1)

            pool.wait_ge(pow_ready, 1)

            def do(what, n, lane, rr):
                if what == "split":
                    pool.wait_ge(x_hi[lane], rr + 1)
                    nc.gpsimd.tensor_tensor(x_r[lane][1], x_in[lane], f32(x_r[lane][0]), ALU.subtract)\
                      .then_inc(x_lo[lane], 1)
                if what == "norm":
                    pool.wait_ge(variances[lane], rr + 1)
                    ln_rstd(lane, LB).then_inc(rstds[lane], 1)

            cycles(pool, do)

            for lane in range(LANES):
                pool.wait_ge(x1_kept[lane], ROUNDS)
            for place in range(2):
                nc.gpsimd.memset(vals[place], 1.0).then_inc(v_ones, 1)
                for part in kd_r[place]:
                    nc.gpsimd.memset(f32(part), 0.0).then_inc(k_zeros, 1)

            def do(what, part, g, place):
                if what == "copy":
                    wait_if(pool, x_turned, g)
                    nc.gpsimd.tensor_copy(xg, xcols(g)).then_inc(xg_copied, 1)
                if what == "rstd":
                    pool.wait_ge(var2, g + 1)
                    ln_rstd(0, GB).then_inc(rstd2, 1)
                if what == "add":
                    pool.wait_ge(att_work, g * ATT_WORK + 2)
                    nc.gpsimd.tensor_tensor(y_f, y_f, xcols(g), ALU.add).then_inc(y_sums, 1)

            groups(pool, [("copy", 0, 0), ("add", 0, 2), ("rstd", 0, 2)], do)

            pool.wait_ge(late_weights_in, 16 * LATE)
            for k, (comp, sign) in enumerate(((ALU.is_equal, 1), (ALU.is_gt, 1), (ALU.is_gt, -1))):
                nc.gpsimd.affine_select(out=raw2["adjk"][:, k * P:(k + 1) * P], in_=nadjT, compare_op=comp, fill=0.0,
                                        base=0, pattern=[[-sign, P]], channel_multiplier=sign).then_inc(adjk_made, 1)
            pool.wait_ge(hat_work_done, 4)
            nc.gpsimd.tensor_tensor(hat_work[:, 5:6], hat_work[:, 4:5], minus_half[:, 0:1], ALU.pow)\
              .then_inc(hat_pow, 1)
            for n, (name, (hi, lo)) in enumerate(splits2):
                pool.wait_ge(late_hi, n + 1)
                nc.gpsimd.tensor_tensor(lo, raw2[name], f32(hi), ALU.subtract).then_inc(late_lo, 1)

            def x2_low(g):
                pool.wait_ge(x2_hi, g + 1)
                nc.gpsimd.tensor_tensor(x2_r[1], xcols(g), f32(x2_r[0]), ALU.subtract).then_inc(x2_lo, 1)

            x2_low(0)
            with pool.Fori(1, GROUPS) as g:
                x2_low(g)

            pool.wait_ge(bn_var, 1)
            nc.gpsimd.tensor_tensor(bn_work[:, 8:10], bn_work[:, 6:8], minus_half[:, 0:2], ALU.pow)\
              .then_inc(bn_rstd, 1)

            def second_pass(i, u):
                g = i * 2 + u
                pool.wait_ge(aggb_hi, g + 1)
                nc.gpsimd.tensor_tensor(agg_r[u][1], acols(g), f32(agg_r[u][0]), ALU.subtract).then_inc(aggb_lo, 1)

            def hidden_low(i, u):
                g = i * 2 + u
                pool.wait_ge(hid_hi, g * 2 + 2)
                nc.gpsimd.tensor_tensor(hid_r[u][1][:, GC:2 * GC], hid_f[1], f32(hid_r[u][0][:, GC:2 * GC]),
                                        ALU.subtract).then_inc(hid_lo, 1)

            second_pass(0, 0)
            with pool.Fori(0, GROUPS // 2 - 1) as i:
                second_pass(i, 1)
                hidden_low(i, 0)
                second_pass(i + 1, 0)
                hidden_low(i, 1)
            second_pass(GROUPS // 2 - 1, 1)
            hidden_low(GROUPS // 2 - 1, 0)
            hidden_low(GROUPS // 2 - 1, 1)

            pool.wait_ge(bn_var, 2)
            nc.gpsimd.tensor_tensor(bn_work[:, 8:9], bn_work[:, 6:7], minus_half[:, 0:1], ALU.pow)\
              .then_inc(bn_rstd, 1)

            def do(what, part, g, place):
                if what == "third":
                    pool.wait_ge(var3, g + 1)
                    ln_rstd(0, GB).then_inc(rstd3, 1)
                if what == "third_low":
                    pool.wait_ge(x3_hi, g + 1)
                    nc.gpsimd.tensor_tensor(x3_r[place][1], x3_f[place], f32(x3_r[place][0]), ALU.subtract)\
                      .then_inc(x3_lo, 1)
                if what == "fourth":
                    pool.wait_ge(var4, g + 1)
                    wait_if(pool, out_ready, g)
                    ln_rstd(1, GB).then_inc(rstd4, 1)
                    pool.wait_ge(rstd4, g + 1)
                    _, (_, _, _, mean, _, rstd) = ln_cols(1, GB)
                    nc.gpsimd.tensor_tensor(shift_cols, mean, rstd, ALU.mult).then_inc(shift4, 1)

            groups(pool, [("third", 0, 0), ("third_low", 0, 0), ("fourth", 0, 2)], do)

        @block.scalar
        def _(act):
            def copy(dst, src):
                return nc.scalar.activation(dst, src, ACT.Copy)

            act.wait_ge(weights_in, 16 * NW)
            for name, (hi, _) in splits:
                copy(hi, raw[name]).then_inc(weights_hi, 1)
            act.wait_ge(rowsum_product, 1)
            for b in range(GB):
                ins = copy(gcn_bias0[:, b * P:(b + 1) * P], bank(0, 0)[:, 0:P])
            ins.then_inc(bias0_made, 1)
            act.wait_ge(consts_made, 1)

            def do(what, n, lane, rr):
                if what == "split":
                    act.wait_ge(x_loaded[lane], rr * 16 + 16)
                    wait_if(act, gcn_sums[lane], rr * 8 - 6)
                    copy(x_r[lane][0], x_in[lane]).then_inc(x_hi[lane], 1)
                if what == "gcn":
                    for half in range(2):
                        cols = slice(half * HALF, (half + 1) * HALF)
                        k = 2 * n + half
                        if n == 0:
                            act.wait_ge(gcn_sums[lane], rr * 8 + k + 1)
                            copy(mid_r[lane][0][:, cols], bank(lane, half)).then_inc(gcn_hi[lane], 1)
                        elif n == 1:
                            act.wait_ge(gcn_biased[lane], rr * 4 + half + 1)
                            nc.scalar.activation(h_r[lane][0][:, cols], tmp[lane][:, cols], ACT.Relu)\
                              .then_inc(gcn_hi[lane], 1)
                        elif n == 2:
                            act.wait_ge(gcn_biased[lane], rr * 4 + 2 + half + 1)
                            copy(mid_r[lane][0][:, cols], tmp[lane][:, cols]).then_inc(gcn_hi[lane], 1)
                        else:
                            act.wait_ge(gcn_sums[lane], rr * 8 + k + 1)
                            nc.scalar.activation(h_r[lane][0][:, cols], bank(lane, 2 + half), ACT.Relu)\
                              .then_inc(gcn_hi[lane], 1)
                if what == "lstm":
                    step = STEPS[n]
                    cols = step_cols(step)
                    if n:
                        act.wait_ge(states[lane], rr * NSTEP + n)
                    for j, gate in enumerate(step[4]):
                        act.wait_ge(gate_sums[lane], rr * NGATE + gate_at[n] + j + 1)
                        at = (step[0] - 1) * 4 + gate
                        nc.scalar.activation(gate_f[lane][gate][:, 0:cols], bank(lane, gate)[:, 0:cols],
                                             ACT.Tanh if gate == G else ACT.Sigmoid,
                                             bias=lstm_bias[:, at:at + 1]).then_inc(gates_open[lane], 1)
                    act.wait_ge(cells[lane], rr * NSTEP + n + 1)
                    nc.scalar.activation(gate_f[lane][G][:, 0:cols], cell_f[lane][:, 0:cols], ACT.Tanh)\
                      .then_inc(cell_tanh[lane], 1)

            cycles(act, do)

            act.wait_ge(k_zeros, 4)

            def do(what, part, g, place):
                if what == "turned":
                    act.wait_ge(x_turned, g + 1)
                    wait_if(act, v_sums, g)
                    copy(xT_r[0], banks[:, 4, :]).then_inc(xT_hi, 1)
                if what == "keys":
                    act.wait_ge(k_sums, g + 1)
                    wait_if(act, scores, (g - 1) * GB)
                    for h in range(HEADS):
                        copy(key_block(kd_r[place][0], h), by_batch(banks[h * DH:(h + 1) * DH, 4, :], GB))\
                            .then_inc(k_hi, 1)
                if what == "queries":
                    act.wait_ge(q_sums, g + 1)
                    wait_if(act, scores, g * GB)
                    nc.scalar.activation(q_r[0], banks[:, 5, :], ACT.Copy, scale=DH ** -0.5).then_inc(q_hi, 1)
                if what == "exp":
                    act.wait_ge(shifted, g * GB + part + 1)
                    nc.scalar.activation(prob[part], prob[part], ACT.Exp).then_inc(exps, 1)
                if what == "probT":
                    act.wait_ge(prob_turned, g * GB + part + 1)
                    wait_if(act, attended, (g - 1) * GB + part + 1)
                    copy(probT[part], banks[:, 2 + part % 2, :]).then_inc(probT_kept, 1)
                if what == "attended":
                    act.wait_ge(attended, g * GB + GB)
                    for j in range(2):
                        copy(attT[j], banks[:, 6 + j, :]).then_inc(att_kept, 1)

            groups(act, [("exp", 0, 1), ("probT", 3, 2), ("exp", 1, 1), ("attended", 0, 2), ("turned", 0, 0),
                         ("exp", 2, 1), ("probT", 0, 1), ("keys", 0, 0), ("exp", 3, 1), ("queries", 0, 0),
                         ("probT", 1, 1), ("probT", 2, 1)], do)

            act.wait_ge(late_weights_in, 16 * LATE)
            act.wait_ge(adjk_made, 3)
            act.wait_ge(hat_turned, 1)
            for name, (hi, _) in splits2:
                copy(hi, raw2[name]).then_inc(late_hi, 1)

            def first_pass_x(g):
                wait_if(act, agg_sums, g)
                copy(x2_r[0], xcols(g)).then_inc(x2_hi, 1)

            def first_pass(g):
                act.wait_ge(agg_sums, g + 1)
                wait_if(act, w1_sums, g * 2)
                copy(agg_r[0][0], banks[:, 0, :]).then_inc(agg_hi, 1)
                copy(acols(g), banks[:, 0, :]).then_inc(agg_kept, 1)

            act.wait_ge(late_lo, len(splits2))
            first_pass_x(0)
            first_pass_x(1)
            first_pass(0)
            with act.Fori(1, GROUPS - 1) as g:
                first_pass_x(g + 1)
                first_pass(g)
            first_pass(GROUPS - 1)

            act.wait_ge(bn_work_done, 6)

            def hidden(i, u):
                g = i * 2 + u
                for m in range(2):
                    act.wait_ge(w1b_sums, g * 2 + m + 1)
                    wait_if(act, hid_lo, g * 2)
                    nc.scalar.activation(hid_f[m], banks[:, 2 * u + m, :], ACT.Relu, bias=bn_work[:, 14 + m:15 + m],
                                         scale=bn_work[:, 10 + m:11 + m]).then_inc(hid_kept, 1)

            def second_sums(i, u):
                g = i * 2 + u
                act.wait_ge(w2_sums, g + 1)
                copy(acols(g), banks[:, 4 + u, :]).then_inc(z_kept, 1)

            def hidden_pair(i):
                hidden(i, 1)
                second_sums(i, 0)
                hidden(i + 1, 0)
                second_sums(i, 1)

            hidden(0, 0)
            hidden_pair(0)
            with act.Fori(1, GROUPS // 2 - 1) as i:
                hidden_pair(i)
            hidden(GROUPS // 2 - 1, 1)
            second_sums(GROUPS // 2 - 1, 0)
            second_sums(GROUPS // 2 - 1, 1)

            act.wait_ge(bn_work_done, 11)

            def do(what, part, g, place):
                if what == "scaled":
                    wait_if(act, z_turned, g)
                    nc.scalar.activation(z_f, acols(g), ACT.Identity, bias=bn_work[:, 14:15],
                                         scale=bn_work[:, 10:11]).then_inc(z_scaled, 1)
                if what == "x3":
                    act.wait_ge(x3_kept, g + 1)
                    wait_if(act, mixed, (g - 1) * GB)
                    copy(x3_r[place][0], x3_f[place]).then_inc(x3_hi, 1)
                if what == "mixed":
                    act.wait_ge(mixed, g * GB + part + 1)
                    wait_if(act, w3_sums, g)
                    at = part * 3 * P
                    copy(mix_r[0][:, at:at + 3 * P], banks[:, 2 + part, 0:3 * P]).then_inc(mixed_hi, 1)
                if what == "sums":
                    act.wait_ge(w3_sums, g + 1)
                    wait_if(act, o_turned, g)
                    nc.scalar.activation(oT_f, banks[:, 1, :], ACT.Identity, bias=out_bias).then_inc(w3_kept, 1)
                if what == "norm":
                    act.wait_ge(shift4, g + 1)
                    wait_if(act, out_stored[place], (g - place) * 8)
                    _, (_, _, _, _, _, rstd) = ln_cols(1, GB)
                    for b in range(GB):
                        ins = nc.scalar.activation(o_f[place][:, b * P:(b + 1) * P], y4[:, b * P:(b + 1) * P],
                                                   ACT.Identity, bias=shift_cols[:, b:b + 1], scale=rstd[:, b:b + 1])
                    ins.then_inc(out_ready, 1)

            groups(act, [("scaled", 0, 0)] + [("mixed", b, 1) for b in range(GB)] + [("x3", 0, 0), ("sums", 0, 1),
                         ("norm", 0, 2)], do)

        @block.vector
        def _(dve):
            dve.wait_ge(weights_in, 16 * NW)
            dve.wait_ge(ident_one, 1)
            nc.vector.tensor_tensor(lstm_bias, bias_parts[:, 0:4 * SKIPS], bias_parts[:, 4 * SKIPS:8 * SKIPS], ALU.add)
            nc.vector.tensor_copy(ident_bf[:, :], ident)
            for b in range(GB):
                ins = nc.vector.tensor_scalar(mask[:, b * P:(b + 1) * P], raw["adj"], 0.0, MASKED,
                                              ALU.is_equal, ALU.mult)
            ins.then_inc(consts_made, 1)
            dve.wait_ge(bias0_made, 1)

            def do(what, n, lane, rr):
                if what == "gcn":
                    for half in range(2):
                        cols = slice(half * HALF, (half + 1) * HALF)
                        k = 2 * n + half
                        if n == 0:
                            dve.wait_ge(gcn_hi[lane], rr * 8 + k + 1)
                            nc.vector.tensor_tensor(mid_r[lane][1][:, cols], bank(lane, half),
                                                    f32(mid_r[lane][0][:, cols]), ALU.subtract)\
                              .then_inc(gcn_lo[lane], 1)
                        elif n == 1 or n == 2:
                            dve.wait_ge(gcn_sums[lane], rr * 8 + k + 1)
                            nc.vector.tensor_tensor(tmp[lane][:, cols], bank(lane, (2 if n == 1 else 0) + half),
                                                    gcn_bias0 if n == 1 else gcn_bias1, ALU.add)\
                              .then_inc(gcn_biased[lane], 1)
                            dve.wait_ge(gcn_hi[lane], rr * 8 + k + 1)
                            dst = (h_r if n == 1 else mid_r)[lane]
                            nc.vector.scalar_tensor_tensor(
                                out=dst[1][:, cols], in0=tmp[lane][:, cols], scalar=0.0,
                                in1=f32(dst[0][:, cols]), op0=ALU.max if n == 1 else ALU.add,
                                op1=ALU.subtract).then_inc(gcn_lo[lane], 1)
                        else:
                            dve.wait_ge(gcn_hi[lane], rr * 8 + k + 1)
                            nc.vector.scalar_tensor_tensor(
                                out=h_r[lane][1][:, cols], in0=bank(lane, 2 + half), scalar=0.0,
                                in1=f32(h_r[lane][0][:, cols]), op0=ALU.max, op1=ALU.subtract)\
                              .then_inc(gcn_lo[lane], 1)
                if what == "lstm":
                    step = STEPS[n]
                    p, t, _, _, gates = step
                    cols = step_cols(step)
                    gi, gf, gg, go = (gate_f[lane][q][:, 0:cols] for q in range(4))
                    cell = cell_f[lane][:, 0:cols]
                    at = rr * NGATE + gate_at[n]
                    dve.wait_ge(gates_open[lane], at + 2)
                    if t == 0:
                        nc.vector.tensor_tensor(cell, gi, gg, ALU.mult).then_inc(cells[lane], 1)
                    else:
                        later = rr * NLATER + sum(q[1] > 0 for q in STEPS[:n])
                        nc.vector.tensor_tensor(gi, gi, gg, ALU.mult)
                        dve.wait_ge(gates_open[lane], at + 3)
                        nc.vector.tensor_tensor(cell, gf, cell, ALU.mult).then_inc(cell_parts[lane], 1)
                        dve.wait_ge(cell_parts[lane], later + 1)
                        nc.vector.tensor_tensor(cell, cell, gi, ALU.add).then_inc(cells[lane], 1)
                    last = t == p - 1
                    src = h_f[lane] if last else hs_f[lane]
                    dst = h_r[lane] if last else hs_r[lane]
                    view = (lambda a: windows(a, step)) if last else (lambda a: like_windows(a, step))
                    dve.wait_ge(cell_tanh[lane], rr * NSTEP + n + 1)
                    nc.vector.tensor_tensor(view(src), like_windows(gate_f[lane][O], step),
                                            like_windows(gate_f[lane][G], step), ALU.mult).then_inc(states[lane], 1)
                    if n == NSTEP - 1:
                        return
                    dve.wait_ge(states[lane], rr * NSTEP + n + 1)
                    nc.vector.tensor_copy(view(dst[0]), view(src)).then_inc(states_hi[lane], 1)
                    dve.wait_ge(states_hi[lane], rr * (NSTEP - 1) + n + 1)
                    nc.vector.tensor_tensor(view(dst[1]), view(src), f32(view(dst[0])), ALU.subtract)\
                      .then_inc(states_lo[lane], 1)
                if what == "residual":
                    dve.wait_ge(x_again[lane], rr * 16 + 16)
                    for half in range(2):
                        cols = slice(half * HALF, (half + 1) * HALF)
                        dve.wait_ge(h_turned[lane], rr * 2 + half + 1)
                        nc.vector.tensor_tensor(h_f[lane][:, cols], tmp[lane][:, cols], bank(lane, half), ALU.add)\
                          .then_inc(norm_work[lane], 1)
                if what == "statistics":
                    dve.wait_ge(norm_work[lane], rr * 5 + 2)
                    ln_statistics(dve, h_f[lane], lane, LB, norm_work[lane], rr * 5 + 2, variances[lane])
                if what == "norm":
                    dve.wait_ge(rstds[lane], rr + 1)
                    at = rr * LANES + lane
                    ln_apply(xcols(at, LC), h_f[lane], lane, LB).then_inc(x1_kept[lane], 1)

            cycles(dve, do)

            dve.wait_ge(v_ones, 2)

            def do(what, part, g, place):
                if what == "turned":
                    dve.wait_ge(xT_hi, g + 1)
                    nc.vector.tensor_tensor(xT_r[1], banks[:, 4, :], f32(xT_r[0]), ALU.subtract).then_inc(xT_lo, 1)
                if what == "keys":
                    dve.wait_ge(k_hi, g * HEADS + HEADS)
                    for h in range(HEADS):
                        hi, lo = (key_block(kd_r[place][j], h) for j in range(2))
                        ins = nc.vector.tensor_tensor(lo, by_batch(banks[h * DH:(h + 1) * DH, 4, :], GB), f32(hi),
                                                      ALU.subtract)
                    ins.then_inc(k_lo, 1)
                if what == "queries":
                    dve.wait_ge(q_hi, g + 1)
                    nc.vector.scalar_tensor_tensor(out=q_r[1], in0=banks[:, 5, :], scalar=DH ** -0.5, in1=f32(q_r[0]),
                                                   op0=ALU.mult, op1=ALU.subtract).then_inc(q_lo, 1)
                if what == "values":
                    dve.wait_ge(v_sums, g + 1)
                    wait_if(dve, attended, (g - 1) * GB)
                    nc.vector.tensor_copy(vals[place].rearrange("q (n d) -> q n d", d=VW)[:, :, 0:DH],
                                          banks[:, 5, :].rearrange("q (n d) -> q n d", d=DH)).then_inc(v_kept, 1)
                if what == "soft":
                    dve.wait_ge(scores, g * GB + part + 1)
                    score = banks[:, part % 2, :].rearrange("q (h j) -> q h j", h=HEADS)
                    largest = maxes[:, part * HEADS:(part + 1) * HEADS]
                    nc.vector.tensor_reduce(out=largest, in_=score, axis=AX.X, op=ALU.max).then_inc(row_max, 1)
                    dve.wait_ge(row_max, g * GB + part + 1)
                    wait_if(dve, prob_turned, (g - 1) * GB + part + 1)
                    nc.vector.tensor_tensor(prob[part].rearrange("q (h j) -> q h j", h=HEADS), score,
                                            largest.unsqueeze(2).broadcast_to([P, HEADS, P]),
                                            ALU.subtract).then_inc(shifted, 1)
                if what == "divide":
                    dve.wait_ge(att_turned, g + 1)
                    n = GB * HEADS // 2
                    outs = [banks[:, 6 + j, :].rearrange("q (b h d) -> q b h d", b=GB, h=2) for j in range(2)]
                    dens = [rden[:, j * n:(j + 1) * n].rearrange("q (b h) -> q b h", h=2) for j in range(2)]
                    for j in range(2):
                        ins = nc.vector.reciprocal(dens[j].unsqueeze(3), outs[j][:, :, :, DH:DH + 1])
                    ins.then_inc(att_work, 1)
                    dve.wait_ge(att_work, g * ATT_WORK + 1)
                    for j in range(2):
                        dst = y_f.rearrange("q (b k h d) -> q b k h d", b=GB, k=2, h=2)[:, :, j, :, :]
                        ins = nc.vector.tensor_tensor(dst, outs[j][:, :, :, 0:DH],
                                                      dens[j].unsqueeze(3).broadcast_to([P, GB, 2, DH]), ALU.mult)
                    ins.then_inc(att_work, 1)
                if what == "add":
                    dve.wait_ge(y_sums, g + 1)
                    ln_statistics(dve, y_f, 0, GB, att_work, g * ATT_WORK + 2, var2)
                if what == "norm":
                    dve.wait_ge(rstd2, g + 1)
                    ln_apply(xcols(g), y_f, 0, GB).then_inc(x2_kept, 1)

            groups(dve, [("soft", 0, 1), ("soft", 1, 1), ("values", 0, 1), ("turned", 0, 0), ("soft", 2, 1),
                         ("divide", 0, 2), ("keys", 0, 0), ("soft", 3, 1), ("queries", 0, 0), ("add", 0, 2),
                         ("norm", 0, 2)], do)

            dve.wait_ge(late_weights_in, 16 * LATE)
            dve.wait_ge(adjk_made, 3)
            nc.vector.tensor_tensor(nadj, nadj, ident, ALU.add)
            nc.vector.tensor_tensor(nadjT, nadjT, ident, ALU.add).then_inc(hat_work_done, 1)
            dve.wait_ge(hat_work_done, 1)
            nc.vector.tensor_reduce(out=hat_work[:, 0:1], in_=nadj, axis=AX.X, op=ALU.add)
            nc.vector.tensor_reduce(out=hat_work[:, 1:2], in_=nadjT, axis=AX.X, op=ALU.add)
            nc.vector.tensor_tensor(diag, nadj, ident, ALU.mult).then_inc(hat_work_done, 1)
            dve.wait_ge(hat_work_done, 2)
            nc.vector.tensor_reduce(out=hat_work[:, 2:3], in_=diag, axis=AX.X, op=ALU.add)
            nc.vector.tensor_tensor(hat_work[:, 3:4], hat_work[:, 0:1], hat_work[:, 1:2], ALU.add)\
              .then_inc(hat_work_done, 1)
            dve.wait_ge(hat_work_done, 3)
            nc.vector.tensor_tensor(hat_work[:, 4:5], hat_work[:, 3:4], hat_work[:, 2:3], ALU.subtract)\
              .then_inc(hat_work_done, 1)
            dve.wait_ge(hat_pow, 1)
            nc.vector.tensor_scalar(diag, ident, hat_work[:, 5:6], None, ALU.mult).then_inc(hat_work_done, 1)
            nc.vector.tensor_scalar(nadjT, nadjT, hat_work[:, 5:6], None, ALU.mult).then_inc(hat_work_done, 1)
            dve.wait_ge(hat_work_done, 6)
            dve.wait_ge(hat_product, 1)
            nc.vector.tensor_tensor(raw2["hatT"], nadjT, banks[:, 1, 0:P], ALU.mult).then_inc(hat_turned, 1)

            def first_low(g):
                dve.wait_ge(agg_kept, g + 1)
                nc.vector.tensor_tensor(agg_r[0][1], banks[:, 0, :], f32(agg_r[0][0]), ALU.subtract)\
                  .then_inc(agg_lo, 1)

            bn1_v = bn1_stats.rearrange("q (m g k) -> q m g k", m=2, k=6)
            bn2_v = bn2_stats.rearrange("q (g k) -> q g k", k=6)

            def stat_cols(v, g):
                return v[:, g, :] if isinstance(g, int) else v[:, bass.ds(g, 1), :].squeeze()

            def first_stats(g):
                for m in range(2):
                    dve.wait_ge(w1_sums, g * 2 + m + 1)
                    at = m * GROUPS * 6 + g * 6
                    dst = bn1_stats[:, at:at + 6] if isinstance(at, int) else bn1_stats[:, bass.ds(at, 6)]
                    nc.vector.bn_stats(dst, banks[:, 1 + m, :]).then_inc(bn1_done, 1)

            first_low(0)
            with dve.Fori(0, GROUPS - 1) as g:
                first_low(g + 1)
                first_stats(g)
            first_stats(GROUPS - 1)

            dve.wait_ge(bn1_done, 2 * GROUPS)
            for m in range(2):
                ins = nc.vector.bn_aggr(bn_work[:, 2 * m:2 * m + 2], bn1_v[:, m, :, :].rearrange("q g k -> q (g k)"))
            ins.then_inc(bn_work_done, 1)
            dve.wait_ge(bn_work_done, 1)
            mv = bn_work[:, 0:4].rearrange("q (m k) -> q m k", k=2)
            nc.vector.tensor_tensor(bn_work[:, 4:6], mv[:, :, 0], bn_cols[:, 0:2], ALU.add).then_inc(bn_work_done, 1)
            nc.vector.tensor_scalar(bn_work[:, 6:8], mv[:, :, 1], EPS, None, ALU.add).then_inc(bn_var, 1)
            dve.wait_ge(bn_work_done, 2)
            nc.vector.tensor_tensor(bn_work[:, 12:14], bn_cols[:, 0:2], bn_work[:, 4:6], ALU.subtract)\
              .then_inc(bn_work_done, 1)
            dve.wait_ge(bn_rstd, 1)
            nc.vector.tensor_tensor(bn_work[:, 10:12], bn_work[:, 8:10], bn_cols[:, 2:4], ALU.mult)\
              .then_inc(bn_work_done, 1)
            dve.wait_ge(bn_work_done, 4)
            nc.vector.tensor_tensor(bn_work[:, 16:18], bn_work[:, 12:14], bn_work[:, 10:12], ALU.mult)\
              .then_inc(bn_work_done, 1)
            dve.wait_ge(bn_work_done, 5)
            nc.vector.tensor_tensor(bn_work[:, 14:16], bn_work[:, 16:18], bn_cols[:, 4:6], ALU.add)\
              .then_inc(bn_work_done, 1)

            def agg_high(i, u):
                g = i * 2 + u
                wait_if(dve, w1b_sums, (g - 2) * 2 + 2)
                nc.vector.tensor_copy(agg_r[u][0], acols(g)).then_inc(aggb_hi, 1)

            def hidden_parts(i, u):
                g = i * 2 + u
                wait_if(dve, w2_sums, g - 1)
                for m in range(2):
                    cols = slice(m * GC, (m + 1) * GC)
                    dve.wait_ge(hid_kept, g * 2 + m + 1)
                    nc.vector.tensor_copy(hid_r[u][0][:, cols], hid_f[m]).then_inc(hid_hi, 1)
                dve.wait_ge(hid_hi, g * 2 + 2)
                nc.vector.tensor_tensor(hid_r[u][1][:, 0:GC], hid_f[0], f32(hid_r[u][0][:, 0:GC]), ALU.subtract)\
                  .then_inc(hid_lo, 1)

            def second_stats(i, u):
                g = i * 2 + u
                dve.wait_ge(z_kept, g + 1)
                at = g * 6
                dst = bn2_stats[:, at:at + 6] if isinstance(at, int) else bn2_stats[:, bass.ds(at, 6)]
                nc.vector.bn_stats(dst, acols(g)).then_inc(bn2_done, 1)

            agg_high(0, 0)
            agg_high(0, 1)
            hidden_parts(0, 0)
            agg_high(1, 0)
            hidden_parts(0, 1)
            second_stats(0, 0)
            with dve.Fori(1, GROUPS // 2 - 1) as i:
                agg_high(i, 1)
                hidden_parts(i, 0)
                second_stats(i - 1, 1)
                agg_high(i + 1, 0)
                hidden_parts(i, 1)
                second_stats(i, 0)
            last_pair = GROUPS // 2 - 1
            agg_high(last_pair, 1)
            hidden_parts(last_pair, 0)
            second_stats(last_pair - 1, 1)
            hidden_parts(last_pair, 1)
            second_stats(last_pair, 0)
            second_stats(last_pair, 1)

            dve.wait_ge(bn2_done, GROUPS)
            nc.vector.bn_aggr(bn_work[:, 0:2], bn2_stats).then_inc(bn_work_done, 1)
            dve.wait_ge(bn_work_done, 7)
            nc.vector.tensor_tensor(bn_work[:, 4:5], bn_work[:, 0:1], bn_cols[:, 6:7], ALU.add)\
              .then_inc(bn_work_done, 1)
            nc.vector.tensor_scalar(bn_work[:, 6:7], bn_work[:, 1:2], EPS, None, ALU.add).then_inc(bn_var, 1)
            dve.wait_ge(bn_work_done, 8)
            nc.vector.tensor_tensor(bn_work[:, 12:13], bn_cols[:, 6:7], bn_work[:, 4:5], ALU.subtract)\
              .then_inc(bn_work_done, 1)
            dve.wait_ge(bn_rstd, 2)
            dve.wait_ge(hid_kept, 2 * GROUPS)
            nc.vector.tensor_tensor(bn_work[:, 10:11], bn_work[:, 8:9], bn_cols[:, 7:8], ALU.mult)\
              .then_inc(bn_work_done, 1)
            dve.wait_ge(bn_work_done, 10)
            nc.vector.scalar_tensor_tensor(out=bn_work[:, 14:15], in0=bn_work[:, 12:13], scalar=bn_work[:, 10:11],
                                           in1=bn_cols[:, 8:9], op0=ALU.mult, op1=ALU.add).then_inc(bn_work_done, 1)

            def do(what, part, g, place):
                if what == "third":
                    dve.wait_ge(z_turned, g + 1)
                    nc.vector.tensor_tensor(y3, banks[:, 0, :], xcols(g), ALU.add).then_inc(ln3_work, 1)
                    dve.wait_ge(ln3_work, g * 4 + 1)
                    ln_statistics(dve, y3, 0, GB, ln3_work, g * 4 + 1, var3)
                if what == "third_norm":
                    dve.wait_ge(rstd3, g + 1)
                    wait_if(dve, x3_lo, g - 1)
                    ln_apply(x3_f[place], y3, 0, GB).then_inc(x3_kept, 1)
                if what == "mixed":
                    at = part * 3 * P
                    dve.wait_ge(mixed_hi, g * GB + part + 1)
                    nc.vector.tensor_tensor(mix_r[1][:, at:at + 3 * P], banks[:, 2 + part, 0:3 * P],
                                            f32(mix_r[0][:, at:at + 3 * P]), ALU.subtract).then_inc(mixed_lo, 1)
                if what == "fourth":
                    dve.wait_ge(o_turned, g + 1)
                    wait_if(dve, out_ready, g)
                    nc.vector.tensor_tensor(y4, banks[:, 6, :], x3_f[place], ALU.add).then_inc(ln4_work, 1)
                    dve.wait_ge(ln4_work, g * 4 + 1)
                    ln_statistics(dve, y4, 1, GB, ln4_work, g * 4 + 1, var4, negate=True)

            groups(dve, [("mixed", b, 1) for b in range(GB)] + [("third", 0, 0), ("fourth", 0, 2),
                         ("third_norm", 0, 0)], do)

        @block.tensor
        def _(pe):
            pe.wait_ge(weights_in, 16 * NW)
            pe.matmul(bank(0, 0)[:, 0:P], raw["bg0"], raw["adjT"], start=True, stop=True).then_inc(rowsum_product, 1)
            pe.wait_ge(weights_lo, len(splits))
            pe.wait_ge(ident_one, 1)
            pe.wait_ge(bias0_made, 1)

            def do(what, n, lane, rr):
                if what == "gcn":
                    for half in range(2):
                        k = 2 * n + half
                        out = bank(lane, (0, 2, 0, 2)[n] + half)
                        if n == 0:
                            pe.wait_ge(x_lo[lane], rr + 1)
                            wait_if(pe, norm_work[lane], rr * 5 - 3)
                        else:
                            pe.wait_ge(gcn_hi[lane], rr * 8 + 2 * (n - 1) + half + 1)
                            pe.wait_ge(gcn_lo[lane], rr * 8 + 2 * (n - 1) + half + 1)
                        if n == 1:
                            ins = mm3(pe, out, wg0_r, cut(mid_r[lane], half * HALF, (half + 1) * HALF))
                        else:
                            src = (x_r, None, h_r, mid_r)[n][lane]
                            moving = wg1_r if n == 2 else adjT_r
                            for b in range(LB // 2):
                                at = half * HALF + b * P
                                ins = mm3(pe, out[:, b * P:(b + 1) * P], cut(src, at, at + P), moving)
                        ins.then_inc(gcn_sums[lane], 1)
                if what == "lstm":
                    step = STEPS[n]
                    p, t, _, _, gates = step
                    if n == 0:
                        pe.wait_ge(gcn_hi[lane], rr * 8 + 7)
                        pe.wait_ge(gcn_lo[lane], rr * 8 + 7)
                    if n == 1:
                        pe.wait_ge(gcn_lo[lane], rr * 8 + 8)
                    inputs = [windows(h_r[lane][j], step) for j in range(2)]
                    if t == 0 and n > 1:
                        pe.wait_ge(states_lo[lane], rr * (NSTEP - 1) + n)
                    for j, gate in enumerate(gates):
                        out = like_windows(bank(lane, gate), step)
                        free = last_use[gate_at[n] + j]
                        if free is not None:
                            pe.wait_ge(gates_open[lane], rr * NGATE + free)
                        elif gate == O:
                            pe.wait_ge(gcn_lo[lane], rr * 8 + 8)
                        at = ((p - 1) * 4 + gate) * P
                        ins = mm3(pe, out, cut(wih_r, at, at + P), inputs, stop=(t == 0))
                        if t == 0:
                            ins.then_inc(gate_sums[lane], 1)
                    if t:
                        pe.wait_ge(states_lo[lane], rr * (NSTEP - 1) + n)
                        carried = [like_windows(hs_r[lane][j], step) for j in range(2)]
                        for gate in gates:
                            at = ((p - 2) * 4 + gate) * P
                            mm3(pe, like_windows(bank(lane, gate), step), cut(whh_r, at, at + P), carried,
                                start=False).then_inc(gate_sums[lane], 1)
                if what == "residual":
                    pe.wait_ge(states[lane], rr * NSTEP + NSTEP)
                    pe.wait_ge(gates_open[lane], rr * NGATE + NGATE)
                    for half in range(2):
                        for b in range(LB // 2):
                            at = half * HALF + b * P
                            ins = pe.transpose(bank(lane, half)[:, b * P:(b + 1) * P], h_f[lane][:, at:at + P], ident)
                        ins.then_inc(h_turned[lane], 1)

            cycles(pe, do)

            for lane in range(LANES):
                pe.wait_ge(x1_kept[lane], ROUNDS)

            def do(what, part, g, place):
                if what == "turn":
                    pe.wait_ge(xg_copied, g + 1)
                    wait_if(pe, k_lo, g)
                    for b in range(GB):
                        ins = pe.transpose(banks[:, 4, b * P:(b + 1) * P], xg[:, b * P:(b + 1) * P], ident)
                    ins.then_inc(x_turned, 1)
                if what == "keys":
                    pe.wait_ge(xT_lo, g + 1)
                    mm3(pe, banks[:, 4, :], cut(wqkv_r, P, 2 * P), xT_r).then_inc(k_sums, 1)
                if what == "queries":
                    wait_if(pe, v_kept, g)
                    mm3(pe, banks[:, 5, :], cut(wqkv_r, 0, P), xT_r).then_inc(q_sums, 1)
                if what == "values":
                    pe.wait_ge(q_lo, g + 1)
                    for b in range(GB):
                        ins = mm3(pe, banks[:, 5, b * P:(b + 1) * P], cut(xT_r, b * P, (b + 1) * P),
                                  cut(wqkv_r, 2 * P, 3 * P))
                    ins.then_inc(v_sums, 1)
                if what == "score":
                    if part == 0:
                        pe.wait_ge(k_lo, g + 1)
                        pe.wait_ge(q_lo, g + 1)
                    wait_if(pe, shifted, g * GB + part - 1)
                    out = banks[:, part % 2, :]
                    keys = kd_r[place]
                    at = part * HEADS * P
                    pe.matmul(out, ident_bf[:, :], mask[:, :], start=True, stop=False)
                    mm3(pe, out, cut(q_r, part * P, (part + 1) * P), cut(keys, at, at + HEADS * P), start=False)\
                        .then_inc(scores, 1)
                if what == "probT":
                    pe.wait_ge(exps, g * GB + part + 1)
                    wait_if(pe, probT_kept, g * GB + part - 1)
                    for h in range(HEADS):
                        ins = pe.transpose(banks[:, 2 + part % 2, h * P:(h + 1) * P],
                                           prob[part][:, h * P:(h + 1) * P], ident)
                    ins.then_inc(prob_turned, 1)
                if what == "attend":
                    if part == 0:
                        pe.wait_ge(v_kept, g + 1)
                        wait_if(pe, att_work, (g - 1) * ATT_WORK + 2)
                    pe.wait_ge(probT_kept, g * GB + part + 1)
                    for h in range(HEADS):
                        at, rows = (part * HEADS + h) * VW, (h % 2) * VW
                        ins = pe.matmul(banks[rows:rows + VW, 6 + h // 2, part * P:(part + 1) * P],
                                        vals[place][:, at:at + VW], probT[part][:, h * P:(h + 1) * P],
                                        start=True, stop=True)
                    ins.then_inc(attended, 1)
                if what == "attended":
                    pe.wait_ge(att_kept, g * 2 + 2)
                    for j in range(2):
                        for b in range(GB):
                            ins = pe.transpose(banks[:, 6 + j, b * P:(b + 1) * P], attT[j][:, b * P:(b + 1) * P],
                                               ident)
                    ins.then_inc(att_turned, 1)

            groups(pe, [("score", 0, 1), ("probT", 3, 2), ("score", 1, 1), ("attend", 2, 2), ("attend", 3, 2),
                        ("values", 0, 1), ("turn", 0, 0), ("score", 2, 1), ("attended", 0, 2), ("probT", 0, 1),
                        ("keys", 0, 0), ("attend", 0, 1), ("score", 3, 1), ("queries", 0, 0), ("probT", 1, 1),
                        ("attend", 1, 1), ("probT", 2, 1)], do)

            pe.wait_ge(hat_work_done, 5)
            pe.wait_ge(att_work, GROUPS * ATT_WORK)
            pe.wait_ge(ones_made, 1)
            pe.matmul(banks[:, 1, 0:P], ones_sq, diag, start=True, stop=True).then_inc(hat_product, 1)
            pe.wait_ge(late_lo, len(splits2))

            def aggregate(g):
                pe.wait_ge(x2_lo, g + 1)
                wait_if(pe, agg_kept, g)
                wait_if(pe, agg_lo, g)
                for b in range(GB):
                    ins = mm3(pe, banks[:, 0, b * P:(b + 1) * P], cut(x2_r, b * P, (b + 1) * P), hatT_r)
                ins.then_inc(agg_sums, 1)

            def first_layer(g):
                pe.wait_ge(agg_lo, g + 1)
                for m in range(2):
                    wait_if(pe, bn1_done, (g - 1) * 2 + m + 1)
                    mm3(pe, banks[:, 1 + m, :], cut(w1_r, m * P, (m + 1) * P), agg_r[0]).then_inc(w1_sums, 1)

            aggregate(0)
            aggregate(1)
            first_layer(0)
            with pe.Fori(1, GROUPS - 1) as g:
                aggregate(g + 1)
                first_layer(g)
            first_layer(GROUPS - 1)

            pe.wait_ge(bn1_done, 2 * GROUPS)

            def first_again(i, u):
                g = i * 2 + u
                pe.wait_ge(aggb_lo, g + 1)
                for m in range(2):
                    wait_if(pe, hid_kept, (g - 2) * 2 + m + 1)
                    mm3(pe, banks[:, 2 * u + m, :], cut(w1_r, m * P, (m + 1) * P), agg_r[u]).then_inc(w1b_sums, 1)

            def second_layer(i, u):
                g = i * 2 + u
                pe.wait_ge(hid_lo, g * 2 + 2)
                wait_if(pe, z_kept, g - 1)
                out = banks[:, 4 + u, :]
                mm3(pe, out, cut(w2_r, 0, P), cut(hid_r[u], 0, GC), stop=False)
                mm3(pe, out, cut(w2_r, P, 2 * P), cut(hid_r[u], GC, 2 * GC), start=False).then_inc(w2_sums, 1)

            last_pair = GROUPS // 2 - 1
            first_again(0, 0)
            first_again(0, 1)
            second_layer(0, 0)
            first_again(1, 0)
            second_layer(0, 1)
            with pe.Fori(1, last_pair) as i:
                first_again(i, 1)
                second_layer(i, 0)
                first_again(i + 1, 0)
                second_layer(i, 1)
            first_again(last_pair, 1)
            second_layer(last_pair, 0)
            second_layer(last_pair, 1)

            pe.wait_ge(bn2_done, GROUPS)
            pe.wait_ge(z_kept, GROUPS)

            def do(what, part, g, place):
                if what == "turn":
                    pe.wait_ge(z_scaled, g + 1)
                    wait_if(pe, ln3_work, (g - 1) * 4 + 1)
                    for b in range(GB):
                        ins = pe.transpose(banks[:, 0, b * P:(b + 1) * P], z_f[:, b * P:(b + 1) * P], ident)
                    ins.then_inc(z_turned, 1)
                if what == "mix":
                    pe.wait_ge(x3_lo, g + 1)
                    wait_if(pe, mixed_lo, (g - 1) * GB + part + 1)
                    mm3(pe, banks[:, 2 + part, 0:3 * P], cut(x3_r[place], part * P, (part + 1) * P), adjk_r)\
                        .then_inc(mixed, 1)
                if what == "sums":
                    pe.wait_ge(mixed_lo, g * GB + GB)
                    wait_if(pe, w3_kept, g)
                    for k in range(3):
                        mixes = [m.rearrange("q (b k t) -> q b k t", b=GB, k=3)[:, :, k, :] for m in mix_r]
                        ins = mm3(pe, by_batch(banks[:, 1, :], GB), cut(w3_r, k * P, (k + 1) * P), mixes,
                                  start=k == 0, stop=k == 2)
                    ins.then_inc(w3_sums, 1)
                if what == "back":
                    pe.wait_ge(w3_kept, g + 1)
                    wait_if(pe, ln4_work, (g - 1) * 4 + 1)
                    for b in range(GB):
                        ins = pe.transpose(banks[:, 6, b * P:(b + 1) * P], oT_f[:, b * P:(b + 1) * P], ident)
                    ins.then_inc(o_turned, 1)

            groups(pe, [("mix", b, 1) for b in range(GB)] + [("back", 0, 2), ("turn", 0, 0), ("sums", 0, 1)], do)


_INS = ['x', 'adj', 'adjT', 'Wg0', 'bg0', 'Wg1', 'bg1', 'WihT', 'WhhT', 'bih', 'bhh', 'Wqkv', 'W1T', 'b1', 'g1', 'be1',
        'W2T', 'b2', 'g2', 'be2', 'W3', 'bias3']


def kernel(x, adj, L0_gnn_Wg0, L0_gnn_bg0, L0_gnn_Wg1, L0_gnn_bg1, L0_gnn_Wih, L0_gnn_Whh, L0_gnn_bih, L0_gnn_bhh,
           L1_gnn_W, L2_gnn_W1, L2_gnn_b1, L2_gnn_g1, L2_gnn_be1, L2_gnn_W2, L2_gnn_b2, L2_gnn_g2, L2_gnn_be2,
           L3_gnn_W, L3_gnn_bias):
    import numpy as np
    import concourse.bacc as bacc
    from concourse.bass_utils import run_bass_kernel_spmd

    def gate_columns(a):
        return np.asarray(a).reshape(SKIPS * 4, P).T

    def halves(a):
        return np.asarray(a).reshape(2, P).T

    laid = {
        'x': np.asarray(x).transpose(1, 0, 2),
        'adj': adj, 'adjT': np.asarray(adj).T,
        'Wg0': L0_gnn_Wg0, 'bg0': L0_gnn_bg0, 'Wg1': L0_gnn_Wg1, 'bg1': L0_gnn_bg1,
        'WihT': np.asarray(L0_gnn_Wih).transpose(2, 0, 1).reshape(P, -1),
        'WhhT': np.asarray(L0_gnn_Whh)[1:].transpose(2, 0, 1).reshape(P, -1),
        'bih': gate_columns(L0_gnn_bih), 'bhh': gate_columns(L0_gnn_bhh),
        'Wqkv': L1_gnn_W,
        'W1T': np.asarray(L2_gnn_W1).T, 'b1': halves(L2_gnn_b1), 'g1': halves(L2_gnn_g1), 'be1': halves(L2_gnn_be1),
        'W2T': np.asarray(L2_gnn_W2).T.reshape(2, P, P).transpose(1, 0, 2).reshape(P, -1),
        'b2': L2_gnn_b2, 'g2': L2_gnn_g2, 'be2': L2_gnn_be2,
        'W3': np.asarray(L3_gnn_W).transpose(1, 0, 2).reshape(P, -1), 'bias3': L3_gnn_bias,
    }
    nc = bacc.Bacc("TRN2", target_bir_lowering=False, num_devices=1)
    arrays, args = {}, []
    for name in _INS:
        a = np.ascontiguousarray(laid[name])
        arrays[f"in_{name}_dram"] = a
        args.append(nc.dram_tensor(f"in_{name}_dram", a.shape, mybir.dt.from_np(a.dtype), kind="ExternalInput").ap())
    shape = laid['x'].shape
    args.append(nc.dram_tensor("out_dram", shape, F32, kind="ExternalOutput").ap())
    gnn_stack(nc, *args)
    r = run_bass_kernel_spmd(nc, [arrays], core_ids=[0])
    return r.results[0]["out_dram"].transpose(1, 0, 2)
```

```python
from contextlib import ExitStack

import concourse.bass as bass
from concourse import mybir

ALU = mybir.AluOpType
ACT = mybir.ActivationFunctionType
AX = mybir.AxisListType
F32 = mybir.dt.float32
F32R = mybir.dt.float32r
BF16 = mybir.dt.bfloat16

P = 128
EPS = 1e-5
MASKED = -1e30
LANES = 3
LB = 8
LC = LB * P
HALF = LC // 2
GB = 4
GC = GB * P
HEADS = 4
DH = P // HEADS
VW = 2 * DH
SKIPS = 4
I, F, G, O = range(4)

SP_ORDER = """
load_0 load_1 load_2
"""
PE_ORDER = """
residual_0' lstm2_2' lstm6_1' lstm3_2' gcn0_0 lstm7_1' lstm4_2' gcn1_0 lstm8_1' lstm5_2' gcn2_0 lstm9_1'
lstm6_2' gcn3_0 lstm10_1' lstm7_2' lstm0_0 lstm8_2' lstm1_0 residual_1' lstm9_2' lstm2_0 lstm10_2' lstm3_0
residual_2' gcn0_1 lstm4_0 gcn1_1 lstm5_0 gcn2_1 lstm6_0 gcn3_1 gcn0_2 lstm7_0 lstm0_1 gcn1_2 lstm8_0 lstm1_1
gcn2_2 lstm9_0 lstm2_1 gcn3_2 lstm10_0 lstm3_1 lstm0_2 lstm4_1 lstm1_2 lstm5_1
"""
ACT_ORDER = """
tanh3_1' tanh10_0' gates0_2' tanh0_2' gates4_1' tanh4_1' gates1_2' tanh1_2' gates5_1' tanh5_1' gates2_2'
tanh2_2' gates6_1' split_0 tanh6_1' gates3_2' tanh3_2' gcn0_0 gates7_1' tanh7_1' gates4_2' tanh4_2' gcn1_0
gates8_1' gates5_2' tanh8_1' tanh5_2' gcn2_0 gates9_1' gates6_2' tanh9_1' tanh6_2' gcn3_0 gates10_1' gates7_2'
tanh10_1' tanh7_2' gates0_0 tanh0_0 gates8_2' gates1_0 tanh8_2' tanh1_0 gates9_2' tanh9_2' gates2_0 tanh2_0
gates10_2' split_1 tanh10_2' gates3_0 tanh3_0 gcn0_1 gates4_0 tanh4_0 split_2 gcn1_1 gates5_0 tanh5_0 gcn2_1
gates6_0 tanh6_0 gcn3_1 gcn0_2 gates7_0 tanh7_0 gates0_1 tanh0_1 gcn1_2 gates8_0 gates1_1 tanh8_0 tanh1_1
gcn2_2 gates9_0 gates2_1 tanh9_0 gcn3_2 tanh2_1 gates10_0 gates3_1
"""
DVE_ORDER = """
gcn0_0 cell7_1' hidden7_1' cell4_2' hidden4_2' gcn1_0 cell8_1' cell5_2' hidden8_1' hidden5_2' gcn2_0 norm_0'
cell9_1' cell6_2' hidden9_1' hidden6_2' gcn3_0 cell10_1' cell7_2' hidden7_2' cell0_0 hidden0_0 cell8_2'
hidden10_1' cell1_0 hidden8_2' hidden1_0 residual_1' cell9_2' hidden9_2' statistics_1' cell2_0 hidden2_0
cell10_2' norm_1' hidden10_2' cell3_0 residual_2' hidden3_0 statistics_2' gcn0_1 cell4_0 hidden4_0 gcn1_1
cell5_0 hidden5_0 gcn2_1 cell6_0 hidden6_0 gcn3_1 gcn0_2 cell7_0 norm_2' hidden7_0 cell0_1 gcn1_2 hidden0_1
cell8_0 cell1_1 hidden8_0 hidden1_1 gcn2_2 cell9_0 cell2_1 hidden9_0 gcn3_2 hidden2_1 cell10_0 cell3_1
hidden3_1 cell0_2 hidden0_2 cell4_1 hidden4_1 cell1_2 hidden1_2 hidden10_0 cell5_1 residual_0 hidden5_1
cell2_2 statistics_0 hidden2_2 cell6_1 hidden6_1 cell3_2 hidden3_2
"""
POOL_ORDER = """
low0_2' low1_2' low5_1' low2_2' split_0 low6_1' low3_2' low7_1' statistics_0' low4_2' low8_1' low5_2' low9_1'
low6_2' low7_2' low0_0 low8_2' low1_0 low9_2' statistics_1' low2_0 split_1 low3_0 low4_0 statistics_2' split_2
low5_0 low6_0 low7_0 low0_1 low8_0 low1_1 low9_0 low2_1 low3_1 low4_1
"""


def order_of(text):
    steps = []
    for word in text.split():
        step, lane = word.split("_")
        what = step.rstrip("0123456789")
        steps.append((what, int(step[len(what):] or 0), int(lane.rstrip("'")), lane.count("'")))
    return steps



def lstm_steps():
    steps = [(1, 0, 0, P, (I, G, O)), (1, 0, 1, P, (I, G, O))]
    for p in range(2, SKIPS + 1):
        for t in range(p):
            steps.append((p, t, None, P // p, (I, G, O) if t == 0 else (I, G, F, O)))
    return steps


def wait_if(eng, sem, value):
    if not (isinstance(value, int) and value <= 0):
        eng.wait_ge(sem, value)


def gnn_stack(nc, x_sbd, adj, adjT, Wg0, bg0, Wg1, bg1, WihT, WhhT, bih, bhh, Wqkv, W1T, b1, g1, be1,
              W2T, b2, g2, be2, W3, bias3, out_tbd):
    B = x_sbd.shape[1]
    UNITS = B // LB
    GROUPS = B // GB
    STEPS = lstm_steps()
    NSTEP = len(STEPS)
    NGATE = sum(len(s[4]) for s in STEPS)
    NLATER = sum(s[1] > 0 for s in STEPS)
    gate_at = []
    for s in STEPS:
        gate_at.append((gate_at[-1] + len(STEPS[len(gate_at) - 1][4])) if gate_at else 0)
    BEHIND = 2
    PEEL = BEHIND + 1
    FULL = UNITS // LANES

    def exists(lane, rr):
        return rr >= 0 and rr * LANES + lane < UNITS

    def units_of(lane):
        return (UNITS - lane + LANES - 1) // LANES

    def cycles(eng, order, do):
        assert max(late for _, _, _, late in order) <= BEHIND
        for k in range(PEEL):
            for at, (_, _, lane, late) in enumerate(order):
                if exists(lane, k - late):
                    do(at, k - late, k)
        with eng.Fori(PEEL, FULL) as k:
            for at, (_, _, lane, late) in enumerate(order):
                do(at, k - late if late else k, k)
        for k in range(FULL, FULL + PEEL + 1):
            for at, (_, _, lane, late) in enumerate(order):
                if exists(lane, k - late):
                    do(at, k - late, k)

    def groups(eng, order, do, pairs=2):
        for head in range(2 * pairs):
            for what, part, late in order:
                if head >= late:
                    do(what, part, head - late, (head - late) % 2)
        with eng.Fori(pairs, GROUPS // 2) as i:
            for head in range(2):
                for what, part, late in order:
                    do(what, part, i * 2 + (head - late), (head - late) % 2)
        for head in range(GROUPS, GROUPS + max(late for _, _, late in order)):
            for what, part, late in order:
                if late > head - GROUPS:
                    do(what, part, head - late, (head - late) % 2)

    ctx = ExitStack()
    with ctx:
        def sb(name, cols, dt=F32):
            return ctx.enter_context(nc.sbuf_tensor(name, [P, cols], dt))

        def sem(name):
            return ctx.enter_context(nc.semaphore(name))

        def lane_sems(name):
            return [sem(f"{name}_{s}") for s in range(LANES)]

        banks = ctx.enter_context(nc.psum_tensor("banks", [P, 8, 512], F32))

        xs_all = sb("x_all", B * P)
        consts = sb("consts", 1024)
        mask = sb("mask", GC, BF16)
        ident_bf = sb("ident_bf", P, BF16)

        class Area:
            def __init__(self, whole, at=0):
                self.whole, self.at = whole, at

            def take(self, cols):
                self.at += cols
                assert self.at <= self.whole.shape[1], (self.at, self.whole.shape)
                return self.whole[:, self.at - cols:self.at]

        def pair(pool, cols):
            return (pool.take(cols), pool.take(cols))

        def cut(hl, a, b):
            return (hl[0][:, a:b], hl[1][:, a:b])

        c = Area(consts)
        ident = c.take(P)
        gcn_bias0 = c.take(P)
        gcn_bias1 = c.take(P)
        out_bias = c.take(1)
        lstm_bias = c.take(SKIPS * 4)
        bias_parts = c.take(2 * SKIPS * 4)
        minus_half = c.take(2 * LB)
        bn_cols = c.take(16)
        bn_work = c.take(32)
        small = [c.take(6 * LB + 6 * LB) for _ in range(LANES)]
        rden = c.take(GB * HEADS)
        maxes = c.take(GB * HEADS)
        shift_cols = c.take(GB)
        hat_work = c.take(8)
        ones_sq = c.take(P)

        wqkv_r = pair(Area(sb("wqkv_rounded", 2 * 3 * P, F32R)), 3 * P)

        early = ExitStack()
        r = Area(early.enter_context(nc.sbuf_tensor("early_rounded", [P, LANES * 4 * LC + 2 * (7 * 4 + 3) * P],
                                                    F32R)))
        order = list(range(1, LANES)) + [0]
        mid_h = {lane: (pair(r, LC), pair(r, LC)) for lane in order}
        mid_r = [mid_h[lane][0] for lane in range(LANES)]
        h_r = [mid_h[lane][1] for lane in range(LANES)]
        x_r = h_r
        wih_r = pair(r, SKIPS * 4 * P)
        whh_r = pair(r, (SKIPS - 1) * 4 * P)
        wg0_r, wg1_r, adjT_r = pair(r, P), pair(r, P), pair(r, P)
        hs_r = mid_r

        f = Area(early.enter_context(nc.sbuf_tensor("early_scratch", [P, LANES * 9 * HALF], F32)))
        x_in = [f.take(LC) for _ in range(LANES)]
        h_f = [f.take(LC) for _ in range(LANES)]
        gate_all = [f.take(4 * HALF) for _ in range(LANES)]
        gate_f = [[g[:, j * HALF:(j + 1) * HALF] for j in range(4)] for g in gate_all]
        tmp = [g[:, 0:LC] for g in gate_all]
        cell_f = [f.take(HALF) for _ in range(LANES)]
        hs_f = [g[O] for g in gate_f]

        w = Area(xs_all)
        raw = {"ih": w.take(SKIPS * 4 * P), "hh": w.take((SKIPS - 1) * 4 * P), "g0": w.take(P), "g1": w.take(P),
               "adjT": w.take(P), "qkv": w.take(3 * P), "adj": w.take(P), "bg0": w.take(P)}
        splits = [("adjT", adjT_r), ("g0", wg0_r), ("g1", wg1_r), ("ih", wih_r), ("hh", whh_r), ("qkv", wqkv_r)]

        early.close()

        kept_r = Area(sb("kept_rounded", 6 * GC + 2 * 11 * P, F32R))
        w1_r, w2_r, w3_r = pair(kept_r, 2 * P), pair(kept_r, 2 * P), pair(kept_r, 3 * P)
        hatT_r, adjk_r = pair(kept_r, P), pair(kept_r, 3 * P)
        assert kept_r.whole.shape[1] + 14 * P <= (LANES - 1) * 4 * LC
        kept = Area(sb("kept_scratch", 14 * P + GROUPS * 18))
        raw2 = {"w1": kept.take(2 * P), "w2": kept.take(2 * P), "w3": kept.take(3 * P), "hatT": kept.take(P),
                "adjk": kept.take(3 * P)}
        nadj, nadjT, diag = kept.take(P), kept.take(P), kept.take(P)
        splits2 = [("w1", w1_r), ("w2", w2_r), ("w3", w3_r), ("hatT", hatT_r), ("adjk", adjk_r)]
        bn1_stats = kept.take(GROUPS * 2 * 6)
        bn2_stats = kept.take(GROUPS * 6)
        x2_r = pair(kept_r, GC)
        agg_r = [pair(kept_r, GC) for _ in range(2)]
        x3_r = agg_r

        mid = ExitStack()
        rm = Area(mid.enter_context(nc.sbuf_tensor("attention_rounded", [P, 20 * GC], F32R)))
        xT_r, q_r = pair(rm, GC), pair(rm, GC)
        kd_r = [pair(rm, HEADS * GC) for _ in range(2)]
        fm = Area(mid.enter_context(nc.sbuf_tensor("attention_scratch", [P, 18 * GC], F32)))
        xg = fm.take(GC)
        prob = [fm.take(HEADS * P) for _ in range(GB)]
        probT = [fm.take(HEADS * P) for _ in range(GB)]
        vals = [fm.take(GB * HEADS * VW) for _ in range(2)]
        attT = [fm.take(GC) for _ in range(2)]
        y_f, x2_f = fm.take(GC), fm.take(GC)
        mid.close()

        r2 = Area(sb("late_rounded", 8 * GC, F32R))
        hid_r = [pair(r2, 2 * GC) for _ in range(2)]
        mix_r = pair(Area(r2.whole), GB * 3 * P)
        f3 = Area(sb("late_scratch", 12 * GC))
        hid_f = [f3.take(GC) for _ in range(2)]
        z_f = f3.take(GC)
        y3 = f3.take(GC)
        x3_f = [f3.take(GC) for _ in range(2)]
        y4 = f3.take(GC)
        oT_f = f3.take(GC)
        o_f = [f3.take(GC) for _ in range(2)]
        x2_back = [f3.take(GC) for _ in range(2)]
        x2_away = nc.dram_tensor("x2_away", [P, B, P], F32, kind="Internal").ap()

        weights_in, lstm_weights_in, lstm_weights_lo = sem("weights_in"), sem("lstm_weights_in"), sem("lstm_weights_lo")
        late_weights_in = sem("late_weights_in")
        ident_zero, ident_one = sem("ident_zero"), sem("ident_one")
        weights_hi, weights_lo = sem("weights_hi"), sem("weights_lo")
        rowsum_product = sem("rowsum_product")
        bias0_made, consts_made = sem("bias0_made"), sem("consts_made")
        pow_ready = sem("pow_ready")
        ones_made = sem("ones_made")

        x_loaded = lane_sems("x_loaded")
        x_hi, x_lo = lane_sems("x_hi"), lane_sems("x_lo")
        gcn_sums = lane_sems("gcn_sums")
        gcn_biased = lane_sems("gcn_biased")
        gcn_hi, gcn_lo = lane_sems("gcn_hi"), lane_sems("gcn_lo")
        gate_sums = lane_sems("gate_sums")
        gates_open = lane_sems("gates_open")
        cell_parts = lane_sems("cell_parts")
        cells = lane_sems("cells")
        cell_tanh = lane_sems("cell_tanh")
        states = lane_sems("states")
        states_hi, states_lo = lane_sems("states_hi"), lane_sems("states_lo")
        h_turned = lane_sems("h_turned")
        norm_work = lane_sems("norm_work")
        variances, rstds = lane_sems("variances"), lane_sems("rstds")
        x1_kept = lane_sems("x1_kept")

        def mm3(pe, out, wt, mv, start=True, stop=True):
            pe.matmul(out, wt[0], mv[0], start=start, stop=False)
            pe.matmul(out, wt[1], mv[0], start=False, stop=False)
            return pe.matmul(out, wt[0], mv[1], start=False, stop=stop)

        def f32(ap):
            return ap.bitcast(F32)

        def by_batch(ap, n):
            return ap.rearrange("q (b t) -> q b t", b=n)

        def windows(ap, step):
            p, t, half, nw, _ = step
            if half is not None:
                return ap[:, half * HALF:(half + 1) * HALF]
            return by_batch(ap, LB)[:, :, 0:nw * p].rearrange("q b (w p) -> q b w p", p=p)[:, :, :, t]

        def step_cols(step):
            return HALF if step[2] is not None else LB * step[3]

        def like_windows(ap, step):
            n = step_cols(step)
            return ap[:, 0:n] if step[2] is not None else ap[:, 0:n].rearrange("q (b w) -> q b w", b=LB)

        SETS = {step[0:3]: at % 2 for at, step in enumerate(order_of(PE_ORDER))}
        assert len(SETS) % 2 == 0

        def bank_set(what, n, lane):
            return SETS[(what, n, lane)]

        def bank(which, n):
            return banks[:, 4 * which + n, :]

        def ln_cols(s, nb):
            t = small[s]
            st = t[:, 0:6 * nb].rearrange("q (b k) -> q b k", k=6)
            rest = [t[:, 6 * LB + j * LB:6 * LB + j * LB + nb] for j in range(6)]
            return st, rest

        def ln_statistics(dve, y, s, nb, work, base, done, negate=False):
            st, (d, m2, q, mean, var, _) = ln_cols(s, nb)
            for b in range(nb):
                ins = nc.vector.bn_stats(st[:, b, :], y[:, b * P:(b + 1) * P])
            ins.then_inc(work, 1)
            dve.wait_ge(work, base + 1)
            nc.vector.tensor_tensor(d, st[:, :, 1], st[:, :, 4], ALU.subtract)
            nc.vector.scalar_tensor_tensor(out=m2, in0=st[:, :, 2], scalar=P * EPS, in1=st[:, :, 5],
                                           op0=ALU.add, op1=ALU.add).then_inc(work, 1)
            dve.wait_ge(work, base + 2)
            nc.vector.scalar_tensor_tensor(out=q, in0=d, scalar=0.25, in1=d, op0=ALU.mult, op1=ALU.mult)
            nc.vector.scalar_tensor_tensor(out=mean, in0=d, scalar=-0.5 if negate else 0.5, in1=st[:, :, 4],
                                           op0=ALU.mult, op1=ALU.subtract if negate else ALU.add).then_inc(work, 1)
            dve.wait_ge(work, base + 3)
            nc.vector.scalar_tensor_tensor(out=var, in0=m2, scalar=1.0 / P, in1=q,
                                           op0=ALU.mult, op1=ALU.add).then_inc(done, 1)

        def ln_moments(pool, s, nb, work, base, done):
            st, (d, m2, q, mean, var, half) = ln_cols(s, nb)
            pool.wait_ge(work, base + 1)
            nc.gpsimd.tensor_tensor(d, st[:, :, 1], st[:, :, 4], ALU.subtract)
            nc.gpsimd.tensor_tensor(m2, st[:, :, 2], st[:, :, 5], ALU.add).then_inc(work, 1)
            pool.wait_ge(work, base + 2)
            nc.gpsimd.tensor_tensor(half, d, minus_half[:, 0:nb], ALU.mult)
            nc.gpsimd.tensor_scalar(m2, m2, 1.0 / P, EPS, ALU.mult, ALU.add).then_inc(work, 1)
            pool.wait_ge(work, base + 3)
            nc.gpsimd.tensor_tensor(q, half, half, ALU.mult)
            nc.gpsimd.tensor_tensor(mean, st[:, :, 4], half, ALU.subtract).then_inc(work, 1)
            pool.wait_ge(work, base + 4)
            nc.gpsimd.tensor_tensor(var, m2, q, ALU.add).then_inc(done, 1)

        def ln_sums(y, s, nb):
            st, _ = ln_cols(s, nb)
            for b in range(nb):
                ins = nc.vector.bn_stats(st[:, b, :], y[:, b * P:(b + 1) * P])
            return ins

        def ln_rstd(s, nb):
            _, (_, _, _, _, var, rstd) = ln_cols(s, nb)
            return nc.gpsimd.tensor_tensor(rstd, var, minus_half[:, 0:nb], ALU.pow)

        def ln_apply(dst, y, s, nb):
            _, (_, _, _, mean, _, rstd) = ln_cols(s, nb)
            for b in range(nb):
                ins = nc.vector.tensor_scalar(dst[:, b * P:(b + 1) * P], y[:, b * P:(b + 1) * P],
                                              mean[:, b:b + 1], rstd[:, b:b + 1], ALU.subtract, ALU.mult)
            return ins

        xg_copied, x_turned, xT_hi, xT_lo = sem("xg_copied"), sem("x_turned"), sem("xT_hi"), sem("xT_lo")
        k_sums, k_hi, k_lo, q_sums, q_hi, q_lo = (sem("k_sums"), sem("k_hi"), sem("k_lo"), sem("q_sums"),
                                                  sem("q_hi"), sem("q_lo"))
        v_sums, v_kept, v_ones, k_zeros, k0_zeros = (sem("v_sums"), sem("v_kept"), sem("v_ones"), sem("k_zeros"),
                                                    sem("k0_zeros"))
        scores, row_max, shifted, exps = sem("scores"), sem("row_max"), sem("shifted"), sem("exps")
        prob_turned, probT_kept, attended = sem("prob_turned"), sem("probT_kept"), sem("attended")
        y_sums = sem("y_sums")
        att_kept, att_turned = sem("att_kept"), sem("att_turned")
        att_work, var2, rstd2, x2_kept = sem("att_work"), sem("var2"), sem("rstd2"), sem("x2_kept")
        ATT_WORK = 6
        LN_WORK = 4
        hat_work_done, hat_pow, hat_product, hat_turned = (sem("hat_work_done"), sem("hat_pow"),
                                                           sem("hat_product"), sem("hat_turned"))
        adjk_made = sem("adjk_made")
        late_hi, late_lo = sem("late_hi"), sem("late_lo")
        x2_hi, x2_lo, agg_sums, agg_kept, agg_lo = (sem("x2_hi"), sem("x2_lo"), sem("agg_sums"), sem("agg_kept"),
                                                    sem("agg_lo"))
        w1_sums, bn1_done = sem("w1_sums"), sem("bn1_done")
        bn_work_done, bn_var, bn_rstd = sem("bn_work_done"), sem("bn_var"), sem("bn_rstd")
        aggb_hi, aggb_lo, w1b_sums, hid_kept, hid_hi, hid_lo = (sem("aggb_hi"), sem("aggb_lo"), sem("w1b_sums"),
                                                                sem("hid_kept"), sem("hid_hi"), sem("hid_lo"))
        w2_sums, z_kept, bn2_done = sem("w2_sums"), sem("z_kept"), sem("bn2_done")
        z_scaled, z_turned, ln3_work, var3, rstd3, x3_kept = (sem("z_scaled"), sem("z_turned"), sem("ln3_work"),
                                                              sem("var3"), sem("rstd3"), sem("x3_kept"))
        x3_hi, x3_lo, mixed, mixed_hi, mixed_lo = (sem("x3_hi"), sem("x3_lo"), sem("mixed"), sem("mixed_hi"),
                                                   sem("mixed_lo"))
        w3_sums, w3_kept, o_turned = sem("w3_sums"), sem("w3_kept"), sem("o_turned")
        ln4_work, var4, rstd4, shift4 = sem("ln4_work"), sem("var4"), sem("rstd4"), sem("shift4")
        x2_stored, x2_loaded = sem("x2_stored"), [sem(f"x2_loaded_{u}") for u in range(2)]
        out_ready, out_stored = sem("out_ready"), [sem(f"out_stored_{u}") for u in range(2)]

        NCONV, NLSTM = 5, 6

        def key_block(ap, h):
            return ap.rearrange("q (b h j) -> q b h j", b=GB, h=HEADS)[h * DH:(h + 1) * DH, :, h, :]

        def xcols(g, n=GC):
            if isinstance(g, int):
                return xs_all[:, g * n:(g + 1) * n]
            return xs_all[:, bass.ds(g * n, n)]

        def round_batches(rr, lane):
            first = rr * (LANES * LB) + lane * LB
            return slice(first, first + LB) if isinstance(first, int) else bass.ds(first, LB)

        block = ctx.enter_context(nc.Block())

        @block.sync
        def _(sp):
            def load(dst, src, sem=weights_in):
                sp.dma_start(dst, src).then_inc(sem, 16)

            load(raw["adjT"], adjT)
            load(raw["g0"], Wg0)
            load(raw["g1"], Wg1)
            load(raw["bg0"], bg0.unsqueeze(0).broadcast_to([P, P]))
            load(gcn_bias1, bg1.unsqueeze(0).broadcast_to([P, P]))

            ORDER = order_of(SP_ORDER)

            def do(at_event, rr, k):
                what, n, lane, _ = ORDER[at_event]
                if what == "load":
                    wait_if(sp, norm_work[lane], rr * 5 - 3)
                    sp.dma_start(by_batch(x_in[lane], LB), x_sbd[:, round_batches(rr, lane), :])\
                      .then_inc(x_loaded[lane], 16)

            cycles(sp, ORDER, do)

            for lane in range(1, LANES):
                sp.wait_ge(x1_kept[lane], units_of(lane))
            for dst, src in ((raw2["w1"], W1T), (raw2["w2"], W2T), (raw2["w3"], W3), (nadj, adj), (nadjT, adjT)):
                sp.dma_start(dst, src).then_inc(late_weights_in, 16)
            sp.dma_start(out_bias, bias3.unsqueeze(1)).then_inc(late_weights_in, 16)
            for j, v in enumerate((b1, g1, be1)):
                sp.dma_start(bn_cols[:, 2 * j:2 * j + 2], v).then_inc(late_weights_in, 16)
            for j, v in enumerate((b2, g2, be2)):
                sp.dma_start(bn_cols[:, 6 + j:7 + j], v.unsqueeze(1)).then_inc(late_weights_in, 16)

            def rows(g):
                return slice(g * GB, g * GB + GB) if isinstance(g, int) else bass.ds(g * GB, GB)

            def put_away(g):
                sp.wait_ge(x2_kept, g + 1)
                sp.dma_start(x2_away[:, rows(g), :], by_batch(x2_f, GB)).then_inc(x2_stored, 16)

            put_away(0)
            with sp.Fori(1, GROUPS) as g:
                put_away(g)

            def fetch(g, u):
                if isinstance(g, int) and g == 0:
                    sp.wait_ge(x2_stored, 16 * GROUPS)
                    sp.wait_ge(bn1_done, 2 * GROUPS)
                wait_if(sp, ln3_work, (g - 2) * LN_WORK + 1)
                sp.dma_start(by_batch(x2_back[u], GB), x2_away[:, rows(g), :]).then_inc(x2_loaded[u], 16)

            def put(g, u):
                sp.wait_ge(out_ready, g + 1)
                sp.dma_start(out_tbd[:, rows(g), :], by_batch(o_f[u], GB)).then_inc(out_stored[u], 16)

            for g in range(3):
                fetch(g, g % 2)
            with sp.Fori(0, GROUPS // 2 - 2) as i:
                for u in range(2):
                    fetch(i * 2 + (u + 3), (u + 1) % 2)
                    put(i * 2 + u, u)
            fetch(GROUPS - 1, 1)
            for g in range(GROUPS - 4, GROUPS):
                put(g, g % 2)
            for u in range(2):
                sp.wait_ge(out_stored[u], 16 * (GROUPS // 2))

        LATE = 5 + 1 + 6

        @block.gpsimd
        def _(pool):
            nc.gpsimd.memset(ident, 0.0).then_inc(ident_zero, 1)
            nc.gpsimd.memset(minus_half, -0.5).then_inc(pow_ready, 1)
            nc.gpsimd.memset(ones_sq, 1.0).then_inc(ones_made, 1)
            pool.wait_ge(ident_zero, 1)
            nc.gpsimd.affine_select(out=ident, in_=ident, compare_op=ALU.not_equal, fill=1.0, base=0,
                                    pattern=[[-1, P]], channel_multiplier=1).then_inc(ident_one, 1)
            for n, (name, (hi, lo)) in enumerate(splits[:3]):
                pool.wait_ge(weights_hi, n + 1)
                nc.gpsimd.tensor_tensor(lo, raw[name], f32(hi), ALU.subtract).then_inc(weights_lo, 1)

            pool.wait_ge(pow_ready, 1)

            ORDER = order_of(POOL_ORDER)

            def do(at_event, rr, k):
                what, n, lane, _ = ORDER[at_event]
                if what == "split":
                    pool.wait_ge(x_hi[lane], rr + 1)
                    nc.gpsimd.tensor_tensor(x_r[lane][1], x_in[lane], f32(x_r[lane][0]), ALU.subtract)\
                      .then_inc(x_lo[lane], 1)
                if what == "low":
                    p, t = STEPS[n][0:2]
                    src, dst = (h_f[lane], h_r[lane]) if t == p - 1 else (hs_f[lane], hs_r[lane])
                    view = windows if t == p - 1 else like_windows
                    pool.wait_ge(states_hi[lane], rr * (NSTEP - 1) + n + 1)
                    nc.gpsimd.tensor_tensor(view(dst[1], STEPS[n]), view(src, STEPS[n]), f32(view(dst[0], STEPS[n])),
                                            ALU.subtract).then_inc(states_lo[lane], 1)
                if what == "statistics":
                    pool.wait_ge(variances[lane], rr + 1)
                    ln_rstd(lane, LB).then_inc(rstds[lane], 1)

            cycles(pool, ORDER, do)

            pool.wait_ge(late_weights_in, 16 * LATE)
            for k, (comp, sign) in enumerate(((ALU.is_equal, 1), (ALU.is_gt, 1), (ALU.is_gt, -1))):
                nc.gpsimd.affine_select(out=raw2["adjk"][:, k * P:(k + 1) * P], in_=nadjT, compare_op=comp, fill=0.0,
                                        base=0, pattern=[[-sign, P]], channel_multiplier=sign).then_inc(adjk_made, 1)

            for lane in range(LANES):
                pool.wait_ge(x1_kept[lane], units_of(lane))

            def do(what, part, g, place):
                if what == "copy":
                    wait_if(pool, x_turned, g)
                    nc.gpsimd.tensor_copy(xg, xcols(g)).then_inc(xg_copied, 1)
                    if isinstance(g, int) and g == 0:
                        prepare()
                    if isinstance(g, int) and g == 1:
                        split_late_weights()
                if what == "rstd":
                    ln_moments(pool, 0, GB, att_work, g * ATT_WORK + 2, var2)
                    pool.wait_ge(var2, g + 1)
                    ln_rstd(0, GB).then_inc(rstd2, 1)
                if what == "add":
                    pool.wait_ge(att_work, g * ATT_WORK + 2)
                    nc.gpsimd.tensor_tensor(y_f, y_f, xcols(g), ALU.add).then_inc(y_sums, 1)
                if what == "x2_low":
                    pool.wait_ge(x2_hi, g + 1)
                    nc.gpsimd.tensor_tensor(x2_r[1], x2_f, f32(x2_r[0]), ALU.subtract).then_inc(x2_lo, 1)

            def prepare():
                for part in kd_r[1]:
                    nc.gpsimd.memset(f32(part), 0.0).then_inc(k_zeros, 1)
                for v in vals:
                    nc.gpsimd.memset(v, 1.0).then_inc(v_ones, 1)
                pool.wait_ge(hat_work_done, 4)
                nc.gpsimd.tensor_tensor(hat_work[:, 5:6], hat_work[:, 4:5], minus_half[:, 0:1], ALU.pow)\
                  .then_inc(hat_pow, 1)

            def split_late_weights():
                for n, (name, (hi, lo)) in enumerate(splits2):
                    pool.wait_ge(late_hi, n + 1)
                    nc.gpsimd.tensor_tensor(lo, raw2[name], f32(hi), ALU.subtract).then_inc(late_lo, 1)

            groups(pool, [("add", 0, 3), ("rstd", 0, 3), ("copy", 0, 0), ("x2_low", 0, 3)], do, pairs=3)

            pool.wait_ge(bn_var, 1)
            nc.gpsimd.tensor_tensor(bn_work[:, 8:10], bn_work[:, 6:8], minus_half[:, 0:2], ALU.pow)\
              .then_inc(bn_rstd, 1)

            def second_pass(i, u):
                g = i * 2 + u
                pool.wait_ge(aggb_hi, g + 1)
                nc.gpsimd.tensor_tensor(agg_r[u][1], xcols(g), f32(agg_r[u][0]), ALU.subtract).then_inc(aggb_lo, 1)

            def hidden_low(i, u):
                g = i * 2 + u
                pool.wait_ge(hid_hi, g * 2 + 2)
                nc.gpsimd.tensor_tensor(hid_r[u][1][:, GC:2 * GC], hid_f[1], f32(hid_r[u][0][:, GC:2 * GC]),
                                        ALU.subtract).then_inc(hid_lo, 1)

            second_pass(0, 0)
            with pool.Fori(0, GROUPS // 2 - 1) as i:
                second_pass(i, 1)
                hidden_low(i, 0)
                second_pass(i + 1, 0)
                hidden_low(i, 1)
            second_pass(GROUPS // 2 - 1, 1)
            hidden_low(GROUPS // 2 - 1, 0)
            hidden_low(GROUPS // 2 - 1, 1)

            pool.wait_ge(bn_var, 2)
            nc.gpsimd.tensor_tensor(bn_work[:, 8:9], bn_work[:, 6:7], minus_half[:, 0:1], ALU.pow)\
              .then_inc(bn_rstd, 1)

            def do(what, part, g, place):
                if what == "third":
                    pool.wait_ge(var3, g + 1)
                    ln_rstd(0, GB).then_inc(rstd3, 1)
                if what == "third_low":
                    pool.wait_ge(x3_hi, g + 1)
                    nc.gpsimd.tensor_tensor(x3_r[place][1], x3_f[place], f32(x3_r[place][0]), ALU.subtract)\
                      .then_inc(x3_lo, 1)
                if what == "fourth":
                    pool.wait_ge(var4, g + 1)
                    wait_if(pool, out_ready, g)
                    ln_rstd(1, GB).then_inc(rstd4, 1)
                    pool.wait_ge(rstd4, g + 1)
                    _, (_, _, _, mean, _, rstd) = ln_cols(1, GB)
                    nc.gpsimd.tensor_tensor(shift_cols, mean, rstd, ALU.mult).then_inc(shift4, 1)

            groups(pool, [("third", 0, 0), ("fourth", 0, 2), ("third_low", 0, 0)], do, pairs=3)

        @block.scalar
        def _(act):
            def copy(dst, src):
                return nc.scalar.activation(dst, src, ACT.Copy)

            for dst, src in ((raw["ih"], WihT), (raw["hh"], WhhT), (bias_parts[:, 0:SKIPS * 4], bih),
                             (bias_parts[:, SKIPS * 4:2 * SKIPS * 4], bhh), (raw["qkv"], Wqkv), (raw["adj"], adj)):
                act.dma_start(dst, src).then_inc(lstm_weights_in, 16)
            act.wait_ge(weights_in, 16 * NCONV)
            for name, (hi, _) in splits[:3]:
                copy(hi, raw[name]).then_inc(weights_hi, 1)
            act.wait_ge(rowsum_product, 1)
            copy(gcn_bias0, bank(0, 0)[:, 0:P]).then_inc(bias0_made, 1)
            act.wait_ge(lstm_weights_in, 16 * NLSTM)
            for name, (hi, _) in splits[3:]:
                copy(hi, raw[name]).then_inc(weights_hi, 1)
            act.wait_ge(consts_made, 1)

            ORDER = order_of(ACT_ORDER)

            def do(at_event, rr, k):
                what, n, lane, _ = ORDER[at_event]
                if what == "split":
                    act.wait_ge(x_loaded[lane], rr * 16 + 16)
                    copy(x_r[lane][0], x_in[lane]).then_inc(x_hi[lane], 1)
                if what == "gcn":
                    for half in range(2):
                        cols = slice(half * HALF, (half + 1) * HALF)
                        at = 2 * n + half
                        if n == 0:
                            act.wait_ge(gcn_sums[lane], rr * 8 + at + 1)
                            copy(mid_r[lane][0][:, cols], bank(bank_set(what, n, lane), half)).then_inc(gcn_hi[lane], 1)
                        elif n == 1:
                            act.wait_ge(gcn_biased[lane], rr * 4 + half + 1)
                            nc.scalar.activation(h_r[lane][0][:, cols], tmp[lane][:, cols], ACT.Relu)\
                              .then_inc(gcn_hi[lane], 1)
                        elif n == 2:
                            act.wait_ge(gcn_biased[lane], rr * 4 + 2 + half + 1)
                            copy(mid_r[lane][0][:, cols], tmp[lane][:, cols]).then_inc(gcn_hi[lane], 1)
                        else:
                            act.wait_ge(gcn_sums[lane], rr * 8 + at + 1)
                            nc.scalar.activation(h_r[lane][0][:, cols],
                                                 bank(bank_set(what, n, lane), 2 + half), ACT.Relu)\
                              .then_inc(gcn_hi[lane], 1)
                if what == "gates":
                    step = STEPS[n]
                    cols = step_cols(step)
                    if n:
                        act.wait_ge(states[lane], rr * NSTEP + n)
                    for j, gate in enumerate(step[4]):
                        act.wait_ge(gate_sums[lane], rr * NGATE + gate_at[n] + j + 1)
                        at = (step[0] - 1) * 4 + gate
                        nc.scalar.activation(gate_f[lane][gate][:, 0:cols],
                                             bank(bank_set("lstm", n, lane), gate)[:, 0:cols],
                                             ACT.Tanh if gate == G else ACT.Sigmoid,
                                             bias=lstm_bias[:, at:at + 1]).then_inc(gates_open[lane], 1)
                if what == "tanh":
                    cols = step_cols(STEPS[n])
                    act.wait_ge(cells[lane], rr * NSTEP + n + 1)
                    nc.scalar.activation(gate_f[lane][G][:, 0:cols], cell_f[lane][:, 0:cols], ACT.Tanh)\
                      .then_inc(cell_tanh[lane], 1)

            cycles(act, ORDER, do)

            def do(what, part, g, place):
                if what == "turned":
                    act.wait_ge(x_turned, g + 1)
                    wait_if(act, v_sums, g)
                    copy(xT_r[0], banks[:, 4, :]).then_inc(xT_hi, 1)
                    if isinstance(g, int) and g == 1:
                        act.wait_ge(adjk_made, 3)
                        act.wait_ge(hat_turned, 1)
                        for name, (hi, _) in splits2:
                            copy(hi, raw2[name]).then_inc(late_hi, 1)
                if what == "keys":
                    act.wait_ge(k_sums, g + 1)
                    if isinstance(g, int) and g < 2:
                        act.wait_ge(k_zeros if g else k0_zeros, 2)
                    wait_if(act, scores, (g - 1) * GB)
                    for h in range(HEADS):
                        copy(key_block(kd_r[place][0], h), by_batch(banks[h * DH:(h + 1) * DH, 4, :], GB))\
                            .then_inc(k_hi, 1)
                if what == "queries":
                    act.wait_ge(q_sums, g + 1)
                    wait_if(act, scores, g * GB)
                    nc.scalar.activation(q_r[0], banks[:, 5, :], ACT.Copy, scale=DH ** -0.5).then_inc(q_hi, 1)
                if what == "exp":
                    act.wait_ge(shifted, g * GB + part + 1)
                    nc.scalar.activation(prob[part], prob[part], ACT.Exp).then_inc(exps, 1)
                if what == "probT":
                    act.wait_ge(prob_turned, g * GB + part + 1)
                    wait_if(act, attended, (g - 1) * GB + part + 1)
                    copy(probT[part], banks[:, 2 + part % 2, :]).then_inc(probT_kept, 1)
                if what == "attended":
                    act.wait_ge(attended, g * GB + GB)
                    for j in range(2):
                        copy(attT[j], banks[:, 6 + j, :]).then_inc(att_kept, 1)
                if what == "round":
                    act.wait_ge(x2_kept, g + 1)
                    wait_if(act, agg_sums, g)
                    copy(x2_r[0], x2_f).then_inc(x2_hi, 1)
                if what == "aggregated":
                    act.wait_ge(agg_sums, g + 1)
                    wait_if(act, w1_sums, g * 2)
                    copy(agg_r[0][0], banks[:, 4, :])
                    copy(xcols(g), banks[:, 4, :]).then_inc(agg_kept, 1)

            groups(act, [("turned", 0, 2), ("exp", 2, 3), ("probT", 0, 3), ("keys", 0, 2), ("probT", 1, 3),
                         ("probT", 2, 3), ("exp", 3, 3), ("queries", 0, 2), ("probT", 3, 3), ("round", 0, 4),
                         ("attended", 0, 3), ("exp", 0, 2), ("exp", 1, 2), ("aggregated", 0, 4)], do, pairs=3)

            act.wait_ge(bn_work_done, 6)

            def hidden(i, u):
                g = i * 2 + u
                for m in range(2):
                    act.wait_ge(w1b_sums, g * 2 + m + 1)
                    wait_if(act, hid_lo, g * 2)
                    nc.scalar.activation(hid_f[m], banks[:, 2 * u + m, :], ACT.Relu, bias=bn_work[:, 14 + m:15 + m],
                                         scale=bn_work[:, 10 + m:11 + m]).then_inc(hid_kept, 1)

            def second_sums(i, u):
                g = i * 2 + u
                act.wait_ge(w2_sums, g + 1)
                copy(xcols(g), banks[:, 4 + u, :]).then_inc(z_kept, 1)

            def hidden_pair(i):
                hidden(i, 1)
                second_sums(i, 0)
                hidden(i + 1, 0)
                second_sums(i, 1)

            hidden(0, 0)
            hidden_pair(0)
            with act.Fori(1, GROUPS // 2 - 1) as i:
                hidden_pair(i)
            hidden(GROUPS // 2 - 1, 1)
            second_sums(GROUPS // 2 - 1, 0)
            second_sums(GROUPS // 2 - 1, 1)

            act.wait_ge(bn_work_done, 11)

            def do(what, part, g, place):
                if what == "scaled":
                    wait_if(act, z_turned, g)
                    nc.scalar.activation(z_f, xcols(g), ACT.Identity, bias=bn_work[:, 14:15],
                                         scale=bn_work[:, 10:11]).then_inc(z_scaled, 1)
                if what == "x3":
                    act.wait_ge(x3_kept, g + 1)
                    wait_if(act, mixed, (g - 1) * GB)
                    copy(x3_r[place][0], x3_f[place]).then_inc(x3_hi, 1)
                if what == "mixed":
                    act.wait_ge(mixed, g * GB + part + 1)
                    wait_if(act, w3_sums, g)
                    at = part * 3 * P
                    copy(mix_r[0][:, at:at + 3 * P], banks[:, 2 + part, 0:3 * P]).then_inc(mixed_hi, 1)
                if what == "sums":
                    act.wait_ge(w3_sums, g + 1)
                    wait_if(act, o_turned, g)
                    nc.scalar.activation(oT_f, banks[:, 1, :], ACT.Identity, bias=out_bias).then_inc(w3_kept, 1)
                if what == "norm":
                    act.wait_ge(shift4, g + 1)
                    wait_if(act, out_stored[place], (g - place) * 8)
                    _, (_, _, _, _, _, rstd) = ln_cols(1, GB)
                    for b in range(GB):
                        ins = nc.scalar.activation(o_f[place][:, b * P:(b + 1) * P], y4[:, b * P:(b + 1) * P],
                                                   ACT.Identity, bias=shift_cols[:, b:b + 1], scale=rstd[:, b:b + 1])
                    ins.then_inc(out_ready, 1)

            groups(act, [("x3", 0, 2), ("sums", 0, 3), ("scaled", 0, 0), ("mixed", 0, 2), ("mixed", 1, 2),
                         ("mixed", 2, 2), ("mixed", 3, 2), ("norm", 0, 3)], do, pairs=3)

        @block.vector
        def _(dve):
            dve.wait_ge(lstm_weights_in, 16 * NLSTM)
            dve.wait_ge(ident_one, 1)
            nc.vector.tensor_tensor(lstm_bias, bias_parts[:, 0:4 * SKIPS], bias_parts[:, 4 * SKIPS:8 * SKIPS], ALU.add)
            nc.vector.tensor_copy(ident_bf[:, :], ident)
            for b in range(GB):
                ins = nc.vector.tensor_scalar(mask[:, b * P:(b + 1) * P], raw["adj"], 0.0, MASKED,
                                              ALU.is_equal, ALU.mult)
            ins.then_inc(consts_made, 1)
            for n, (name, (hi, lo)) in enumerate(splits[3:]):
                dve.wait_ge(weights_hi, n + 4)
                nc.vector.tensor_tensor(lo, raw[name], f32(hi), ALU.subtract).then_inc(lstm_weights_lo, 1)
            dve.wait_ge(bias0_made, 1)

            ORDER = order_of(DVE_ORDER)

            def do(at_event, rr, k):
                what, n, lane, _ = ORDER[at_event]
                if what == "gcn":
                    for half in range(2):
                        cols = slice(half * HALF, (half + 1) * HALF)
                        at = 2 * n + half
                        if n == 0:
                            dve.wait_ge(gcn_hi[lane], rr * 8 + at + 1)
                            nc.vector.tensor_tensor(mid_r[lane][1][:, cols], bank(bank_set(what, n, lane), half),
                                                    f32(mid_r[lane][0][:, cols]), ALU.subtract)\
                              .then_inc(gcn_lo[lane], 1)
                        elif n == 1 or n == 2:
                            dve.wait_ge(gcn_sums[lane], rr * 8 + at + 1)
                            bias = (gcn_bias0 if n == 1 else gcn_bias1).unsqueeze(1).broadcast_to([P, LB // 2, P])
                            nc.vector.tensor_tensor(
                                by_batch(tmp[lane][:, cols], LB // 2),
                                by_batch(bank(bank_set(what, n, lane), (2 if n == 1 else 0) + half), LB // 2), bias,
                                ALU.add)\
                              .then_inc(gcn_biased[lane], 1)
                            dve.wait_ge(gcn_hi[lane], rr * 8 + at + 1)
                            dst = (h_r if n == 1 else mid_r)[lane]
                            nc.vector.scalar_tensor_tensor(
                                out=dst[1][:, cols], in0=tmp[lane][:, cols], scalar=0.0,
                                in1=f32(dst[0][:, cols]), op0=ALU.max if n == 1 else ALU.add,
                                op1=ALU.subtract).then_inc(gcn_lo[lane], 1)
                        else:
                            dve.wait_ge(gcn_hi[lane], rr * 8 + at + 1)
                            nc.vector.scalar_tensor_tensor(
                                out=h_r[lane][1][:, cols], in0=bank(bank_set(what, n, lane), 2 + half), scalar=0.0,
                                in1=f32(h_r[lane][0][:, cols]), op0=ALU.max, op1=ALU.subtract)\
                              .then_inc(gcn_lo[lane], 1)
                if what == "cell":
                    step = STEPS[n]
                    p, t, _, _, gates = step
                    cols = step_cols(step)
                    gi, gf, gg, go = (gate_f[lane][q][:, 0:cols] for q in range(4))
                    cell = cell_f[lane][:, 0:cols]
                    at = rr * NGATE + gate_at[n]
                    dve.wait_ge(gates_open[lane], at + 2)
                    if t == 0:
                        nc.vector.tensor_tensor(cell, gi, gg, ALU.mult).then_inc(cells[lane], 1)
                    else:
                        later = rr * NLATER + sum(q[1] > 0 for q in STEPS[:n])
                        nc.vector.tensor_tensor(gi, gi, gg, ALU.mult)
                        dve.wait_ge(gates_open[lane], at + 3)
                        nc.vector.tensor_tensor(cell, gf, cell, ALU.mult).then_inc(cell_parts[lane], 1)
                        dve.wait_ge(cell_parts[lane], later + 1)
                        nc.vector.tensor_tensor(cell, cell, gi, ALU.add).then_inc(cells[lane], 1)
                if what == "hidden":
                    step = STEPS[n]
                    p, t, _, _, gates = step
                    last = t == p - 1
                    if n == 0:
                        wait_if(dve, x1_kept[lane], rr)
                    src = h_f[lane] if last else hs_f[lane]
                    dst = h_r[lane] if last else hs_r[lane]
                    view = (lambda a: windows(a, step)) if last else (lambda a: like_windows(a, step))
                    dve.wait_ge(cell_tanh[lane], rr * NSTEP + n + 1)
                    nc.vector.tensor_tensor(view(src), like_windows(gate_f[lane][O], step),
                                            like_windows(gate_f[lane][G], step), ALU.mult).then_inc(states[lane], 1)
                    if n == NSTEP - 1:
                        return
                    dve.wait_ge(states[lane], rr * NSTEP + n + 1)
                    nc.vector.tensor_copy(view(dst[0]), view(src)).then_inc(states_hi[lane], 1)
                if what == "residual":
                    for half in range(2):
                        cols = slice(half * HALF, (half + 1) * HALF)
                        dve.wait_ge(h_turned[lane], rr * 2 + half + 1)
                        nc.vector.tensor_tensor(h_f[lane][:, cols], x_in[lane][:, cols],
                                                bank(bank_set(what, n, lane), half), ALU.add)\
                          .then_inc(norm_work[lane], 1)
                if what == "statistics":
                    dve.wait_ge(norm_work[lane], rr * 5 + 2)
                    ln_statistics(dve, h_f[lane], lane, LB, norm_work[lane], rr * 5 + 2, variances[lane])
                if what == "norm":
                    dve.wait_ge(rstds[lane], rr + 1)
                    at = rr * LANES + lane
                    ln_apply(xcols(at, LC), h_f[lane], lane, LB).then_inc(x1_kept[lane], 1)

            cycles(dve, ORDER, do)

            for lane in range(LANES):
                dve.wait_ge(x1_kept[lane], units_of(lane))
            for part in kd_r[0]:
                nc.vector.memset(f32(part), 0.0).then_inc(k0_zeros, 1)

            dve.wait_ge(late_weights_in, 16 * LATE)
            dve.wait_ge(adjk_made, 3)
            nc.vector.tensor_tensor(nadj, nadj, ident, ALU.add)
            nc.vector.tensor_tensor(nadjT, nadjT, ident, ALU.add).then_inc(hat_work_done, 1)
            dve.wait_ge(hat_work_done, 1)
            nc.vector.tensor_reduce(out=hat_work[:, 0:1], in_=nadj, axis=AX.X, op=ALU.add)
            nc.vector.tensor_reduce(out=hat_work[:, 1:2], in_=nadjT, axis=AX.X, op=ALU.add)
            nc.vector.tensor_tensor(diag, nadj, ident, ALU.mult).then_inc(hat_work_done, 1)
            dve.wait_ge(hat_work_done, 2)
            nc.vector.tensor_reduce(out=hat_work[:, 2:3], in_=diag, axis=AX.X, op=ALU.add)
            nc.vector.tensor_tensor(hat_work[:, 3:4], hat_work[:, 0:1], hat_work[:, 1:2], ALU.add)\
              .then_inc(hat_work_done, 1)
            dve.wait_ge(hat_work_done, 3)
            nc.vector.tensor_tensor(hat_work[:, 4:5], hat_work[:, 3:4], hat_work[:, 2:3], ALU.subtract)\
              .then_inc(hat_work_done, 1)

            def do(what, part, g, place):
                if what == "turned":
                    dve.wait_ge(xT_hi, g + 1)
                    nc.vector.tensor_tensor(xT_r[1], banks[:, 4, :], f32(xT_r[0]), ALU.subtract).then_inc(xT_lo, 1)
                if what == "keys":
                    dve.wait_ge(k_hi, g * HEADS + HEADS)
                    for h in range(HEADS):
                        hi, lo = (key_block(kd_r[place][j], h) for j in range(2))
                        ins = nc.vector.tensor_tensor(lo, by_batch(banks[h * DH:(h + 1) * DH, 4, :], GB), f32(hi),
                                                      ALU.subtract)
                    ins.then_inc(k_lo, 1)
                if what == "queries":
                    dve.wait_ge(q_hi, g + 1)
                    nc.vector.scalar_tensor_tensor(out=q_r[1], in0=banks[:, 5, :], scalar=DH ** -0.5, in1=f32(q_r[0]),
                                                   op0=ALU.mult, op1=ALU.subtract).then_inc(q_lo, 1)
                    if isinstance(g, int) and g == 0:
                        finish_hat()
                if what == "values":
                    dve.wait_ge(v_sums, g + 1)
                    if isinstance(g, int) and g == 0:
                        dve.wait_ge(v_ones, 2)
                    wait_if(dve, attended, (g - 1) * GB)
                    nc.vector.tensor_copy(vals[place].rearrange("q (n d) -> q n d", d=VW)[:, :, 0:DH],
                                          banks[:, 5, :].rearrange("q (n d) -> q n d", d=DH)).then_inc(v_kept, 1)
                if what == "soft":
                    dve.wait_ge(scores, g * GB + part + 1)
                    score = banks[:, part % 2, :].rearrange("q (h j) -> q h j", h=HEADS)
                    largest = maxes[:, part * HEADS:(part + 1) * HEADS]
                    nc.vector.tensor_reduce(out=largest, in_=score, axis=AX.X, op=ALU.max).then_inc(row_max, 1)
                    dve.wait_ge(row_max, g * GB + part + 1)
                    wait_if(dve, prob_turned, (g - 1) * GB + part + 1)
                    nc.vector.tensor_tensor(prob[part].rearrange("q (h j) -> q h j", h=HEADS), score,
                                            largest.unsqueeze(2).broadcast_to([P, HEADS, P]),
                                            ALU.subtract).then_inc(shifted, 1)
                if what == "divide":
                    dve.wait_ge(att_turned, g + 1)
                    n = GB * HEADS // 2
                    outs = [banks[:, 6 + j, :].rearrange("q (b h d) -> q b h d", b=GB, h=2) for j in range(2)]
                    dens = [rden[:, j * n:(j + 1) * n].rearrange("q (b h) -> q b h", h=2) for j in range(2)]
                    for j in range(2):
                        ins = nc.vector.reciprocal(dens[j].unsqueeze(3), outs[j][:, :, :, DH:DH + 1])
                    ins.then_inc(att_work, 1)
                    dve.wait_ge(att_work, g * ATT_WORK + 1)
                    for j in range(2):
                        dst = y_f.rearrange("q (b k h d) -> q b k h d", b=GB, k=2, h=2)[:, :, j, :, :]
                        ins = nc.vector.tensor_tensor(dst, outs[j][:, :, :, 0:DH],
                                                      dens[j].unsqueeze(3).broadcast_to([P, GB, 2, DH]), ALU.mult)
                    ins.then_inc(att_work, 1)
                if what == "add":
                    dve.wait_ge(y_sums, g + 1)
                    ln_sums(y_f, 0, GB).then_inc(att_work, 1)
                if what == "norm":
                    dve.wait_ge(rstd2, g + 1)
                    wait_if(dve, x2_lo, g)
                    wait_if(dve, x2_stored, g * 16)
                    ln_apply(x2_f, y_f, 0, GB).then_inc(x2_kept, 1)
                if what == "agg_low":
                    dve.wait_ge(agg_kept, g + 1)
                    nc.vector.tensor_tensor(agg_r[0][1], banks[:, 4, :], f32(agg_r[0][0]), ALU.subtract)\
                      .then_inc(agg_lo, 1)
                if what == "stats":
                    dve.wait_ge(w1_sums, g * 2 + part + 1)
                    at = part * GROUPS * 6 + g * 6
                    dst = bn1_stats[:, at:at + 6] if isinstance(at, int) else bn1_stats[:, bass.ds(at, 6)]
                    nc.vector.bn_stats(dst, banks[:, 5, :]).then_inc(bn1_done, 1)

            def finish_hat():
                dve.wait_ge(hat_pow, 1)
                nc.vector.tensor_scalar(diag, ident, hat_work[:, 5:6], None, ALU.mult).then_inc(hat_work_done, 1)
                nc.vector.tensor_scalar(nadjT, nadjT, hat_work[:, 5:6], None, ALU.mult).then_inc(hat_work_done, 1)
                dve.wait_ge(hat_work_done, 6)
                dve.wait_ge(hat_product, 1)
                nc.vector.tensor_tensor(raw2["hatT"], nadjT, banks[:, 0, 0:P], ALU.mult).then_inc(hat_turned, 1)

            groups(dve, [("queries", 0, 1), ("norm", 0, 3), ("soft", 0, 1), ("soft", 1, 1), ("stats", 1, 4),
                         ("soft", 2, 1), ("agg_low", 0, 3), ("divide", 0, 2), ("values", 0, 1),
                         ("turned", 0, 0), ("soft", 3, 1), ("add", 0, 2), ("stats", 0, 3), ("keys", 0, 0)], do, pairs=3)

            bn1_v = bn1_stats.rearrange("q (m g k) -> q m g k", m=2, k=6)

            dve.wait_ge(bn1_done, 2 * GROUPS)
            for m in range(2):
                ins = nc.vector.bn_aggr(bn_work[:, 2 * m:2 * m + 2], bn1_v[:, m, :, :].rearrange("q g k -> q (g k)"))
            ins.then_inc(bn_work_done, 1)
            dve.wait_ge(bn_work_done, 1)
            mv = bn_work[:, 0:4].rearrange("q (m k) -> q m k", k=2)
            nc.vector.tensor_tensor(bn_work[:, 4:6], mv[:, :, 0], bn_cols[:, 0:2], ALU.add).then_inc(bn_work_done, 1)
            nc.vector.tensor_scalar(bn_work[:, 6:8], mv[:, :, 1], EPS, None, ALU.add).then_inc(bn_var, 1)
            dve.wait_ge(bn_work_done, 2)
            nc.vector.tensor_tensor(bn_work[:, 12:14], bn_cols[:, 0:2], bn_work[:, 4:6], ALU.subtract)\
              .then_inc(bn_work_done, 1)
            dve.wait_ge(bn_rstd, 1)
            nc.vector.tensor_tensor(bn_work[:, 10:12], bn_work[:, 8:10], bn_cols[:, 2:4], ALU.mult)\
              .then_inc(bn_work_done, 1)
            dve.wait_ge(bn_work_done, 4)
            nc.vector.tensor_tensor(bn_work[:, 16:18], bn_work[:, 12:14], bn_work[:, 10:12], ALU.mult)\
              .then_inc(bn_work_done, 1)
            dve.wait_ge(bn_work_done, 5)
            nc.vector.tensor_tensor(bn_work[:, 14:16], bn_work[:, 16:18], bn_cols[:, 4:6], ALU.add)\
              .then_inc(bn_work_done, 1)

            def agg_high(i, u):
                g = i * 2 + u
                wait_if(dve, w1b_sums, (g - 2) * 2 + 2)
                nc.vector.tensor_copy(agg_r[u][0], xcols(g)).then_inc(aggb_hi, 1)

            def hidden_parts(i, u):
                g = i * 2 + u
                wait_if(dve, w2_sums, g - 1)
                for m in range(2):
                    cols = slice(m * GC, (m + 1) * GC)
                    dve.wait_ge(hid_kept, g * 2 + m + 1)
                    nc.vector.tensor_copy(hid_r[u][0][:, cols], hid_f[m]).then_inc(hid_hi, 1)
                dve.wait_ge(hid_hi, g * 2 + 2)
                nc.vector.tensor_tensor(hid_r[u][1][:, 0:GC], hid_f[0], f32(hid_r[u][0][:, 0:GC]), ALU.subtract)\
                  .then_inc(hid_lo, 1)

            def second_stats(i, u):
                g = i * 2 + u
                dve.wait_ge(z_kept, g + 1)
                at = g * 6
                dst = bn2_stats[:, at:at + 6] if isinstance(at, int) else bn2_stats[:, bass.ds(at, 6)]
                nc.vector.bn_stats(dst, xcols(g)).then_inc(bn2_done, 1)

            agg_high(0, 0)
            agg_high(0, 1)
            hidden_parts(0, 0)
            agg_high(1, 0)
            hidden_parts(0, 1)
            second_stats(0, 0)
            with dve.Fori(1, GROUPS // 2 - 1) as i:
                agg_high(i, 1)
                hidden_parts(i, 0)
                second_stats(i - 1, 1)
                agg_high(i + 1, 0)
                hidden_parts(i, 1)
                second_stats(i, 0)
            last_pair = GROUPS // 2 - 1
            agg_high(last_pair, 1)
            hidden_parts(last_pair, 0)
            second_stats(last_pair - 1, 1)
            hidden_parts(last_pair, 1)
            second_stats(last_pair, 0)
            second_stats(last_pair, 1)

            dve.wait_ge(bn2_done, GROUPS)
            nc.vector.bn_aggr(bn_work[:, 0:2], bn2_stats).then_inc(bn_work_done, 1)
            dve.wait_ge(bn_work_done, 7)
            nc.vector.tensor_tensor(bn_work[:, 4:5], bn_work[:, 0:1], bn_cols[:, 6:7], ALU.add)\
              .then_inc(bn_work_done, 1)
            nc.vector.tensor_scalar(bn_work[:, 6:7], bn_work[:, 1:2], EPS, None, ALU.add).then_inc(bn_var, 1)
            dve.wait_ge(bn_work_done, 8)
            nc.vector.tensor_tensor(bn_work[:, 12:13], bn_cols[:, 6:7], bn_work[:, 4:5], ALU.subtract)\
              .then_inc(bn_work_done, 1)
            dve.wait_ge(bn_rstd, 2)
            dve.wait_ge(hid_kept, 2 * GROUPS)
            nc.vector.tensor_tensor(bn_work[:, 10:11], bn_work[:, 8:9], bn_cols[:, 7:8], ALU.mult)\
              .then_inc(bn_work_done, 1)
            dve.wait_ge(bn_work_done, 10)
            nc.vector.scalar_tensor_tensor(out=bn_work[:, 14:15], in0=bn_work[:, 12:13], scalar=bn_work[:, 10:11],
                                           in1=bn_cols[:, 8:9], op0=ALU.mult, op1=ALU.add).then_inc(bn_work_done, 1)

            def do(what, part, g, place):
                if what == "third":
                    dve.wait_ge(z_turned, g + 1)
                    wait_if(dve, x3_kept, g)
                    dve.wait_ge(x2_loaded[place], (g - place) * 8 + 16)
                    nc.vector.tensor_tensor(y3, banks[:, 0, :], x2_back[place], ALU.add).then_inc(ln3_work, 1)
                    dve.wait_ge(ln3_work, g * LN_WORK + 1)
                    ln_statistics(dve, y3, 0, GB, ln3_work, g * LN_WORK + 1, var3)
                if what == "third_norm":
                    dve.wait_ge(rstd3, g + 1)
                    wait_if(dve, x3_lo, g - 1)
                    wait_if(dve, ln4_work, (g - 2) * LN_WORK + 1)
                    ln_apply(x3_f[place], y3, 0, GB).then_inc(x3_kept, 1)
                if what == "mixed":
                    at = part * 3 * P
                    dve.wait_ge(mixed_hi, g * GB + part + 1)
                    nc.vector.tensor_tensor(mix_r[1][:, at:at + 3 * P], banks[:, 2 + part, 0:3 * P],
                                            f32(mix_r[0][:, at:at + 3 * P]), ALU.subtract).then_inc(mixed_lo, 1)
                if what == "fourth":
                    dve.wait_ge(o_turned, g + 1)
                    wait_if(dve, out_ready, g)
                    nc.vector.tensor_tensor(y4, banks[:, 6, :], x3_f[place], ALU.add).then_inc(ln4_work, 1)
                    dve.wait_ge(ln4_work, g * LN_WORK + 1)
                    ln_statistics(dve, y4, 1, GB, ln4_work, g * LN_WORK + 1, var4, negate=True)

            groups(dve, [("third_norm", 0, 2), ("third", 0, 1), ("fourth", 0, 3), ("mixed", 0, 2),
                         ("mixed", 1, 2), ("mixed", 2, 2), ("mixed", 3, 2)], do, pairs=3)

        @block.tensor
        def _(pe):
            def banks_free(event, k):
                at, back = event, 0
                for _ in range(2 * len(ORDER)):
                    at -= 2
                    if at < 0:
                        at, back = at + len(ORDER), back + 1
                    what, n, lane, late = ORDER[at]
                    rr = k - (late + back)
                    if isinstance(rr, int) and not exists(lane, rr):
                        continue
                    if what == "lstm":
                        pe.wait_ge(gates_open[lane], rr * NGATE + gate_at[n] + len(STEPS[n][4]))
                    elif what == "residual":
                        pe.wait_ge(norm_work[lane], rr * 5 + 2)
                    elif n in (0, 3):
                        pe.wait_ge(gcn_lo[lane], rr * 8 + 2 * n + 2)
                    else:
                        pe.wait_ge(gcn_biased[lane], rr * 4 + 2 * n)
                    return

            pe.wait_ge(weights_in, 16 * NCONV)
            pe.matmul(bank(0, 0)[:, 0:P], raw["bg0"], raw["adjT"], start=True, stop=True).then_inc(rowsum_product, 1)
            pe.wait_ge(weights_lo, 3)
            pe.wait_ge(ident_one, 1)
            pe.wait_ge(bias0_made, 1)

            ORDER = order_of(PE_ORDER)

            def do(at_event, rr, k):
                what, n, lane, _ = ORDER[at_event]
                banks_of = bank_set(what, n, lane)
                if what == "gcn":
                    for half in range(2):
                        out = bank(banks_of, (0, 2, 0, 2)[n] + half)
                        if half == 0:
                            banks_free(at_event, k)
                        if n == 0:
                            pe.wait_ge(x_lo[lane], rr + 1)
                        else:
                            pe.wait_ge(gcn_hi[lane], rr * 8 + 2 * (n - 1) + half + 1)
                            pe.wait_ge(gcn_lo[lane], rr * 8 + 2 * (n - 1) + half + 1)
                        if n == 1:
                            ins = mm3(pe, out, wg0_r, cut(mid_r[lane], half * HALF, (half + 1) * HALF))
                        else:
                            src = (x_r, None, h_r, mid_r)[n][lane]
                            moving = wg1_r if n == 2 else adjT_r
                            for b in range(LB // 2):
                                at = half * HALF + b * P
                                ins = mm3(pe, out[:, b * P:(b + 1) * P], cut(src, at, at + P), moving)
                        ins.then_inc(gcn_sums[lane], 1)
                if what == "lstm":
                    step = STEPS[n]
                    p, t, _, _, gates = step
                    banks_free(at_event, k)
                    if n < 2:
                        pe.wait_ge(gcn_hi[lane], rr * 8 + 7 + n)
                        pe.wait_ge(gcn_lo[lane], rr * 8 + 7 + n)
                    if n == 0 and isinstance(rr, int) and rr == 0:
                        pe.wait_ge(lstm_weights_lo, 3)
                    inputs = [windows(h_r[lane][j], step) for j in range(2)]
                    if t == 0 and n > 1:
                        pe.wait_ge(states_lo[lane], rr * (NSTEP - 1) + n)
                    for gate in gates:
                        out = like_windows(bank(banks_of, gate), step)
                        at = ((p - 1) * 4 + gate) * P
                        ins = mm3(pe, out, cut(wih_r, at, at + P), inputs, stop=(t == 0))
                        if t == 0:
                            ins.then_inc(gate_sums[lane], 1)
                    if t:
                        pe.wait_ge(states_lo[lane], rr * (NSTEP - 1) + n)
                        carried = [like_windows(hs_r[lane][j], step) for j in range(2)]
                        for gate in gates:
                            at = ((p - 2) * 4 + gate) * P
                            mm3(pe, like_windows(bank(banks_of, gate), step), cut(whh_r, at, at + P), carried,
                                start=False).then_inc(gate_sums[lane], 1)
                if what == "residual":
                    banks_free(at_event, k)
                    pe.wait_ge(states[lane], rr * NSTEP + NSTEP)
                    for half in range(2):
                        for b in range(LB // 2):
                            at = half * HALF + b * P
                            ins = pe.transpose(bank(banks_of, half)[:, b * P:(b + 1) * P],
                                               h_f[lane][:, at:at + P], ident)
                        ins.then_inc(h_turned[lane], 1)

            cycles(pe, ORDER, do)

            for lane in range(LANES):
                pe.wait_ge(x1_kept[lane], units_of(lane))

            ATTENTION = [("score", 1, 1), ("first", 1, 4), ("score", 2, 1), ("aggregate", 0, 3),
                         ("attended", 0, 2), ("values", 0, 1), ("turn", 0, 0), ("probT", 0, 1),
                         ("score", 3, 1), ("keys", 0, 0), ("first", 0, 3), ("attend", 0, 1), ("probT", 1, 1),
                         ("probT", 2, 1), ("queries", 0, 0), ("attend", 1, 1), ("probT", 3, 1),
                         ("attend", 2, 1), ("attend", 3, 1), ("score", 0, 0)]
            BANK = {"turn": 4, "keys": 4, "aggregate": 4, "queries": 5, "values": 5, "first": 5}
            LEFT = {"turn": xT_lo, "keys": k_lo, "aggregate": agg_lo, "queries": q_lo, "values": v_kept,
                    "first": bn1_done}

            def bank_free(what, part, g):
                at = [v[0:2] for v in ATTENTION].index((what, part))
                behind = ATTENTION[at][2]
                for _ in range(8 * len(ATTENTION)):
                    at -= 1
                    if at < 0:
                        at, behind = at + len(ATTENTION), behind - 1
                    user, half, late = ATTENTION[at]
                    if BANK.get(user) != BANK[what]:
                        continue
                    before = g + (behind - late)
                    if isinstance(before, int) and not 0 <= before < GROUPS:
                        continue
                    pe.wait_ge(LEFT[user], before * 2 + (half + 1) if user == "first" else before + 1)
                    return

            def do(what, part, g, place):
                if what == "turn":
                    pe.wait_ge(xg_copied, g + 1)
                    bank_free(what, part, g)
                    for b in range(GB):
                        ins = pe.transpose(banks[:, 4, b * P:(b + 1) * P], xg[:, b * P:(b + 1) * P], ident)
                    ins.then_inc(x_turned, 1)
                if what == "keys":
                    pe.wait_ge(xT_lo, g + 1)
                    bank_free(what, part, g)
                    mm3(pe, banks[:, 4, :], cut(wqkv_r, P, 2 * P), xT_r).then_inc(k_sums, 1)
                if what == "queries":
                    pe.wait_ge(xT_lo, g + 1)
                    bank_free(what, part, g)
                    mm3(pe, banks[:, 5, :], cut(wqkv_r, 0, P), xT_r).then_inc(q_sums, 1)
                    if isinstance(g, int) and g == 0:
                        pe.wait_ge(hat_work_done, 5)
                        pe.wait_ge(ones_made, 1)
                        pe.matmul(banks[:, 0, 0:P], ones_sq, diag, start=True, stop=True).then_inc(hat_product, 1)
                if what == "values":
                    bank_free(what, part, g)
                    for b in range(GB):
                        ins = mm3(pe, banks[:, 5, b * P:(b + 1) * P], cut(xT_r, b * P, (b + 1) * P),
                                  cut(wqkv_r, 2 * P, 3 * P))
                    ins.then_inc(v_sums, 1)
                if what == "score":
                    if part == 0:
                        if isinstance(g, int) and g == 0:
                            pe.wait_ge(hat_turned, 1)
                        pe.wait_ge(k_lo, g + 1)
                        pe.wait_ge(q_lo, g + 1)
                    wait_if(pe, shifted, g * GB + part - 1)
                    out = banks[:, part % 2, :]
                    keys = kd_r[place]
                    at = part * HEADS * P
                    pe.matmul(out, ident_bf[:, :], mask[:, :], start=True, stop=False)
                    mm3(pe, out, cut(q_r, part * P, (part + 1) * P), cut(keys, at, at + HEADS * P), start=False)\
                        .then_inc(scores, 1)
                if what == "probT":
                    pe.wait_ge(exps, g * GB + part + 1)
                    wait_if(pe, probT_kept, g * GB + part - 1)
                    for h in range(HEADS):
                        ins = pe.transpose(banks[:, 2 + part % 2, h * P:(h + 1) * P],
                                           prob[part][:, h * P:(h + 1) * P], ident)
                    ins.then_inc(prob_turned, 1)
                if what == "attend":
                    if part == 0:
                        pe.wait_ge(v_kept, g + 1)
                        wait_if(pe, att_work, (g - 1) * ATT_WORK + 2)
                    pe.wait_ge(probT_kept, g * GB + part + 1)
                    for h in range(HEADS):
                        at, rows = (part * HEADS + h) * VW, (h % 2) * VW
                        ins = pe.matmul(banks[rows:rows + VW, 6 + h // 2, part * P:(part + 1) * P],
                                        vals[place][:, at:at + VW], probT[part][:, h * P:(h + 1) * P],
                                        start=True, stop=True)
                    ins.then_inc(attended, 1)
                if what == "attended":
                    pe.wait_ge(att_kept, g * 2 + 2)
                    for j in range(2):
                        for b in range(GB):
                            ins = pe.transpose(banks[:, 6 + j, b * P:(b + 1) * P], attT[j][:, b * P:(b + 1) * P],
                                               ident)
                    ins.then_inc(att_turned, 1)
                if what == "aggregate":
                    if isinstance(g, int) and g == 0:
                        pe.wait_ge(late_lo, len(splits2))
                    pe.wait_ge(x2_lo, g + 1)
                    bank_free(what, part, g)
                    for b in range(GB):
                        ins = mm3(pe, banks[:, 4, b * P:(b + 1) * P], cut(x2_r, b * P, (b + 1) * P), hatT_r)
                    ins.then_inc(agg_sums, 1)
                if what == "first":
                    pe.wait_ge(agg_lo, g + 1)
                    bank_free(what, part, g)
                    mm3(pe, banks[:, 5, :], cut(w1_r, part * P, (part + 1) * P), agg_r[0]).then_inc(w1_sums, 1)

            groups(pe, ATTENTION, do, pairs=3)

            pe.wait_ge(bn1_done, 2 * GROUPS)

            def first_again(i, u):
                g = i * 2 + u
                pe.wait_ge(aggb_lo, g + 1)
                for m in range(2):
                    wait_if(pe, hid_kept, (g - 2) * 2 + m + 1)
                    mm3(pe, banks[:, 2 * u + m, :], cut(w1_r, m * P, (m + 1) * P), agg_r[u]).then_inc(w1b_sums, 1)

            def second_layer(i, u):
                g = i * 2 + u
                pe.wait_ge(hid_lo, g * 2 + 2)
                wait_if(pe, z_kept, g - 1)
                out = banks[:, 4 + u, :]
                mm3(pe, out, cut(w2_r, 0, P), cut(hid_r[u], 0, GC), stop=False)
                mm3(pe, out, cut(w2_r, P, 2 * P), cut(hid_r[u], GC, 2 * GC), start=False).then_inc(w2_sums, 1)

            last_pair = GROUPS // 2 - 1
            first_again(0, 0)
            first_again(0, 1)
            second_layer(0, 0)
            first_again(1, 0)
            second_layer(0, 1)
            with pe.Fori(1, last_pair) as i:
                first_again(i, 1)
                second_layer(i, 0)
                first_again(i + 1, 0)
                second_layer(i, 1)
            first_again(last_pair, 1)
            second_layer(last_pair, 0)
            second_layer(last_pair, 1)

            pe.wait_ge(bn2_done, GROUPS)
            pe.wait_ge(z_kept, GROUPS)

            def do(what, part, g, place):
                if what == "turn":
                    pe.wait_ge(z_scaled, g + 1)
                    wait_if(pe, ln3_work, (g - 1) * LN_WORK + 1)
                    for b in range(GB):
                        ins = pe.transpose(banks[:, 0, b * P:(b + 1) * P], z_f[:, b * P:(b + 1) * P], ident)
                    ins.then_inc(z_turned, 1)
                if what == "mix":
                    pe.wait_ge(x3_lo, g + 1)
                    wait_if(pe, mixed_lo, (g - 1) * GB + part + 1)
                    mm3(pe, banks[:, 2 + part, 0:3 * P], cut(x3_r[place], part * P, (part + 1) * P), adjk_r)\
                        .then_inc(mixed, 1)
                if what == "sums":
                    pe.wait_ge(mixed_lo, g * GB + GB)
                    wait_if(pe, w3_kept, g)
                    for k in range(3):
                        mixes = [m.rearrange("q (b k t) -> q b k t", b=GB, k=3)[:, :, k, :] for m in mix_r]
                        ins = mm3(pe, by_batch(banks[:, 1, :], GB), cut(w3_r, k * P, (k + 1) * P), mixes,
                                  start=k == 0, stop=k == 2)
                    ins.then_inc(w3_sums, 1)
                if what == "back":
                    pe.wait_ge(w3_kept, g + 1)
                    wait_if(pe, ln4_work, (g - 1) * LN_WORK + 1)
                    for b in range(GB):
                        ins = pe.transpose(banks[:, 6, b * P:(b + 1) * P], oT_f[:, b * P:(b + 1) * P], ident)
                    ins.then_inc(o_turned, 1)

            groups(pe, [("mix", 2, 3), ("mix", 3, 3), ("sums", 0, 3), ("back", 0, 3), ("mix", 0, 2),
                        ("turn", 0, 0), ("mix", 1, 2)], do, pairs=3)


_INS = ['x', 'adj', 'adjT', 'Wg0', 'bg0', 'Wg1', 'bg1', 'WihT', 'WhhT', 'bih', 'bhh', 'Wqkv', 'W1T', 'b1', 'g1', 'be1',
        'W2T', 'b2', 'g2', 'be2', 'W3', 'bias3']


def kernel(x, adj, L0_gnn_Wg0, L0_gnn_bg0, L0_gnn_Wg1, L0_gnn_bg1, L0_gnn_Wih, L0_gnn_Whh, L0_gnn_bih, L0_gnn_bhh,
           L1_gnn_W, L2_gnn_W1, L2_gnn_b1, L2_gnn_g1, L2_gnn_be1, L2_gnn_W2, L2_gnn_b2, L2_gnn_g2, L2_gnn_be2,
           L3_gnn_W, L3_gnn_bias):
    import numpy as np
    import concourse.bacc as bacc
    from concourse.bass_utils import run_bass_kernel_spmd

    def gate_columns(a):
        return np.asarray(a).reshape(SKIPS * 4, P).T

    def halves(a):
        return np.asarray(a).reshape(2, P).T

    laid = {
        'x': np.asarray(x).transpose(1, 0, 2),
        'adj': adj, 'adjT': np.asarray(adj).T,
        'Wg0': L0_gnn_Wg0, 'bg0': L0_gnn_bg0, 'Wg1': L0_gnn_Wg1, 'bg1': L0_gnn_bg1,
        'WihT': np.asarray(L0_gnn_Wih).transpose(2, 0, 1).reshape(P, -1),
        'WhhT': np.asarray(L0_gnn_Whh)[1:].transpose(2, 0, 1).reshape(P, -1),
        'bih': gate_columns(L0_gnn_bih), 'bhh': gate_columns(L0_gnn_bhh),
        'Wqkv': L1_gnn_W,
        'W1T': np.asarray(L2_gnn_W1).T, 'b1': halves(L2_gnn_b1), 'g1': halves(L2_gnn_g1), 'be1': halves(L2_gnn_be1),
        'W2T': np.asarray(L2_gnn_W2).T.reshape(2, P, P).transpose(1, 0, 2).reshape(P, -1),
        'b2': L2_gnn_b2, 'g2': L2_gnn_g2, 'be2': L2_gnn_be2,
        'W3': np.asarray(L3_gnn_W).transpose(1, 0, 2).reshape(P, -1), 'bias3': L3_gnn_bias,
    }
    nc = bacc.Bacc("TRN2", target_bir_lowering=False, num_devices=1)
    arrays, args = {}, []
    for name in _INS:
        a = np.ascontiguousarray(laid[name])
        arrays[f"in_{name}_dram"] = a
        args.append(nc.dram_tensor(f"in_{name}_dram", a.shape, mybir.dt.from_np(a.dtype), kind="ExternalInput").ap())
    shape = laid['x'].shape
    args.append(nc.dram_tensor("out_dram", shape, F32, kind="ExternalOutput").ap())
    gnn_stack(nc, *args)
    r = run_bass_kernel_spmd(nc, [arrays], core_ids=[0])
    return r.results[0]["out_dram"].transpose(1, 0, 2)
```
